# Optimizing a Trainium2 kernel written in Bass

```python
import numpy as np
import jax
import jax.numpy as jnp

def _softmax(x, axis=-1):
    return jax.nn.softmax(x, axis=axis)

def _gelu(x):
    return jax.nn.gelu(x, approximate=True)

def _silu(x):
    return jax.nn.silu(x)

def _sigmoid(x):
    return jax.nn.sigmoid(x)

def _layernorm(x, axis=-1, eps=1e-05):
    m = jnp.mean(x, axis=axis, keepdims=True)
    v = jnp.var(x, axis=axis, keepdims=True)
    return (x - m) / jnp.sqrt(v + eps)

def _scatter_add(tgt, idx, src, axis=0):
    return tgt.at[idx].add(src)

def _segment_sum(src, seg, n):
    return jax.ops.segment_sum(src, seg, n)
kernel_name = 'mk_adj_preln_d4_adj_r2_5eb3d2'

def setup_inputs(seed: int=0):
    np.random.seed(seed)
    _w = jnp.asarray

    def _rec_inputs():
        import jax
        import jax.numpy as jnp
        _gk = jax.random.key(seed)
        x = -0.001547 + 1.001 * jax.random.normal(jax.random.fold_in(_gk, 1), (64, 128, 64), jnp.float32)
        _a = jax.random.bernoulli(jax.random.fold_in(_gk, 2), 0.03125, (64, 128, 128))
        _a = jnp.logical_or(_a, jnp.swapaxes(_a, -1, -2))
        _a = jnp.logical_or(_a, jnp.eye(128, dtype=bool))
        _af = _a.astype(jnp.float32)
        adj = _af
        _nm = jnp.ones((64, 128), dtype=bool)
        nodemask = _nm
        return (x, adj, nodemask)
    x, adj, nodemask = _rec_inputs()

    def _L0_gnn_setup():
        import jax, jax.numpy as jnp
        import numpy as np
        B, N, C, H = (8, 256, 64, 128)
        T, K = (10, 2)
        TAUS = (0.25, 0.5, 0.75)
        WTS = (0.25, 0.5, 0.25)
        EPS_GIN = 0.0
        AVG_DEG = 32.0
        key = jax.random.key(seed)
        ks = jax.random.split(key, 6)
        x = jax.random.normal(ks[0], (B, N, C), jnp.float32)
        u = jax.random.uniform(ks[1], (B, N, N))
        a = u < AVG_DEG / N
        adj = jnp.maximum(a, jnp.swapaxes(a, 1, 2)).astype(jnp.float32)
        mask = jax.random.bernoulli(ks[2], 0.9, (B, N))
        W1 = jax.random.normal(ks[3], (C, H), jnp.float32) / np.float32(np.sqrt(C))
        b1 = jnp.zeros((H,), jnp.float32)
        W2 = jax.random.normal(ks[4], (H, C), jnp.float32) / np.float32(np.sqrt(H))
        b2 = jnp.zeros((C,), jnp.float32)
        return {'x': x, 'adj': adj, 'mask': mask, 'W1': W1, 'b1': b1, 'W2': W2, 'b2': b2}
    _L0_gnn_all = _L0_gnn_setup()
    _L0_gnn_in = {k: v for k, v in _L0_gnn_all.items() if k in ('W1', 'b1', 'W2', 'b2')}
    del _L0_gnn_all

    def _L1_gnn_setup():
        import jax, jax.numpy as jnp
        import numpy as np
        MIN_NORM = 1e-15
        BALL_EPS = 0.004
        C = 1.0
        CLAMP = 1000000.0

        def _artanh(x):
            return jnp.arctanh(jnp.clip(x, -1.0 + 1e-07, 1.0 - 1e-07))

        def _norm(x):
            return jnp.maximum(jnp.linalg.norm(x, axis=-1, keepdims=True), MIN_NORM)

        def mobius_add(x, y, c):
            x2 = jnp.sum(x * x, axis=-1, keepdims=True)
            y2 = jnp.sum(y * y, axis=-1, keepdims=True)
            xy = jnp.sum(x * y, axis=-1, keepdims=True)
            num = (1.0 + 2.0 * c * xy + c * y2) * x + (1.0 - c * x2) * y
            den = 1.0 + 2.0 * c * xy + c * c * x2 * y2
            return num / jnp.maximum(den, MIN_NORM)

        def lambda_x(x, c):
            return 2.0 / jnp.maximum(1.0 - c * jnp.sum(x * x, axis=-1, keepdims=True), MIN_NORM)

        def logmap(p1, p2, c):
            sub = mobius_add(-p1, p2, c)
            sub_norm = _norm(sub)
            sqrt_c = c ** 0.5
            return 2.0 / sqrt_c / lambda_x(p1, c) * _artanh(sqrt_c * sub_norm) * sub / sub_norm

        def expmap(u, p, c):
            sqrt_c = c ** 0.5
            u_norm = _norm(u)
            second = jnp.tanh(sqrt_c / 2.0 * lambda_x(p, c) * u_norm) * u / (sqrt_c * u_norm)
            return mobius_add(p, second, c)

        def proj(x, c):
            norm = _norm(x)
            maxnorm = (1.0 - BALL_EPS) / c ** 0.5
            return jnp.where(norm > maxnorm, x / norm * maxnorm, x)
        key = jax.random.key(seed)
        kx, ka, kw = jax.random.split(key, 3)
        B, N, D = (2, 384, 64)
        x = proj(0.2 * jax.random.normal(kx, (B, N, D), dtype=jnp.float32), C)
        adj = (jax.random.uniform(ka, (B, N, N), dtype=jnp.float32) < 0.05).astype(jnp.float32)
        att_W = jax.random.normal(kw, (2 * D, 1), dtype=jnp.float32) * (1.0 / np.sqrt(2 * D))
        att_b = jnp.zeros((1,), dtype=jnp.float32)
        return {'x': x, 'adj': adj, 'att_W': att_W, 'att_b': att_b}
    _L1_gnn_all = _L1_gnn_setup()
    _L1_gnn_in = {k: v for k, v in _L1_gnn_all.items() if k in ('att_W', 'att_b')}
    del _L1_gnn_all

    def _L2_gnn_setup():
        import jax, jax.numpy as jnp
        import numpy as np
        B, N, DIN, DOUT = (8, 128, 64, 64)
        AVG_D_LOG = 4.86
        EPS = 1e-05
        NEG_BIG = 1000000000.0
        N_AGG, N_SCALE = (4, 3)

        def _pna_forward(x, adj, W_pre, b_pre, W_post, b_post):
            n = adj.shape[1]
            h_i = jnp.broadcast_to(x[:, :, None, :], (x.shape[0], n, n, x.shape[-1]))
            h_j = jnp.broadcast_to(x[:, None, :, :], (x.shape[0], n, n, x.shape[-1]))
            h_cat = jnp.concatenate([h_i, h_j], axis=-1)
            h_mod = jnp.einsum('bnme,ed->bnmd', h_cat, W_pre) + b_pre
            deg = adj.sum(-1)
            deg_safe = jnp.maximum(deg, 1.0)[..., None]
            mask = (adj > 0)[..., None]
            s1 = jnp.einsum('bnm,bnmd->bnd', adj, h_mod)
            mean = s1 / deg_safe
            s2 = jnp.einsum('bnm,bnmd->bnd', adj, h_mod * h_mod)
            var = jax.nn.relu(s2 / deg_safe - mean * mean)
            std = jnp.sqrt(var + EPS)
            mx = jnp.max(jnp.where(mask, h_mod, -NEG_BIG), axis=2)
            mn = jnp.min(jnp.where(mask, h_mod, NEG_BIG), axis=2)
            m = jnp.concatenate([mean, mx, mn, std], axis=-1)
            log_deg = jnp.log(deg + 1.0)[..., None]
            amp = m * (log_deg / AVG_D_LOG)
            att = m * (AVG_D_LOG / jnp.maximum(log_deg, EPS))
            m_all = jnp.concatenate([m, amp, att], axis=-1)
            m_cat = jnp.concatenate([x, m_all], axis=-1)
            return jnp.einsum('bne,ed->bnd', m_cat, W_post) + b_post
        key = jax.random.key(seed)
        k1, k2, k3, k4, k5, k6 = jax.random.split(key, 6)
        inp = jax.random.normal(k1, (B, N, DIN), dtype=jnp.float32)
        adj = jax.random.randint(k2, (B, N, N), 0, 2).astype(jnp.float32)
        W_pre = jax.random.normal(k3, (2 * DIN, DIN), dtype=jnp.float32) / np.sqrt(2 * DIN)
        b_pre = jnp.zeros((DIN,), dtype=jnp.float32)
        post_in = (N_AGG * N_SCALE + 1) * DIN
        W_post = jax.random.normal(k4, (post_in, DOUT), dtype=jnp.float32) / np.sqrt(post_in)
        b_post = jnp.zeros((DOUT,), dtype=jnp.float32)
        return {'input': inp, 'adj': adj, 'W_pre': W_pre, 'b_pre': b_pre, 'W_post': W_post, 'b_post': b_post}
    _L2_gnn_all = _L2_gnn_setup()
    _L2_gnn_in = {k: v for k, v in _L2_gnn_all.items() if k in ('W_pre', 'b_pre', 'W_post', 'b_post')}
    del _L2_gnn_all

    def _L3_gnn_setup():
        import jax, jax.numpy as jnp
        import numpy as np
        NORM = 1.0

        def _glorot(key, shape):
            fan_in, fan_out = shape
            lim = float(np.sqrt(6.0 / (fan_in + fan_out)))
            return jax.random.uniform(key, shape, jnp.float32, -lim, lim)

        def _gcn_layer(h, adj, W, b):
            msg = h @ W + b
            agg = jnp.einsum('bij,bjd->bid', adj, msg) / NORM
            return jax.nn.relu(agg)
        key = jax.random.key(seed)
        ks = jax.random.split(key, 12)
        B, N = (8, 1024)
        latent, hidden, out_dim = (64, 128, 64)
        inp = {'latent_features': jax.random.normal(ks[0], (B, N, latent), jnp.float32), 'adjacency_matrix': jax.random.uniform(ks[1], (B, N, N), jnp.float32), 'node_mask': jnp.ones((B, N, 1), jnp.float32), 'W0': _glorot(ks[2], (latent, hidden)), 'b0': jnp.zeros((hidden,), jnp.float32), 'W1': _glorot(ks[3], (hidden, hidden)), 'b1': jnp.zeros((hidden,), jnp.float32), 'W2': _glorot(ks[4], (hidden, hidden)), 'b2': jnp.zeros((hidden,), jnp.float32), 'Wout': _glorot(ks[5], (hidden, out_dim)), 'bout': jnp.zeros((out_dim,), jnp.float32)}
        return inp
    _L3_gnn_all = _L3_gnn_setup()
    _L3_gnn_in = {k: v for k, v in _L3_gnn_all.items() if k in ('W0', 'b0', 'W1', 'b1', 'W2', 'b2', 'Wout', 'bout')}
    del _L3_gnn_all
    return {'x': x, 'adj': adj, 'nodemask': nodemask, 'L0_gnn_W1': _L0_gnn_in['W1'], 'L0_gnn_b1': _L0_gnn_in['b1'], 'L0_gnn_W2': _L0_gnn_in['W2'], 'L0_gnn_b2': _L0_gnn_in['b2'], 'L1_gnn_att_W': _L1_gnn_in['att_W'], 'L1_gnn_att_b': _L1_gnn_in['att_b'], 'L2_gnn_W_pre': _L2_gnn_in['W_pre'], 'L2_gnn_b_pre': _L2_gnn_in['b_pre'], 'L2_gnn_W_post': _L2_gnn_in['W_post'], 'L2_gnn_b_post': _L2_gnn_in['b_post'], 'L3_gnn_W0': _L3_gnn_in['W0'], 'L3_gnn_b0': _L3_gnn_in['b0'], 'L3_gnn_W1': _L3_gnn_in['W1'], 'L3_gnn_b1': _L3_gnn_in['b1'], 'L3_gnn_W2': _L3_gnn_in['W2'], 'L3_gnn_b2': _L3_gnn_in['b2'], 'L3_gnn_Wout': _L3_gnn_in['Wout'], 'L3_gnn_bout': _L3_gnn_in['bout']}

def reference(x, adj, nodemask, L0_gnn_W1, L0_gnn_b1, L0_gnn_W2, L0_gnn_b2, L1_gnn_att_W, L1_gnn_att_b, L2_gnn_W_pre, L2_gnn_b_pre, L2_gnn_W_post, L2_gnn_b_post, L3_gnn_W0, L3_gnn_b0, L3_gnn_W1, L3_gnn_b1, L3_gnn_W2, L3_gnn_b2, L3_gnn_Wout, L3_gnn_bout):
    import jax
    import jax.numpy as jnp

    def _L0_gnn_ref(x, adj, mask, W1, b1, W2, b2):
        import jax, jax.numpy as jnp
        import numpy as np
        B, N, C, H = (8, 256, 64, 128)
        T, K = (10, 2)
        TAUS = (0.25, 0.5, 0.75)
        WTS = (0.25, 0.5, 0.25)
        EPS_GIN = 0.0
        AVG_DEG = 32.0
        Bc, Nc, Cc = x.shape
        eye = jnp.eye(Nc, dtype=bool)
        adj_ = jnp.where(eye, 1.0, adj)
        neigh = (adj_ > 0) & ~eye
        ni = neigh.astype(jnp.int32)
        rank = jnp.cumsum(ni, axis=-1) - ni
        nb = ni.sum(-1)
        skip = jnp.where(nb > T, (nb + K - 1) // K, 1)
        skip = jnp.maximum(skip, 1)
        sk = skip[:, :, None]
        rem = neigh & (sk > 1) & (rank % sk == sk - 1) & mask[:, :, None]
        rem = rem | jnp.swapaxes(rem, 1, 2)
        adj_d = jnp.where(rem, 0.0, adj_)
        nd = adj_d > 0
        vals = jnp.where(nd[..., None], x[:, None, :, :], jnp.inf)
        s = jnp.sort(vals, axis=2)
        nv = nd.sum(2)
        agg = jnp.zeros_like(x)
        for tau, w in zip(TAUS, WTS):
            pos = jnp.asarray(tau, x.dtype) * jnp.maximum(nv - 1, 0).astype(x.dtype)
            lo = jnp.floor(pos).astype(jnp.int32)
            hi = jnp.ceil(pos).astype(jnp.int32)
            frac = (pos - lo.astype(x.dtype))[..., None]
            idx_lo = jnp.broadcast_to(lo[:, :, None, None], (Bc, Nc, 1, Cc))
            idx_hi = jnp.broadcast_to(hi[:, :, None, None], (Bc, Nc, 1, Cc))
            v_lo = jnp.take_along_axis(s, idx_lo, axis=2)[:, :, 0, :]
            v_hi = jnp.take_along_axis(s, idx_hi, axis=2)[:, :, 0, :]
            agg = agg + jnp.asarray(w, x.dtype) * (v_lo + frac * (v_hi - v_lo))
        agg = jnp.where(nv[..., None] > 0, agg, 0.0)
        out = (1.0 + EPS_GIN) * x + agg
        h = jax.nn.relu(out @ W1 + b1)
        y = h @ W2 + b2
        return y * mask[..., None].astype(y.dtype)

    def _L1_gnn_ref(x, adj, att_W, att_b):
        import jax, jax.numpy as jnp
        import numpy as np
        MIN_NORM = 1e-15
        BALL_EPS = 0.004
        C = 1.0
        CLAMP = 1000000.0

        def _artanh(x):
            return jnp.arctanh(jnp.clip(x, -1.0 + 1e-07, 1.0 - 1e-07))

        def _norm(x):
            return jnp.maximum(jnp.linalg.norm(x, axis=-1, keepdims=True), MIN_NORM)

        def mobius_add(x, y, c):
            x2 = jnp.sum(x * x, axis=-1, keepdims=True)
            y2 = jnp.sum(y * y, axis=-1, keepdims=True)
            xy = jnp.sum(x * y, axis=-1, keepdims=True)
            num = (1.0 + 2.0 * c * xy + c * y2) * x + (1.0 - c * x2) * y
            den = 1.0 + 2.0 * c * xy + c * c * x2 * y2
            return num / jnp.maximum(den, MIN_NORM)

        def lambda_x(x, c):
            return 2.0 / jnp.maximum(1.0 - c * jnp.sum(x * x, axis=-1, keepdims=True), MIN_NORM)

        def logmap(p1, p2, c):
            sub = mobius_add(-p1, p2, c)
            sub_norm = _norm(sub)
            sqrt_c = c ** 0.5
            return 2.0 / sqrt_c / lambda_x(p1, c) * _artanh(sqrt_c * sub_norm) * sub / sub_norm

        def expmap(u, p, c):
            sqrt_c = c ** 0.5
            u_norm = _norm(u)
            second = jnp.tanh(sqrt_c / 2.0 * lambda_x(p, c) * u_norm) * u / (sqrt_c * u_norm)
            return mobius_add(p, second, c)

        def proj(x, c):
            norm = _norm(x)
            maxnorm = (1.0 - BALL_EPS) / c ** 0.5
            return jnp.where(norm > maxnorm, x / norm * maxnorm, x)
        c = C
        b, n, d = x.shape
        x_i = x[:, :, None, :]
        x_j = x[:, None, :, :]
        x_local = logmap(x_i, x_j, c)
        x_self = logmap(x, x, c)
        feats = jnp.concatenate([jnp.broadcast_to(x_self[:, :, None, :], x_local.shape), x_local], axis=-1)
        logits = jnp.einsum('bijk,ko->bijo', feats, att_W)[..., 0] + att_b[0]
        att = jax.nn.sigmoid(logits) * adj
        support_t = jnp.einsum('bij,bijd->bid', att, x_local)
        support_t = jnp.clip(support_t, -CLAMP, CLAMP)
        return proj(expmap(support_t, x, c), c)

    def _L2_gnn_ref(input, adj, W_pre, b_pre, W_post, b_post):
        import jax, jax.numpy as jnp
        import numpy as np
        B, N, DIN, DOUT = (8, 128, 64, 64)
        AVG_D_LOG = 4.86
        EPS = 1e-05
        NEG_BIG = 1000000000.0
        N_AGG, N_SCALE = (4, 3)

        def _pna_forward(x, adj, W_pre, b_pre, W_post, b_post):
            n = adj.shape[1]
            h_i = jnp.broadcast_to(x[:, :, None, :], (x.shape[0], n, n, x.shape[-1]))
            h_j = jnp.broadcast_to(x[:, None, :, :], (x.shape[0], n, n, x.shape[-1]))
            h_cat = jnp.concatenate([h_i, h_j], axis=-1)
            h_mod = jnp.einsum('bnme,ed->bnmd', h_cat, W_pre) + b_pre
            deg = adj.sum(-1)
            deg_safe = jnp.maximum(deg, 1.0)[..., None]
            mask = (adj > 0)[..., None]
            s1 = jnp.einsum('bnm,bnmd->bnd', adj, h_mod)
            mean = s1 / deg_safe
            s2 = jnp.einsum('bnm,bnmd->bnd', adj, h_mod * h_mod)
            var = jax.nn.relu(s2 / deg_safe - mean * mean)
            std = jnp.sqrt(var + EPS)
            mx = jnp.max(jnp.where(mask, h_mod, -NEG_BIG), axis=2)
            mn = jnp.min(jnp.where(mask, h_mod, NEG_BIG), axis=2)
            m = jnp.concatenate([mean, mx, mn, std], axis=-1)
            log_deg = jnp.log(deg + 1.0)[..., None]
            amp = m * (log_deg / AVG_D_LOG)
            att = m * (AVG_D_LOG / jnp.maximum(log_deg, EPS))
            m_all = jnp.concatenate([m, amp, att], axis=-1)
            m_cat = jnp.concatenate([x, m_all], axis=-1)
            return jnp.einsum('bne,ed->bnd', m_cat, W_post) + b_post
        return _pna_forward(input, adj, W_pre, b_pre, W_post, b_post)

    def _L3_gnn_ref(latent_features, adjacency_matrix, node_mask, W0, b0, W1, b1, W2, b2, Wout, bout):
        import jax, jax.numpy as jnp
        import numpy as np
        NORM = 1.0

        def _glorot(key, shape):
            fan_in, fan_out = shape
            lim = float(np.sqrt(6.0 / (fan_in + fan_out)))
            return jax.random.uniform(key, shape, jnp.float32, -lim, lim)

        def _gcn_layer(h, adj, W, b):
            msg = h @ W + b
            agg = jnp.einsum('bij,bjd->bid', adj, msg) / NORM
            return jax.nn.relu(agg)
        h = _gcn_layer(latent_features, adjacency_matrix, W0, b0)
        h = _gcn_layer(h, adjacency_matrix, W1, b1)
        h = _gcn_layer(h, adjacency_matrix, W2, b2)
        return (h @ Wout + bout) * node_mask
    h = jnp.maximum(_layernorm(x, axis=-1), 0.0)
    x = x + _L0_gnn_ref(h, adj, nodemask, L0_gnn_W1, L0_gnn_b1, L0_gnn_W2, L0_gnn_b2)
    h = jnp.maximum(_layernorm(x, axis=-1), 0.0)
    x = x + _L1_gnn_ref(h, adj, L1_gnn_att_W, L1_gnn_att_b)
    h = jnp.maximum(_layernorm(x, axis=-1), 0.0)
    x = x + _L2_gnn_ref(h, adj, L2_gnn_W_pre, L2_gnn_b_pre, L2_gnn_W_post, L2_gnn_b_post)
    h = jnp.maximum(_layernorm(x, axis=-1), 0.0)
    x = x + _L3_gnn_ref(h, adj, nodemask[..., None], L3_gnn_W0, L3_gnn_b0, L3_gnn_W1, L3_gnn_b1, L3_gnn_W2, L3_gnn_b2, L3_gnn_Wout, L3_gnn_bout)
    return x

_drawn_inputs = setup_inputs


def setup_inputs(seed=0):
    import zlib

    import numpy as np

    out = dict(_drawn_inputs(seed))
    spreads = {'L0_gnn_b1': (0.0, 0.1),
     'L0_gnn_b2': (0.0, 0.1),
     'L2_gnn_b_pre': (0.0, 0.1),
     'L2_gnn_b_post': (0.0, 0.1),
     'L3_gnn_b0': (0.0, 0.1),
     'L3_gnn_b1': (0.0, 0.1),
     'L3_gnn_b2': (0.0, 0.8),
     'L3_gnn_bout': (0.0, 0.8)}
    factors = {}
    for name, (base, spread) in spreads.items():
        noise = np.random.default_rng([zlib.crc32(name.encode()), seed]).standard_normal(out[name].shape)
        drawn = base * np.exp(spread * noise) if base else spread * noise
        out[name] = jnp.asarray(drawn.astype(out[name].dtype))
    for name, factor in factors.items():
        out[name] = (out[name] * factor).astype(out[name].dtype)
    return out
```

```python
from contextlib import ExitStack

import concourse.bass as bass
from concourse import mybir

ALU = mybir.AluOpType
ACT = mybir.ActivationFunctionType
F32 = mybir.dt.float32
BF16 = mybir.dt.bfloat16
I32 = mybir.dt.int32
U8 = mybir.dt.uint8
AX = mybir.AxisListType.X

SLOTS = 20
RING = 5
QG = 4
SG = 8
BIG = 2.0 ** 100
ROUND = 2.0 ** 23
TAUS = ((0.25, 0.25), (0.5, 0.5), (0.75, 0.25))
LAST = 15
MIN_NORM = 1e-15
ATANH_MAX = 1.0 - 2.0 ** -23
LN_EPS = 1e-5
CLAMP = 1000000.0
AVG_D_LOG = 4.86
NEG_BIG = 1000000000.0
BALL = 1.0 - 0.004


def sorting_layers(n):
    layers, p = [], 1
    while p < n:
        k = p
        while k >= 1:
            layers.append([(i + j, i + j + k)
                           for j in range(k % p, n - k, 2 * k)
                           for i in range(min(k, n - j - k))
                           if (i + j) // (2 * p) == (i + j + k) // (2 * p)])
            k //= 2
        p *= 2
    return layers


def live_halves(layers, outputs):
    live, kept = set(outputs), []
    for layer in reversed(layers):
        rows = [(a, b, a in live, b in live) for a, b in layer if a in live or b in live]
        for a, b, _, _ in rows:
            live |= {a, b}
        kept.insert(0, rows)
    return kept


class Steps:
    def __init__(self, eng, sem, per=0, turn=0):
        self.eng, self.sem, self.per, self.turn, self.k = eng, sem, per, turn, 0

    def __call__(self, ins):
        ins.then_inc(self.sem, 1)
        self.k += 1
        return ins

    def wait(self, back=0):
        if self.k > back:
            self.eng.wait_ge(self.sem, self.turn * self.per + self.k - back)

    def end(self):
        assert self.per == self.k, (self.per, self.k)


class Turns:
    def __init__(self, sem, per=1):
        self.sem, self.per = sem, per

    def begin(self, eng):
        eng.sem_inc(self.sem, 2 * self.per)

    def wait(self, eng, turn, k=None, behind=0):
        k = self.per if k is None else k
        eng.wait_ge(self.sem, (turn + (2 - behind)) * self.per + k if behind < 2 else turn * self.per + k)


def starts_free(eng, *sems):
    for s in sems:
        eng.sem_inc(s, 1)


def build(nc, x, adj, nodemask, W, out, stop=99):
    B, N, C = x.shape
    assert N == 128 and C == 64 and B % SG == 0
    HID = W["L0_gnn_W1"].shape[1]
    QUADS, SORTS = B // QG, B // SG
    with ExitStack() as ctx:
        def sb(name, shape, dt=F32):
            return ctx.enter_context(nc.sbuf_tensor(name, shape, dt))

        layer_sems = []

        def sem(name):
            layer_sems.append(nc.alloc_semaphore(name=name))
            return layer_sems[-1]

        def end_layer():
            nc.clear_and_free_semaphores(list(layer_sems))
            nc.all_engine_barrier()
            layer_sems.clear()

        X = sb("X", [N, B, C])
        H = sb("H", [N, B, C])
        AT = sb("AT", [N, B, N], BF16)
        POS = sb("POS", [N, B, N], BF16)
        PARTS = sb("PARTS", [N, 3, B, C], BF16)
        identf = sb("identf", [N, N])
        identb = sb("identb", [N, N], BF16)
        offdiag = sb("offdiag", [N, N], BF16)
        upper = sb("upper", [N, N], BF16)
        onesb = sb("onesb", [N, N], BF16)
        onesf = sb("onesf", [1, N])
        slot_no = sb("slot_no", [N, SLOTS])
        mask = sb("mask", [N, B])
        count = sb("count", [N, B])
        w1 = sb("w1", [2 * C, HID])
        b1 = sb("b1", [HID, 1])
        w2 = sb("w2", [HID, C])
        b2 = sb("b2", [1, C])
        ROOM = 28416
        room = sb("room", [N, ROOM])
        used = [0]

        def take(shape, dt=F32):
            size = 1
            for s in shape[1:]:
                size *= s
            words = size if dt == F32 or dt == I32 else size // 2
            a = used[0]
            used[0] += words
            assert used[0] <= ROOM, used[0]
            piece = room[0:shape[0], a:a + words]
            if dt != F32:
                piece = piece.bitcast(dt)
            names = "abcd"[:len(shape) - 1]
            if len(names) > 1:
                piece = piece.rearrange("p (" + " ".join(names) + ") -> p " + " ".join(names),
                                        **{n: s for n, s in zip(names, shape[1:])})
            return piece

        def stage_constants():
            used[0] = 0
            loaded, made, turned = sem("loaded"), sem("made"), sem("turned")
            mrow8, mrow = take([N, N // 4]), take([N, N])
            mrow8 = mrow8.bitcast(U8)
            with nc.psum_tensor("mT", [N, B], F32) as mT, nc.Block() as block:
                @block.sync
                def _(sp):
                    sp.dma_start(mrow8[0:B, :], nodemask).then_inc(loaded, 16)
                    sp.dma_start(X[:], x.rearrange("g i c -> i g c")).then_inc(loaded, 16)
                    sp.dma_start(w1[0:C, :], W["L0_gnn_W1"]).then_inc(loaded, 16)
                    sp.dma_start(w1[C:2 * C, :], W["L0_gnn_W1"]).then_inc(loaded, 16)
                    sp.dma_start(b1[:], W["L0_gnn_b1"].rearrange("(h a) -> h a", a=1)).then_inc(loaded, 16)
                    sp.dma_start(w2[:], W["L0_gnn_W2"]).then_inc(loaded, 16)
                    sp.dma_start(b2[:], W["L0_gnn_b2"].rearrange("(a c) -> a c", a=1)).then_inc(loaded, 16)
                    sp.wait_ge(loaded, 112)

                @block.gpsimd
                def _(pool):
                    step = Steps(pool, made)
                    step(nc.gpsimd.memset(onesf[:], 1.0))
                    step(nc.gpsimd.memset(onesb[:], 1.0))
                    step(nc.gpsimd.memset(identf[:], 0.0))
                    step.wait()
                    step(nc.gpsimd.affine_select(out=identf[:], in_=identf[:], compare_op=ALU.not_equal,
                                                 fill=1.0, base=0, pattern=[[-1, N]], channel_multiplier=1))
                    step(nc.gpsimd.affine_select(out=upper[:], in_=onesb[:], compare_op=ALU.is_ge,
                                                 fill=0.0, base=0, pattern=[[1, N]], channel_multiplier=-1))
                    step(nc.gpsimd.affine_select(out=offdiag[:], in_=onesb[:], compare_op=ALU.not_equal,
                                                 fill=0.0, base=0, pattern=[[-1, N]], channel_multiplier=1))
                    step(nc.gpsimd.iota(slot_no[:], pattern=[[1, SLOTS]], base=0, channel_multiplier=0,
                                        allow_small_or_imprecise_dtypes=True))
                    step.wait()
                    step(nc.gpsimd.tensor_copy(identb[:], identf[:]))
                    pool.wait_ge(loaded, 112)
                    step(nc.gpsimd.tensor_copy(mrow[0:B, :], mrow8[0:B, :]))

                @block.tensor
                def _(pe):
                    pe.wait_ge(made, 9)
                    nc.tensor.transpose(mT[:], mrow[0:B, :], identf[0:B, 0:B]).then_inc(turned, 1)

                @block.vector
                def _(dve):
                    dve.wait_ge(turned, 1)
                    nc.vector.tensor_copy(mask[:], mT[:]).then_inc(made, 1)

        def stage_positions(tag, thinned):
            used[0] = 0
            kept_ready, summed, step_done = sem(tag + "kept_ready"), sem(tag + "summed"), sem(tag + "step_done")
            if thinned:
                adj_in, adj_free, turned, at_ready = sem("adj_in"), sem("adj_free"), sem("adj_turned"), sem("at_ready")
                neigh_ready, ranked, rem_ready, rem_both = sem("neigh_ready"), sem("ranked"), sem("rem_ready"), sem("rem_both")
            A = take([N, QG, N])
            nat = take([N, QG, N], BF16)
            natT = take([N, QG, N], BF16)
            e1, e2 = take([N, QG, N]), take([N, QG, N])
            rem = take([N, QG, N], BF16)
            keepT = take([N, QG, N], BF16)
            small = [take([N, QG]) for _ in range(8)]
            with ExitStack() as ps:
                tA = ps.enter_context(nc.psum_tensor(tag + "tA", [N, QG, N], F32))
                rank = ps.enter_context(nc.psum_tensor(tag + "rank", [N, QG, N], F32))
                both = ps.enter_context(nc.psum_tensor(tag + "both", [N, QG, N], F32))
                cum = ps.enter_context(nc.psum_tensor(tag + "cum", [N, QG, N], F32))
                nv = ps.enter_context(nc.psum_tensor(tag + "nv", [N, QG], F32))
                block = ps.enter_context(nc.Block())
                bc = [N, QG, N]

                if thinned:
                    @block.sync
                    def _(sp):
                        with sp.Fori(0, QUADS) as q:
                            sp.wait_ge(adj_free, q + 1)
                            sp.dma_start(A, adj[bass.ds(q * QG, QG)].rearrange("g i j -> i g j")).then_inc(adj_in, 16)

                    @block.scalar
                    def _(act):
                        starts_free(act, at_ready)
                        with act.Fori(0, QUADS) as q:
                            act.wait_ge(turned, q + 1)
                            nc.scalar.copy(AT[:, bass.ds(q * QG, QG), :], tA[:]).then_inc(at_ready, 1)

                @block.tensor
                def _(pe):
                    with pe.Fori(0, QUADS) as q:
                        if thinned:
                            pe.wait_ge(adj_in, q * 16 + 16)
                            pe.wait_ge(at_ready, q + 1)
                            for g in range(QG):
                                mm = nc.tensor.transpose(tA[:, g, :], A[:, g, :], identf[:])
                            mm.then_inc(turned, 1)
                            pe.wait_ge(neigh_ready, q * 2 + 2)
                            for g in range(QG):
                                mm = nc.tensor.matmul(rank[:, g, :], natT[:, g, :], upper[:], start=True, stop=True)
                            mm.then_inc(ranked, 1)
                            pe.wait_ge(rem_ready, q + 1)
                            for g in range(QG):
                                nc.tensor.matmul(both[:, g, :], rem[:, g, :], identb[:], start=True, stop=False)
                                mm = nc.tensor.matmul(both[:, g, :], identb[:], rem[:, g, :], start=False, stop=True)
                            mm.then_inc(rem_both, 1)
                        pe.wait_ge(kept_ready, q + 1)
                        nc.tensor.matmul(cum[:], upper[:], keepT, start=True, stop=True)
                        for g in range(QG):
                            mm = nc.tensor.matmul(nv[:, g:g + 1], keepT[:, g, :], onesb[:, 0:1], start=True, stop=True)
                        mm.then_inc(summed, 1)

                @block.vector
                def _(dve):
                    if thinned:
                        starts_free(dve, adj_free)
                    with dve.Fori(0, QUADS) as q:
                        quad = bass.ds(q * QG, QG)
                        step = Steps(dve, step_done, 13 if thinned else 1, q)
                        if thinned:
                            off = offdiag[:].unsqueeze(1).broadcast_to(bc)
                            dve.wait_ge(adj_in, q * 16 + 16)
                            nc.vector.scalar_tensor_tensor(out=nat, in0=A, scalar=0.0, in1=off,
                                                           op0=ALU.is_gt, op1=ALU.mult).then_inc(neigh_ready, 1)
                            dve.wait_ge(at_ready, q + 2)
                            nc.vector.scalar_tensor_tensor(out=natT, in0=AT[:, quad, :], scalar=0.0, in1=off,
                                                           op0=ALU.is_gt, op1=ALU.mult).then_inc(neigh_ready, 1)
                            dve.wait_ge(neigh_ready, q * 2 + 2)
                            dve.sem_inc(adj_free, 1)
                            dve.wait_ge(ranked, q + 1)
                            nb = rank[:, :, N - 1]
                            half, up, skip, cond, cm, sk1, sk2, sk0 = small
                            step(nc.vector.tensor_scalar(half, nb, 0.5, 0.25, ALU.mult, ALU.add))
                            step.wait()
                            step(nc.vector.tensor_scalar(up, half, ROUND, None, ALU.add))
                            step.wait()
                            step(nc.vector.tensor_scalar(skip, up, ROUND, None, ALU.subtract))
                            step(nc.vector.scalar_tensor_tensor(out=cond, in0=nb, scalar=10.5, in1=mask[:, quad],
                                                                op0=ALU.is_gt, op1=ALU.mult))
                            step.wait()
                            step(nc.vector.tensor_scalar(cm, cond, 1.0, None, ALU.subtract))
                            step(nc.vector.tensor_tensor(sk0, skip, cond, ALU.mult))
                            step.wait()
                            step(nc.vector.tensor_tensor(sk1, sk0, cm, ALU.add))
                            step.wait()
                            step(nc.vector.tensor_scalar(sk2, sk1, 2.0, None, ALU.mult))
                            step.wait()
                            step(nc.vector.tensor_tensor(e1, rank[:], sk1.unsqueeze(2).broadcast_to(bc), ALU.is_equal))
                            step(nc.vector.tensor_tensor(e2, rank[:], sk2.unsqueeze(2).broadcast_to(bc), ALU.is_equal))
                            step.wait()
                            step(nc.vector.tensor_tensor(e1, e1, e2, ALU.add))
                            step.wait()
                            nc.vector.tensor_tensor(rem, e1, nat, ALU.mult).then_inc(rem_ready, 1)
                            step(nc.vector.tensor_tensor(e2, natT, identb[:].unsqueeze(1).broadcast_to(bc), ALU.add))
                            step.wait()
                            dve.wait_ge(rem_both, q + 1)
                            nc.vector.scalar_tensor_tensor(out=keepT, in0=both[:], scalar=0.0, in1=e2,
                                                           op0=ALU.is_equal, op1=ALU.mult).then_inc(kept_ready, 1)
                        else:
                            nc.vector.tensor_scalar(keepT, AT[:, quad, :], 0.0, None, ALU.is_gt).then_inc(kept_ready, 1)
                        dve.wait_ge(kept_ready, q + 1)
                        dve.wait_ge(summed, q + 1)
                        nc.vector.tensor_tensor(POS[:, quad, :], cum[:], keepT, ALU.mult)
                        step(nc.vector.tensor_copy(count[:, quad], nv[:]))
                        step.wait()
                        step.end()

        centred, squared, var_ready, root_ready, mean_ready, h_ready, norm_step = [
            ctx.enter_context(nc.semaphore(n)) for n in ("centred", "squared", "var", "root", "mean", "h", "norm_step")]

        def stage_norm(n, parts):
            used[0] = 0
            CH = B // 4
            if parts:
                hi_ready, r1_ready, mid_ready, r2_ready = [sem("norm_" + w) for w in ("hi", "r1", "mid", "r2")]
            mean, var, root, rstd = [take([N, B]) for _ in range(4)]
            eps = take([N, 1])
            xc, sq = take([N, B, C]), take([N, B, C])
            rest = take([N, B, C])
            bc = [N, CH, C]
            with nc.Block() as block:
                @block.gpsimd
                def _(pool):
                    with pool.Fori(0, 4) as t:
                        ch = bass.ds(t * CH, CH)
                        pool.wait_ge(mean_ready, t + 5 * n + 2)
                        nc.gpsimd.tensor_tensor(xc[:, ch], X[:, ch], mean[:, ch].unsqueeze(2).broadcast_to(bc),
                                                ALU.add).then_inc(centred, 1)
                    if parts:
                        with pool.Fori(0, 4) as t:
                            ch = bass.ds(t * CH, CH)
                            pool.wait_ge(hi_ready, t + 1)
                            nc.gpsimd.tensor_tensor(rest[:, ch], H[:, ch], PARTS[:, 0, ch], ALU.subtract).then_inc(r1_ready, 1)
                        with pool.Fori(0, 4) as t:
                            ch = bass.ds(t * CH, CH)
                            pool.wait_ge(mid_ready, t + 1)
                            nc.gpsimd.tensor_tensor(xc[:, ch], rest[:, ch], PARTS[:, 1, ch], ALU.subtract).then_inc(r2_ready, 1)

                @block.scalar
                def _(act):
                    with act.Fori(0, 4) as t:
                        ch = bass.ds(t * CH, CH)
                        act.wait_ge(centred, t + 4 * n + 1)
                        nc.scalar.activation(sq[:, ch], xc[:, ch], ACT.Square).then_inc(squared, 1)
                    act.wait_ge(var_ready, 4 * n + 4)
                    act.wait_ge(mean_ready, 5 * n + 1)
                    nc.scalar.activation(root, var, ACT.Sqrt, bias=eps, scale=1.0 / C).then_inc(root_ready, 1)
                    if parts:
                        with act.Fori(0, 4) as t:
                            ch = bass.ds(t * CH, CH)
                            act.wait_ge(h_ready, t + 4 * n + 1)
                            nc.scalar.copy(PARTS[:, 0, ch], H[:, ch]).then_inc(hi_ready, 1)
                        with act.Fori(0, 4) as t:
                            ch = bass.ds(t * CH, CH)
                            act.wait_ge(r1_ready, t + 1)
                            nc.scalar.copy(PARTS[:, 1, ch], rest[:, ch]).then_inc(mid_ready, 1)
                        with act.Fori(0, 4) as t:
                            ch = bass.ds(t * CH, CH)
                            act.wait_ge(r2_ready, t + 1)
                            nc.scalar.copy(PARTS[:, 2, ch], xc[:, ch])

                @block.vector
                def _(dve):
                    nc.vector.memset(eps, LN_EPS).then_inc(mean_ready, 1)
                    with dve.Fori(0, 4) as t:
                        ch = bass.ds(t * CH, CH)
                        nc.vector.tensor_reduce(root[:, ch], X[:, ch], AX, ALU.add).then_inc(norm_step, 1)
                        dve.wait_ge(norm_step, t + 5 * n + 1)
                        nc.vector.tensor_scalar(mean[:, ch], root[:, ch], -1.0 / C, None, ALU.mult).then_inc(mean_ready, 1)
                    with dve.Fori(0, 4) as t:
                        ch = bass.ds(t * CH, CH)
                        dve.wait_ge(squared, t + 4 * n + 1)
                        nc.vector.tensor_reduce(var[:, ch], sq[:, ch], AX, ALU.add).then_inc(var_ready, 1)
                    dve.wait_ge(root_ready, n + 1)
                    nc.vector.reciprocal(rstd, root).then_inc(norm_step, 1)
                    dve.wait_ge(norm_step, 5 * n + 5)
                    with dve.Fori(0, 4) as t:
                        ch = bass.ds(t * CH, CH)
                        nc.vector.scalar_tensor_tensor(out=H[:, ch], in0=xc[:, ch], scalar=0.0,
                                                       in1=rstd[:, ch].unsqueeze(2).broadcast_to(bc),
                                                       op0=ALU.max, op1=ALU.mult).then_inc(h_ready, 1)

        def hot_slot(dve, s, r, hot, hot_ready, slot_ready):
            k = r % RING
            if r >= RING:
                dve.wait_ge(slot_ready[k], s * (SLOTS // RING) + r // RING)
            nc.vector.tensor_scalar(hot[k], POS[:, bass.ds(s * SG, SG), :].rearrange("p g i -> p (g i)"), float(r + 1),
                                    None, ALU.is_equal).then_inc(hot_ready[k], 1)

        def gather_slot(pe, s, r, hot, hot_ready, slot_ready, pad, pad_sign, piece):
            k = r % RING
            pe.wait_ge(hot_ready[k], s * (SLOTS // RING) + r // RING + 1)
            nc.tensor.matmul(piece, pad_sign, pad[:, r, bass.ds(s * SG, SG)].unsqueeze(2).broadcast_to([N, SG, C]),
                             start=True, stop=True)
            for g in range(SG):
                for part in range(3):
                    mm = nc.tensor.matmul(piece[:, g, :], hot[k][:, g * N:(g + 1) * N],
                                          PARTS[:, part, bass.ds(s * SG + g, 1), :].rearrange("p a c -> p (a c)"),
                                          start=False, stop=True, skip_group_check=True)
            mm.then_inc(slot_ready[k], 1)

        def absent_slots(eng, step, pad):
            for r in range(SLOTS):
                step(eng.tensor_scalar(pad[:, r, :], count[:], float(r), BIG, ALU.is_le, ALU.mult))

        def stage_quantiles():
            used[0] = 0
            layers = live_halves(sorting_layers(SLOTS), range(LAST + 1))
            hot_ready = [sem(f"hot_ready{k}") for k in range(RING)]
            slot_ready = [sem(f"slot_ready{k}") for k in range(RING)]
            slot_copied = [sem(f"slot_copied{k}") for k in range(RING)]
            prep, sorting, first_read = sem("prep"), sem("sorting"), sem("first_read")
            weighted, summed, agg_added = sem("weighted"), sem("agg_summed"), sem("agg_added")
            raw = take([N, SLOTS, SG * C])
            wires = take([N, SLOTS + 2, SG * C])
            hot = [take([N, SG * N], BF16) for _ in range(RING)]
            pad = take([N, SLOTS, B], BF16)
            om = take([N, LAST + 1, B])
            pos = take([N, B])
            TURN = SLOTS // RING

            HOME = [None] * SLOTS
            plan, free = [], list(range(SLOTS + 2))
            for layer in layers:
                rows = []
                for a, b, want_min, want_max in layer:
                    src = [("raw", w) if HOME[w] is None else ("wire", HOME[w]) for w in (a, b)]
                    low = free.pop(0) if want_min else None
                    high = None
                    if want_max:
                        high = free.pop(0) if HOME[b] is None else HOME[b]
                    elif HOME[b] is not None:
                        free.append(HOME[b])
                    if HOME[a] is not None:
                        free.append(HOME[a])
                    rows.append((src[0], src[1], low, high))
                    HOME[a], HOME[b] = low, high
                plan.append(rows)
            HALVES = sum((lo is not None) + (hi is not None) for rows in plan for _, _, lo, hi in rows)
            first_last = max(n for n, rows in enumerate(plan) for r in rows if "raw" in (r[0][0], r[1][0]))

            with ExitStack() as ps:
                gat = [ps.enter_context(nc.psum_tensor(f"gat{b}", [N, SG, C], F32)) for b in range(RING)]
                agg = ps.enter_context(nc.psum_tensor("agg", [N, SG * C], F32))
                block = ps.enter_context(nc.Block())

                @block.tensor
                def _(pe):
                    def gather_turn(s):
                        for r in range(SLOTS):
                            k = r % RING
                            pe.wait_ge(slot_copied[k], s * TURN + r // RING + 1)
                            gather_slot(pe, s, r, hot, hot_ready, slot_ready, pad, identb[:], gat[k][:])

                    def sum_turn(s):
                        pe.wait_ge(agg_added, s + 1)
                        for m in range(LAST + 1):
                            pe.wait_ge(weighted, s * (LAST + 1) + m + 1)
                            mm = nc.tensor.matmul(agg[:], identf[:], wires[:, HOME[m], :], start=(m == 0), stop=(m == LAST))
                            mm.then_inc(summed, 1)

                    starts_free(pe, summed)
                    pe.wait_ge(prep, SLOTS)
                    gather_turn(0)
                    with pe.Fori(0, SORTS - 1) as s:
                        gather_turn(s + 1)
                        sum_turn(s)
                    sum_turn(SORTS - 1)

                @block.scalar
                def _(act):
                    starts_free(act, *slot_copied)
                    with act.Fori(0, SORTS) as s:
                        act.wait_ge(first_read, s + 1)
                        for r in range(SLOTS):
                            k = r % RING
                            act.wait_ge(slot_ready[k], s * TURN + r // RING + 1)
                            nc.scalar.copy(raw[:, r, :], gat[k][:].rearrange("p g c -> p (g c)")).then_inc(slot_copied[k], 1)

                @block.vector
                def _(dve):
                    def sort_turn(s, ahead):
                        step = Steps(dve, sorting, HALVES, s)
                        for k in range(RING):
                            dve.wait_ge(slot_copied[k], (s + 1) * TURN + 1)
                        dve.wait_ge(summed, s * (LAST + 1) + 1)
                        slots = list(range(SLOTS)) if ahead else []
                        for n, rows in enumerate(plan):
                            before = 0
                            for (ka, a), (kb, b), low, high in rows:
                                step.wait(before)
                                before = (low is not None) + (high is not None)
                                va = raw[:, a, :] if ka == "raw" else wires[:, a, :]
                                vb = raw[:, b, :] if kb == "raw" else wires[:, b, :]
                                if low is not None:
                                    step(nc.vector.tensor_tensor(wires[:, low, :], va, vb, ALU.min))
                                if high is not None:
                                    step(nc.vector.tensor_tensor(wires[:, high, :], va, vb, ALU.max))
                                if n > first_last and slots:
                                    hot_slot(dve, s + 1, slots.pop(0), hot, hot_ready, slot_ready)
                            step.wait()
                            if n == first_last:
                                dve.sem_inc(first_read, 1)
                        assert not slots
                        step.end()
                        for m in range(LAST + 1):
                            w = wires[:, HOME[m], :].rearrange("p (g c) -> p g c", c=C)
                            nc.vector.tensor_tensor(w, w, om[:, m, bass.ds(s * SG, SG)].unsqueeze(2).broadcast_to([N, SG, C]),
                                                    ALU.mult).then_inc(weighted, 1)
                        dve.wait_ge(summed, (s + 1) * (LAST + 1) + 1)
                        hs = H[:, bass.ds(s * SG, SG), :]
                        nc.vector.tensor_tensor(hs, hs, agg[:].rearrange("p (g c) -> p g c", c=C), ALU.add).then_inc(agg_added, 1)

                    starts_free(dve, first_read, agg_added)
                    step = Steps(dve, prep)
                    V = nc.vector
                    absent_slots(V, step, pad)
                    shape = [N, LAST + 1, B]
                    d, e = [wires[:, k:k + 2, :].rearrange("p a b -> p (a b)").rearrange("p (m g) -> p m g", g=B)
                            for k in (0, 2)]
                    orders = slot_no[:, 0:LAST + 1].unsqueeze(2).broadcast_to(shape)
                    for n, (tau, w) in enumerate(TAUS):
                        step(V.tensor_scalar(pos, count[:], tau, -tau, ALU.mult, ALU.add))
                        step.wait()
                        step(V.tensor_tensor(d, orders, pos.unsqueeze(1).broadcast_to(shape), ALU.subtract))
                        step.wait()
                        step(V.scalar_tensor_tensor(out=e, in0=d, scalar=-1.0, in1=d, op0=ALU.mult, op1=ALU.max))
                        step.wait()
                        step(V.tensor_scalar(d, e, -w, w, ALU.mult, ALU.add))
                        step.wait()
                        if n == 0:
                            step(V.tensor_scalar(om, d, 0.0, None, ALU.max))
                        else:
                            step(V.scalar_tensor_tensor(out=om, in0=d, scalar=0.0, in1=om, op0=ALU.max, op1=ALU.add))
                        step.wait()
                    for r in range(SLOTS):
                        hot_slot(dve, 0, r, hot, hot_ready, slot_ready)
                    with dve.Fori(0, SORTS - 1) as s:
                        sort_turn(s, True)
                    sort_turn(SORTS - 1, False)

        def stage_general(tag, quantiles):
            flag_step, flagged = sem(tag + "flag_step"), sem(tag + "flagged")
            value_ready, spread, pos_turned = sem(tag + "value_ready"), sem(tag + "spread"), sem(tag + "pos_turned")
            chain, rounds = sem(tag + "chain"), sem(tag + "rounds")
            room_a, room_b = take([N, N, C]), take([N, N, C])
            value, part = take([N, C]), take([N, C])
            absent, order = take([N, N]), take([N, N])
            cnt, top = take([N, 1]), take([N, 1])
            over, flag = take([N, 2], BF16), take([N, 1], I32)
            at, dist, hats = take([N, 1]), take([N, N]), take([N, N])
            scratch = nc.dram_tensor(tag + "scratch", [N, C], F32, kind="Internal").ap()
            PAIRS = N // 2
            with ExitStack() as ps:
                fp = ps.enter_context(nc.psum_tensor(tag + "fp", [N, 2], F32))
                pt = ps.enter_context(nc.psum_tensor(tag + "pt", [N, N], F32))
                block = ps.enter_context(nc.Block())

                @block.gpsimd
                def _(pool):
                    nc.gpsimd.iota(order, pattern=[[1, N]], base=0, channel_multiplier=0,
                                   allow_small_or_imprecise_dtypes=True).then_inc(value_ready, 1)

                @block.sync
                def _(sp):
                    sp.wait_ge(flag_step, 4)
                    crowded = sp.value_load(flag[0:1, 0:1])
                    with sp.If(crowded > 0):
                        with sp.Fori(0, B) as g:
                            sp.wait_ge(value_ready, g + 2)
                            sp.dma_start(scratch, value).then_inc(spread, 16)
                            sp.wait_ge(spread, g * 32 + 16)
                            sp.dma_start(room_a.rearrange("p j c -> p (j c)"),
                                         scratch.rearrange("j c -> (j c)").partition_broadcast(N)).then_inc(spread, 16)

                @block.tensor
                def _(pe):
                    pe.wait_ge(flag_step, 3)
                    nc.tensor.matmul(fp[0:1, 0:1], over[:, 0:1], onesb[:, 0:1], start=True, stop=True).then_inc(flagged, 1)
                    pe.wait_ge(flag_step, 4)
                    crowded = pe.value_load(flag[0:1, 0:1])
                    with pe.If(crowded > 0):
                        with pe.Fori(0, B) as g:
                            pe.wait_ge(value_ready, g + 2)
                            nc.tensor.matmul(pt[:], POS[:, bass.ds(g, 1), :].rearrange("p a i -> p (a i)"), identb[:],
                                             start=True, stop=True).then_inc(pos_turned, 1)

                @block.vector
                def _(dve):
                    V = nc.vector
                    fs = Steps(dve, flag_step)
                    fs(V.tensor_reduce(top, count[:], AX, ALU.max))
                    fs(V.memset(over, 0.0))
                    fs.wait()
                    fs(V.tensor_scalar(over[:, 0:1], top, float(SLOTS), None, ALU.is_gt))
                    dve.wait_ge(flagged, 1)
                    fs(V.tensor_copy(flag[0:1, :], fp[0:1, 0:1]))
                    fs.wait()
                    crowded = dve.value_load(flag[0:1, 0:1])
                    with dve.If(crowded > 0):
                        dve.wait_ge(value_ready, 1)
                        with dve.Fori(0, B) as g:
                            step = Steps(dve, chain, 26 if quantiles else 8, g)

                            def do(ins):
                                step(ins)
                                step.wait()

                            def graph(t):
                                return t[:, bass.ds(g, 1), :].rearrange("p a c -> p (a c)")
                            do(V.tensor_tensor(part, PARTS[:, 0, bass.ds(g, 1), :].rearrange("p a c -> p (a c)"),
                                               PARTS[:, 1, bass.ds(g, 1), :].rearrange("p a c -> p (a c)"), ALU.add))
                            V.tensor_tensor(value, part, PARTS[:, 2, bass.ds(g, 1), :].rearrange("p a c -> p (a c)"),
                                            ALU.add).then_inc(value_ready, 1)
                            dve.wait_ge(value_ready, g + 2)
                            dve.wait_ge(pos_turned, g + 1)
                            do(V.tensor_scalar(absent, pt[:], 0.0, BIG, ALU.is_equal, ALU.mult))
                            dve.wait_ge(spread, g * 32 + 32)
                            padding = absent.unsqueeze(2).broadcast_to([N, N, C])
                            if not quantiles:
                                do(V.tensor_tensor(room_b, room_a, padding, ALU.subtract))
                                do(V.tensor_reduce(value, room_b.rearrange("p j c -> p c j"), AX, ALU.max))
                                do(V.tensor_copy(graph(MAXQ), value))
                                do(V.tensor_tensor(room_b, room_a, padding, ALU.add))
                                do(V.tensor_reduce(value, room_b.rearrange("p j c -> p c j"), AX, ALU.min))
                                do(V.tensor_copy(graph(MINQ), value))
                                step.end()
                            else:
                                do(V.tensor_tensor(room_a, room_a, padding, ALU.max))
                                step(V.tensor_copy(cnt, count[:, bass.ds(g, 1)]))
                                with dve.Fori(0, PAIRS) as r:
                                    ev, od = [t.rearrange("p (k e) c -> p k e c", e=2) for t in (room_a, room_b)]
                                    V.tensor_tensor(od[:, :, 0, :], ev[:, :, 0, :], ev[:, :, 1, :], ALU.min).then_inc(rounds, 1)
                                    V.tensor_tensor(od[:, :, 1, :], ev[:, :, 0, :], ev[:, :, 1, :], ALU.max).then_inc(rounds, 1)
                                    dve.wait_ge(rounds, g * (PAIRS * 6) + r * 6 + 2)
                                    up, down = room_b[:, 1:N - 1].rearrange("p (k e) c -> p k e c", e=2), room_a[:, 1:N - 1].rearrange("p (k e) c -> p k e c", e=2)
                                    V.tensor_tensor(down[:, :, 0, :], up[:, :, 0, :], up[:, :, 1, :], ALU.min).then_inc(rounds, 1)
                                    V.tensor_tensor(down[:, :, 1, :], up[:, :, 0, :], up[:, :, 1, :], ALU.max).then_inc(rounds, 1)
                                    V.tensor_copy(room_a[:, 0, :], room_b[:, 0, :]).then_inc(rounds, 1)
                                    V.tensor_copy(room_a[:, N - 1, :], room_b[:, N - 1, :]).then_inc(rounds, 1)
                                    dve.wait_ge(rounds, g * (PAIRS * 6) + r * 6 + 6)
                                step.wait()
                                for n, (tau, w) in enumerate(TAUS):
                                    do(V.tensor_scalar(at, cnt, -tau, tau, ALU.mult, ALU.add))
                                    do(V.tensor_scalar(dist, order, at, None, ALU.add))
                                    do(V.scalar_tensor_tensor(out=absent, in0=dist, scalar=-1.0, in1=dist, op0=ALU.mult, op1=ALU.max))
                                    do(V.tensor_scalar(dist, absent, -w, w, ALU.mult, ALU.add))
                                    do(V.tensor_scalar(dist, dist, 0.0, None, ALU.max))
                                    if n == 0:
                                        do(V.tensor_copy(hats, dist))
                                    else:
                                        do(V.tensor_tensor(hats, hats, dist, ALU.add))
                                do(V.tensor_tensor(room_a, room_a, hats.unsqueeze(2).broadcast_to([N, N, C]), ALU.mult))
                                do(V.tensor_reduce(part, room_a.rearrange("p j c -> p c j"), AX, ALU.add))
                                do(V.tensor_tensor(value, value, part, ALU.add))
                                do(V.tensor_copy(graph(H), value))
                                step.end()

        def stage_mlp():
            used[0] = 0
            staged, turned, out_ready, hid_done, hid_ready, y_done, stepped, masked = [sem("mlp_" + n) for n in (
                "staged", "turned", "out_ready", "hid_done", "hid_ready", "y_done", "stepped", "masked")]
            h4, oT, hid, ym = take([N, QG, C]), take([N, QG // 2, N]), take([N, QG // 2, 2, N]), take([N, QG, C])
            with ExitStack() as ps:
                tp = ps.enter_context(nc.psum_tensor("mlp_tp", [N, QG // 2, N], F32))
                hp = ps.enter_context(nc.psum_tensor("mlp_hp", [N, 2, QG, N], F32))
                yp = ps.enter_context(nc.psum_tensor("mlp_yp", [N, QG, C], F32))
                block = ps.enter_context(nc.Block())

                @block.gpsimd
                def _(pool):
                    with pool.Fori(0, QUADS) as q:
                        pool.wait_ge(turned, q + 1)
                        nc.gpsimd.tensor_copy(h4, H[:, bass.ds(q * QG, QG), :]).then_inc(staged, 1)

                @block.tensor
                def _(pe):
                    starts_free(pe, turned, y_done)
                    with pe.Fori(0, QUADS) as q:
                        pe.wait_ge(staged, q + 1)
                        pe.wait_ge(out_ready, q + 1)
                        for pair in range(QG // 2):
                            mm = nc.tensor.transpose(tp[:, pair, :], h4[:, 2 * pair:2 * pair + 2, :].rearrange("p g c -> p (g c)"),
                                                     identf[:])
                        mm.then_inc(turned, 1)
                        pe.wait_ge(out_ready, q + 2)
                        pe.wait_ge(hid_ready, q * 2 + 1)
                        for odd in range(2):
                            side = slice(odd * C, odd * C + C)
                            mm = nc.tensor.matmul(hp[:, odd, 0:QG // 2, :], w1[side, :], oT[side], start=True, stop=True)
                        mm.then_inc(hid_done, 1)
                        pe.wait_ge(hid_ready, q * 2 + 3)
                        pe.wait_ge(masked, q + 1)
                        for g in range(QG):
                            nc.tensor.matmul(yp[:, g, :], hid[:, g // 2, g % 2, :], w2[:], start=True, stop=False)
                            mm = nc.tensor.matmul(yp[:, g, :], onesf[:], b2[:], start=False, stop=True)
                        mm.then_inc(y_done, 1)

                @block.scalar
                def _(act):
                    starts_free(act, out_ready, hid_ready)
                    with act.Fori(0, QUADS) as q:
                        act.wait_ge(turned, q + 2)
                        nc.scalar.copy(oT, tp[:]).then_inc(out_ready, 1)
                        act.wait_ge(hid_done, q + 1)
                        act.wait_ge(y_done, q + 1)
                        for odd in range(2):
                            nc.scalar.activation(hid[:, :, odd, :], hp[:, odd, 0:QG // 2, :], ACT.Relu,
                                                 bias=b1[:]).then_inc(hid_ready, 1)

                @block.vector
                def _(dve):
                    starts_free(dve, masked, stepped)
                    with dve.Fori(0, QUADS) as q:
                        quad = bass.ds(q * QG, QG)
                        dve.wait_ge(y_done, q + 2)
                        dve.wait_ge(stepped, q + 1)
                        nc.vector.tensor_tensor(ym, yp[:], mask[:, quad].unsqueeze(2).broadcast_to([N, QG, C]),
                                                ALU.mult).then_inc(masked, 1)
                        dve.wait_ge(masked, q + 2)
                        nc.vector.tensor_tensor(X[:, quad, :], X[:, quad, :], ym, ALU.add).then_inc(stepped, 1)

        def stage_columns():
            loaded, squared, multiplied = sem("att_loaded"), sem("att_squared"), sem("att_multiplied")
            col, act_done = sem("att_col"), sem("att_act")
            sq, hw = take([N, B, C]), take([N, B, C])
            wrow, bcol = take([N, 2 * C]), take([N, 1])
            sd, t1, am, dn, rd, sa, na, rt, zc, zm, lp, lm, at, rz, one = [take([N, B]) for _ in range(15)]
            with nc.Block() as block:
                @block.sync
                def _(sp):
                    sp.dma_start(wrow, W["L1_gnn_att_W"].rearrange("k o -> o k").partition_broadcast(N)
                                 .rearrange("p o k -> p (o k)")).then_inc(loaded, 16)
                    sp.dma_start(bcol, W["L1_gnn_att_b"].partition_broadcast(N)).then_inc(loaded, 16)

                @block.gpsimd
                def _(pool):
                    pool.wait_ge(loaded, 32)
                    nc.gpsimd.tensor_tensor(hw, H[:], wrow[:, 0:C].unsqueeze(1).broadcast_to([N, B, C]),
                                            ALU.mult).then_inc(multiplied, 1)

                @block.scalar
                def _(act):
                    nc.scalar.activation(sq, H[:], ACT.Square).then_inc(squared, 1)
                    act.wait_ge(col, 7)
                    nc.scalar.activation(rt, x2, ACT.Sqrt).then_inc(act_done, 1)
                    act.wait_ge(col, 18)
                    nc.scalar.activation(lp, zm, ACT.Ln, bias=one[:, 0:1]).then_inc(act_done, 1)
                    nc.scalar.activation(lm, zm, ACT.Ln, bias=one[:, 0:1], scale=-1.0).then_inc(act_done, 1)

                @block.vector
                def _(dve):
                    V = nc.vector
                    step = Steps(dve, col)
                    step(V.memset(one, 1.0))
                    dve.wait_ge(squared, 1)
                    step(V.tensor_reduce(x2, sq, AX, ALU.add))
                    dve.wait_ge(multiplied, 1)
                    step(V.tensor_reduce(sd, hw, AX, ALU.add))
                    step.wait()
                    step(V.tensor_tensor(sq, H[:], wrow[:, C:2 * C].unsqueeze(1).broadcast_to([N, B, C]), ALU.mult))
                    step.wait()
                    step(V.tensor_reduce(uw, sq, AX, ALU.add))
                    step(V.tensor_scalar(ox, x2, -1.0, 1.0, ALU.mult, ALU.add))
                    step(V.tensor_scalar(t1, x2, -2.0, 1.0, ALU.mult, ALU.add))
                    step.wait()
                    step(V.tensor_tensor(am, t1, x2, ALU.add))
                    step(V.tensor_tensor(dn, x2, x2, ALU.mult))
                    step(V.tensor_scalar(coef, ox, MIN_NORM, None, ALU.max))
                    step.wait()
                    step(V.tensor_tensor(sa, ox, am, ALU.subtract))
                    step(V.tensor_tensor(dn, dn, t1, ALU.add))
                    step.wait()
                    step(V.tensor_scalar(dn, dn, MIN_NORM, None, ALU.max))
                    step.wait()
                    step(V.reciprocal(rd, dn))
                    step.wait()
                    step(V.tensor_tensor(sa, sa, rd, ALU.mult))
                    step.wait()
                    step(V.scalar_tensor_tensor(out=na, in0=sa, scalar=-1.0, in1=sa, op0=ALU.mult, op1=ALU.max))
                    step.wait()
                    dve.wait_ge(act_done, 1)
                    step(V.tensor_tensor(zc, na, rt, ALU.mult))
                    step.wait()
                    step(V.tensor_scalar(zm, zc, MIN_NORM, ATANH_MAX, ALU.max, ALU.min))
                    step(V.tensor_scalar(na, zc, MIN_NORM, None, ALU.max))
                    step.wait()
                    step(V.reciprocal(rz, na))
                    dve.wait_ge(act_done, 3)
                    step(V.tensor_tensor(at, lp, lm, ALU.subtract))
                    step.wait()
                    step(V.tensor_tensor(at, at, rz, ALU.mult))
                    step(V.tensor_tensor(sa, sa, sd, ALU.mult))
                    step(V.tensor_tensor(cu, coef, uw, ALU.mult))
                    step(V.tensor_tensor(cox, coef, ox, ALU.mult))
                    step.wait()
                    step(V.tensor_tensor(at, at, sa, ALU.mult))
                    step(V.tensor_scalar(ncu, cu, -0.5, None, ALU.mult))
                    step(V.tensor_scalar(hcox, cox, 0.5, None, ALU.mult))
                    step.wait()
                    step(V.tensor_tensor(at, at, coef, ALU.mult))
                    step.wait()
                    step(V.tensor_scalar(selfl, at, 0.5, bcol, ALU.mult, ALU.add))
                    step.wait()

        def stage_pairs():
            def turns(name, per=1):
                return Turns(sem("pr_" + name), per)
            built, turned, copied, formed = turns("built", 10), turns("turned", 4), turns("copied", 4), turns("formed", 3)
            clamped, lns, sums, exps = turns("clamped", 2), turns("lns", 2), turns("sums", 2), turns("exps", 2)
            zmin, lnz, ks, lg, sig = turns("zmin"), turns("lnz", 2), turns("ks", 2), turns("lg", 2), turns("sig", 3)
            weighed, w_turned, w_masked, summed, stored = (turns("weighed"), turns("w_turned"), turns("w_masked"),
                                                           turns("summed"), turns("stored"))
            ready = sem("pr_ready")
            R = C + 3
            left = [[take([N, QG, R + 1]) for _ in range(4)] for _ in range(2)]
            turnT = [[take([N, QG, N]) for _ in range(4)] for _ in range(2)]
            a_, b_, s_, t_ = [[take([N, QG, N]) for _ in range(2)] for _ in range(4)]
            wT = [take([N, QG, N]) for _ in range(2)]
            one = take([N, 1])
            ends = take([N, B, 2])
            HALF = QUADS // 2
            with ExitStack() as ps:
                tp = [ps.enter_context(nc.psum_tensor(f"pr_tp{k}", [N, QG, N], F32)) for k in range(2)]
                gg = [ps.enter_context(nc.psum_tensor(f"pr_gg{k}", [N, QG, N], F32)) for k in range(2)]
                den, d2, wt, so = [ps.enter_context(nc.psum_tensor("pr_" + n, [N, QG, N], F32)) for n in ("den", "d2", "wt", "so")]
                block = ps.enter_context(nc.Block())

                @block.gpsimd
                def _(pool):
                    P = nc.gpsimd

                    def build(q, u):
                        J, D, E, G = left[u]
                        quad = bass.ds(q * QG, QG)

                        def c(t):
                            return t[:, quad].unsqueeze(2)
                        turned.wait(pool, q, behind=2)

                        def put(ins):
                            ins.then_inc(built.sem, 1)
                        put(P.tensor_copy(J[:, :, 0:C], H[:, quad, :]))
                        put(P.tensor_copy(J[:, :, C + 1:C + 2], c(x2)))
                        put(P.tensor_copy(J[:, :, C + 2:C + 3], c(uw)))
                        built.wait(pool, q, 1)
                        put(P.tensor_tensor(G[:, :, 0:C], J[:, :, 0:C], c(cu).broadcast_to([N, QG, C]), ALU.mult))
                        put(P.tensor_scalar(D[:, :, 0:C], J[:, :, 0:C], -2.0, None, ALU.mult))
                        put(P.tensor_copy(D[:, :, C + 1:C + 2], c(x2)))
                        put(P.tensor_scalar(E[:, :, 0:C], J[:, :, 0:C], -2.0, None, ALU.mult))
                        put(P.tensor_copy(E[:, :, C:C + 1], c(x2)))
                        put(P.tensor_copy(G[:, :, C:C + 2], c(ncu).broadcast_to([N, QG, 2])))
                        put(P.tensor_copy(G[:, :, C + 2:C + 3], c(hcox)))

                    def add_logs(q, u):
                        lns.wait(pool, q)
                        P.tensor_tensor(s_[u], b_[u], a_[u], ALU.subtract).then_inc(sums.sem, 1)
                        P.tensor_tensor(t_[u], a_[u], b_[u], ALU.add).then_inc(sums.sem, 1)

                    def artanh_over_z(q, u):
                        lnz.wait(pool, q)
                        P.tensor_tensor(a_[u], a_[u], b_[u], ALU.subtract).then_inc(ks.sem, 1)
                        ks.wait(pool, q, 1)
                        P.tensor_tensor(t_[u], a_[u], t_[u], ALU.mult).then_inc(ks.sem, 1)

                    def weigh(q, u):
                        sig.wait(pool, q)
                        P.tensor_tensor(a_[u], s_[u], t_[u], ALU.mult).then_inc(weighed.sem, 1)

                    for t in (built, sums, ks, weighed):
                        t.begin(pool)
                    for t in left[0] + left[1] + [ends]:
                        P.memset(t, 1.0).then_inc(ready, 1)
                    pool.wait_ge(ready, 9)
                    P.tensor_copy(ends[:, :, 1], x2).then_inc(ready, 1)
                    build(0, 0)
                    build(1, 1)

                    def two_quads(q, ahead):
                        add_logs(q, 0)
                        add_logs(q + 1, 1)
                        if ahead:
                            build(q + 2, 0)
                        artanh_over_z(q, 0)
                        artanh_over_z(q + 1, 1)
                        if ahead:
                            build(q + 3, 1)
                        weigh(q, 0)
                        weigh(q + 1, 1)
                    with pool.Fori(0, HALF - 1) as i:
                        two_quads(i * 2, True)
                    two_quads(QUADS - 2, False)

                @block.tensor
                def _(pe):
                    def form(q, u):
                        built.wait(pe, q)
                        for k, t in enumerate(left[u]):
                            if k < 2:
                                copied.wait(pe, q, 4, behind=1)
                            else:
                                copied.wait(pe, q, k - 1)
                            for g in range(QG):
                                mm = nc.tensor.transpose(tp[k % 2][0:R, g, :], t[:, g, 0:R], identf[:])
                            mm.then_inc(turned.sem, 1)
                        copied.wait(pe, q)
                        clamped.wait(pe, q, behind=1)
                        lg.wait(pe, q, 1, behind=2)
                        for k, (o, K) in enumerate(((den, C + 2), (d2, C + 2), (gg[u], C + 3))):
                            for g in range(QG):
                                mm = nc.tensor.matmul(o[:, g, :], turnT[u][k + 1][0:K, g, :], turnT[u][0][0:K, g, :],
                                                      start=True, stop=True)
                            mm.then_inc(formed.sem, 1)

                    def turn_weights(q, u):
                        weighed.wait(pe, q)
                        w_masked.wait(pe, q, behind=1)
                        for g in range(QG):
                            mm = nc.tensor.transpose(wt[:, g, :], a_[u][:, g, :], identf[:])
                        mm.then_inc(w_turned.sem, 1)

                    def sum_neighbours(q, u):
                        w_masked.wait(pe, q)
                        stored.wait(pe, q, behind=1)
                        for g in range(QG):
                            graph = bass.ds(q * QG + g, 1)
                            nc.tensor.matmul(so[:, g, 0:C], wT[u][:, g, :], H[:, graph, :].rearrange("p a c -> p (a c)"),
                                             start=True, stop=True)
                            mm = nc.tensor.matmul(so[:, g, C:C + 2], wT[u][:, g, :], ends[:, graph, :].rearrange("p a c -> p (a c)"),
                                                  start=True, stop=True)
                        mm.then_inc(summed.sem, 1)

                    for t in (turned, formed, w_turned, summed):
                        t.begin(pe)
                    pe.wait_ge(ready, 10)
                    form(0, 0)
                    form(1, 1)

                    def two_quads(q, ahead):
                        for u in range(2):
                            if ahead:
                                form(q + 2 + u, u)
                            turn_weights(q + u, u)
                            sum_neighbours(q + u, u)
                    with pe.Fori(0, HALF - 1) as i:
                        two_quads(i * 2, True)
                    two_quads(QUADS - 2, False)

                @block.scalar
                def _(act):
                    A = nc.scalar.activation

                    def copy_columns(q, u):
                        for k in range(4):
                            turned.wait(act, q, k + 1)
                            if k == 0:
                                formed.wait(act, q, behind=2)
                            nc.scalar.copy(turnT[u][k][0:R], tp[k % 2][0:R]).then_inc(copied.sem, 1)

                    def logs(q, u):
                        clamped.wait(act, q)
                        A(a_[u], a_[u], ACT.Ln).then_inc(lns.sem, 1)
                        A(b_[u], b_[u], ACT.Ln).then_inc(lns.sem, 1)

                    def roots(q, u):
                        sums.wait(act, q)
                        A(s_[u], s_[u], ACT.Exp, scale=0.5).then_inc(exps.sem, 1)
                        A(t_[u], t_[u], ACT.Exp, scale=-0.5).then_inc(exps.sem, 1)

                    def artanh_logs(q, u):
                        zmin.wait(act, q)
                        A(a_[u], s_[u], ACT.Ln, bias=one).then_inc(lnz.sem, 1)
                        A(b_[u], s_[u], ACT.Ln, bias=one, scale=-1.0).then_inc(lnz.sem, 1)

                    def sigmoid(q, u):
                        lg.wait(act, q)
                        lnz.wait(act, q)
                        A(s_[u], b_[u], ACT.Exp, scale=-1.0).then_inc(sig.sem, 1)
                        sig.wait(act, q, 1)
                        A(b_[u], s_[u], ACT.Ln, bias=one).then_inc(sig.sem, 1)
                        sig.wait(act, q, 2)
                        A(s_[u], b_[u], ACT.Exp, scale=-1.0).then_inc(sig.sem, 1)

                    def store(q, u):
                        summed.wait(act, q)
                        nc.scalar.mul(SUMS[:, bass.ds(q * QG, QG), :], so[:, :, 0:C + 2], 0.5).then_inc(stored.sem, 1)

                    for t in (copied, lns, exps, lnz, sig, stored):
                        t.begin(act)
                    act.wait_ge(ready, 10)
                    nc.scalar.activation(one, left[0][0][:, 0, C:C + 1], ACT.Copy)
                    nc.scalar.preload_act_table_set("natural_log_exp_and_others")
                    copy_columns(0, 0)
                    copy_columns(1, 1)

                    def two_quads(q, ahead):
                        for part in (logs, roots, artanh_logs):
                            part(q, 0)
                            part(q + 1, 1)
                        for u in range(2):
                            sigmoid(q + u, u)
                            if ahead:
                                copy_columns(q + 2 + u, u)
                            store(q + u, u)
                    with act.Fori(0, HALF - 1) as i:
                        two_quads(i * 2, True)
                    two_quads(QUADS - 2, False)

                @block.vector
                def _(dve):
                    V = nc.vector

                    def clamp(q, u):
                        formed.wait(dve, q)
                        w_turned.wait(dve, q, behind=2)
                        V.tensor_scalar(a_[u], den[:], MIN_NORM, None, ALU.max).then_inc(clamped.sem, 1)
                        V.tensor_scalar(b_[u], d2[:], 1e-18, None, ALU.max).then_inc(clamped.sem, 1)

                    def bound(q, u):
                        exps.wait(dve, q)
                        V.tensor_scalar(s_[u], s_[u], ATANH_MAX, None, ALU.min).then_inc(zmin.sem, 1)

                    def logits(q, u):
                        ks.wait(dve, q)
                        V.tensor_tensor(b_[u], gg[u][:], t_[u], ALU.mult).then_inc(lg.sem, 1)
                        lg.wait(dve, q, 1)
                        V.scalar_tensor_tensor(out=b_[u], in0=b_[u], scalar=-40.0,
                                               in1=selfl[:, bass.ds(q * QG, QG)].unsqueeze(2).broadcast_to([N, QG, N]),
                                               op0=ALU.max, op1=ALU.add).then_inc(lg.sem, 1)

                    def mask_weights(q, u):
                        w_turned.wait(dve, q)
                        summed.wait(dve, q, behind=2)
                        V.tensor_tensor(wT[u], wt[:], AT[:, bass.ds(q * QG, QG), :], ALU.mult).then_inc(w_masked.sem, 1)

                    for t in (clamped, zmin, lg, w_masked):
                        t.begin(dve)
                    clamp(0, 0)
                    clamp(1, 1)

                    def two_quads(q, ahead):
                        for part in (bound, logits):
                            part(q, 0)
                            part(q + 1, 1)
                        for u in range(2):
                            if ahead:
                                clamp(q + 2 + u, u)
                            mask_weights(q + u, u)
                    with dve.Fori(0, HALF - 1) as i:
                        two_quads(i * 2, True)
                    two_quads(QUADS - 2, False)

        def stage_expmap():
            step_v, pooled, acted = sem("ex_step"), sem("ex_pool"), sem("ex_act")
            cols = [take([N, B]) for _ in range(20)]
            dot, wa, c1, un2, xu, nn, la, th, kk, y2, xy, a1, dn, ca, cb, rn, nr, ff, i1, i2 = cols
            a, u, t, p = [take([N, B, C]) for _ in range(4)]
            S = SUMS[:, :, 0:C]
            bc = [N, B, C]

            def b(c):
                return c.unsqueeze(2).broadcast_to(bc)
            with nc.Block() as block:
                @block.gpsimd
                def _(pool):
                    pool.wait_ge(step_v, 5)
                    nc.gpsimd.tensor_tensor(p, H[:], b(c1), ALU.mult).then_inc(pooled, 1)
                    pool.wait_ge(step_v, 8)
                    nc.gpsimd.tensor_tensor(p, H[:], u, ALU.mult).then_inc(pooled, 1)
                    pool.wait_ge(step_v, 29)
                    nc.gpsimd.tensor_tensor(p, H[:], b(ca), ALU.mult).then_inc(pooled, 1)

                @block.scalar
                def _(act):
                    act.wait_ge(step_v, 8)
                    nc.scalar.activation(a, u, ACT.Square).then_inc(acted, 1)
                    act.wait_ge(step_v, 10)
                    nc.scalar.activation(nn, un2, ACT.Sqrt).then_inc(acted, 1)
                    act.wait_ge(step_v, 13)
                    nc.scalar.activation(th, la, ACT.Tanh).then_inc(acted, 1)
                    act.wait_ge(step_v, 30)
                    nc.scalar.activation(a, u, ACT.Square).then_inc(acted, 1)
                    act.wait_ge(step_v, 32)
                    nc.scalar.activation(nr, rn, ACT.Sqrt).then_inc(acted, 1)

                @block.vector
                def _(dve):
                    V = nc.vector
                    step = Steps(dve, step_v)

                    def do(ins):
                        step(ins)
                        step.wait()
                    do(V.tensor_tensor(a, H[:], S, ALU.mult))
                    do(V.tensor_reduce(dot, a, AX, ALU.add))
                    do(V.scalar_tensor_tensor(out=wa, in0=dot, scalar=-2.0, in1=SUMS[:, :, C], op0=ALU.mult, op1=ALU.add))
                    do(V.tensor_tensor(wa, wa, SUMS[:, :, C + 1], ALU.add))
                    do(V.scalar_tensor_tensor(out=c1, in0=wa, scalar=-1.0, in1=coef, op0=ALU.mult, op1=ALU.mult))
                    do(V.tensor_tensor(t, S, b(cox), ALU.mult))
                    dve.wait_ge(pooled, 1)
                    do(V.tensor_tensor(u, t, p, ALU.add))
                    do(V.tensor_scalar(u, u, CLAMP, -CLAMP, ALU.min, ALU.max))
                    dve.wait_ge(acted, 1)
                    do(V.tensor_reduce(un2, a, AX, ALU.add))
                    do(V.tensor_scalar(un2, un2, MIN_NORM * MIN_NORM, None, ALU.max))
                    dve.wait_ge(acted, 2)
                    do(V.reciprocal(la, coef))
                    do(V.tensor_tensor(la, la, nn, ALU.mult))
                    do(V.reciprocal(i1, nn))
                    dve.wait_ge(pooled, 2)
                    do(V.tensor_reduce(xu, p, AX, ALU.add))
                    dve.wait_ge(acted, 3)
                    do(V.tensor_tensor(kk, th, i1, ALU.mult))
                    do(V.tensor_reduce(y2, a, AX, ALU.add))
                    do(V.tensor_tensor(y2, y2, kk, ALU.mult))
                    do(V.tensor_tensor(y2, y2, kk, ALU.mult))
                    do(V.tensor_tensor(xy, xu, kk, ALU.mult))
                    do(V.tensor_scalar(xy, xy, 2.0, 1.0, ALU.mult, ALU.add))
                    do(V.tensor_tensor(a1, xy, y2, ALU.add))
                    do(V.tensor_tensor(dn, x2, y2, ALU.mult))
                    do(V.tensor_tensor(dn, dn, xy, ALU.add))
                    do(V.tensor_scalar(dn, dn, MIN_NORM, None, ALU.max))
                    do(V.reciprocal(i2, dn))
                    do(V.tensor_tensor(cb, ox, kk, ALU.mult))
                    do(V.tensor_tensor(cb, cb, i2, ALU.mult))
                    do(V.tensor_tensor(t, u, b(cb), ALU.mult))
                    do(V.tensor_tensor(ca, a1, i2, ALU.mult))
                    dve.wait_ge(pooled, 3)
                    do(V.tensor_tensor(u, t, p, ALU.add))
                    dve.wait_ge(acted, 4)
                    do(V.tensor_reduce(rn, a, AX, ALU.add))
                    do(V.tensor_scalar(rn, rn, MIN_NORM * MIN_NORM, None, ALU.max))
                    dve.wait_ge(acted, 5)
                    do(V.reciprocal(ff, nr))
                    do(V.tensor_scalar(ff, ff, BALL, 1.0, ALU.mult, ALU.min))
                    do(V.tensor_tensor(t, u, b(ff), ALU.mult))
                    do(V.tensor_tensor(X[:], X[:], t, ALU.add))

        def stage_degrees():
            summed, copied, col, logged = sem("dg_summed"), sem("dg_copied"), sem("dg_col"), sem("dg_logged")
            one, t = take([N, 1]), take([N, B])
            with nc.psum_tensor("dg", [N, B], F32) as dg, nc.Block() as block:
                @block.tensor
                def _(pe):
                    with pe.Fori(0, B) as g:
                        nc.tensor.matmul(dg[:, bass.ds(g, 1)], AT[:, bass.ds(g, 1), :].rearrange("p a i -> p (a i)"),
                                         onesb[:, 0:1], start=True, stop=True).then_inc(summed, 1)

                @block.scalar
                def _(act):
                    act.wait_ge(col, 2)
                    nc.scalar.activation(t, degree, ACT.Ln, bias=one).then_inc(logged, 1)

                @block.vector
                def _(dve):
                    V = nc.vector
                    step = Steps(dve, col)

                    def do(ins):
                        step(ins)
                        step.wait()
                    do(V.memset(one, 1.0))
                    dve.wait_ge(summed, B)
                    do(V.tensor_copy(degree, dg[:]))
                    do(V.tensor_scalar(rdeg, degree, 1.0, None, ALU.max))
                    do(V.reciprocal(rdeg, rdeg))
                    do(V.tensor_tensor(share, degree, rdeg, ALU.mult))
                    dve.wait_ge(logged, 1)
                    do(V.tensor_scalar(amp, t, 1.0 / AVG_D_LOG, None, ALU.mult))
                    do(V.tensor_scalar(t, t, LN_EPS, None, ALU.max))
                    do(V.reciprocal(t, t))
                    do(V.tensor_scalar(att, t, AVG_D_LOG, None, ALU.mult))

        def load_pna():
            loaded = sem("pna_loaded")
            with nc.Block() as block:
                @block.sync
                def _(sp):
                    for side in (0, C):
                        rows = slice(side, side + C)
                        sp.dma_start(wcat[rows, 0:C], W["L2_gnn_W_pre"][0:C, :]).then_inc(loaded, 16)
                        sp.dma_start(wcat[rows, C:2 * C], W["L2_gnn_W_pre"][C:2 * C, :]).then_inc(loaded, 16)
                        sp.dma_start(wcat[rows, 2 * C:3 * C], W["L2_gnn_W_post"][0:C, :]).then_inc(loaded, 16)
                    for k in range(2):
                        sp.dma_start(wm[:, k], W["L2_gnn_W_post"][C:, :].rearrange("(s k p) c -> k p s c", k=2, p=N)[k])\
                          .then_inc(loaded, 16)
                    sp.dma_start(bias[:, 0:C], W["L2_gnn_b_pre"].partition_broadcast(N)).then_inc(loaded, 16)
                    sp.dma_start(bias[:, 2 * C:3 * C], W["L2_gnn_b_post"].partition_broadcast(N)).then_inc(loaded, 16)
                    sp.wait_ge(loaded, 160)

                @block.gpsimd
                def _(pool):
                    nc.gpsimd.memset(bias[:, C:2 * C], 0.0)

        def stage_neighbour_terms():
            staged, turned, turn_copied, formed, q_ready, hi, r1, mid, r2, lo = [sem("nt_" + n) for n in (
                "staged", "turned", "turn_copied", "formed", "q_ready", "hi", "r1", "mid", "r2", "lo")]
            h4, hT, Q, ra, rb = take([N, QG, C]), take([N, 2, N]), take([N, QG, C]), take([N, QG, C]), take([N, QG, C])
            pt = [take([N, QG, C], BF16) for _ in range(2)]
            with ExitStack() as ps:
                tp = ps.enter_context(nc.psum_tensor("nt_tp", [N, 2, N], F32))
                qp = ps.enter_context(nc.psum_tensor("nt_qp", [N, 2, 512], F32))
                block = ps.enter_context(nc.Block())

                @block.gpsimd
                def _(pool):
                    with pool.Fori(0, QUADS) as q:
                        quad = bass.ds(q * QG, QG)
                        pool.wait_ge(turned, q + 1)
                        nc.gpsimd.tensor_copy(h4, H[:, quad, :]).then_inc(staged, 1)
                        pool.wait_ge(hi, q + 1)
                        nc.gpsimd.tensor_tensor(ra, Q, pt[0], ALU.subtract).then_inc(r1, 1)
                        pool.wait_ge(mid, q + 1)
                        nc.gpsimd.tensor_tensor(rb, ra, pt[1], ALU.subtract).then_inc(r2, 1)

                @block.tensor
                def _(pe):
                    starts_free(pe, turned)
                    with pe.Fori(0, QUADS) as q:
                        pe.wait_ge(staged, q + 1)
                        pe.wait_ge(turn_copied, q + 1)
                        for pair in range(2):
                            mm = nc.tensor.transpose(tp[:, pair, :], h4[:, 2 * pair:2 * pair + 2, :].rearrange("p g c -> p (g c)"),
                                                     identf[:])
                        mm.then_inc(turned, 1)
                        pe.wait_ge(turn_copied, q + 2)
                        pe.wait_ge(q_ready, q + 1)
                        for g in range(QG):
                            side = slice((g % 2) * C, (g % 2) * C + C)
                            mm = nc.tensor.matmul(qp[:, g % 2, (g // 2) * C:(g // 2 + 1) * C], hT[side, g // 2, :],
                                                  wcat[side, C:2 * C], start=True, stop=True)
                            mm.then_inc(formed, 1)

                @block.scalar
                def _(act):
                    starts_free(act, turn_copied, q_ready)
                    with act.Fori(0, QUADS) as q:
                        quad = bass.ds(q * QG, QG)
                        act.wait_ge(turned, q + 2)
                        nc.scalar.copy(hT, tp[:]).then_inc(turn_copied, 1)
                        act.wait_ge(formed, q * 4 + 4)
                        act.wait_ge(lo, q + 1)
                        nc.scalar.copy(Q.rearrange("p (a b) c -> p b a c", b=2),
                                       qp[:, :, 0:2 * C].rearrange("p b (a c) -> p b a c", a=2)).then_inc(q_ready, 1)
                        act.wait_ge(q_ready, q + 2)
                        nc.scalar.copy(pt[0], Q).then_inc(hi, 1)
                        act.wait_ge(r1, q + 1)
                        nc.scalar.copy(pt[1], ra).then_inc(mid, 1)
                        act.wait_ge(r2, q + 1)
                        nc.scalar.copy(PARTS[:, 2, quad, :], rb)

                @block.vector
                def _(dve):
                    starts_free(dve, lo)
                    with dve.Fori(0, QUADS) as q:
                        quad = bass.ds(q * QG, QG)
                        dve.wait_ge(hi, q + 1)
                        nc.vector.tensor_copy(PARTS[:, 0, quad, :], pt[0])
                        dve.wait_ge(mid, q + 1)
                        nc.vector.tensor_copy(PARTS[:, 1, quad, :], pt[1]).then_inc(lo, 1)

        def stage_extremes():
            hot_ready = [sem(f"x_hot_ready{k}") for k in range(RING)]
            slot_ready = [sem(f"x_slot_ready{k}") for k in range(RING)]
            flipped = [sem(f"x_flipped{k}") for k in range(RING)]
            prep, maxed, minned = sem("x_prep"), sem("x_maxed"), sem("x_minned")
            hot = [take([N, SG * N], BF16) for _ in range(RING)]
            pad = take([N, SLOTS, B], BF16)
            minus, twice = take([N, N], BF16), take([N, N], BF16)
            TURN = SLOTS // RING
            with ExitStack() as ps:
                gat = [ps.enter_context(nc.psum_tensor(f"x_gat{b}", [N, SG, C], F32)) for b in range(RING)]
                block = ps.enter_context(nc.Block())

                @block.gpsimd
                def _(pool):
                    step = Steps(pool, prep)
                    step(nc.gpsimd.tensor_scalar(minus, identb[:], -1.0, None, ALU.mult))
                    step(nc.gpsimd.tensor_scalar(twice, identb[:], 2.0, None, ALU.mult))
                    absent_slots(nc.gpsimd, step, pad)

                @block.tensor
                def _(pe):
                    def flip(s, r):
                        k = r % RING
                        pe.wait_ge(maxed, s * SLOTS + r + 1)
                        nc.tensor.matmul(gat[k][:], twice, pad[:, r, bass.ds(s * SG, SG)].unsqueeze(2).broadcast_to([N, SG, C]),
                                         start=False, stop=True, skip_group_check=True).then_inc(flipped[k], 1)
                    pe.wait_ge(prep, SLOTS + 2)
                    with pe.Fori(0, SORTS) as s:
                        for r in range(SLOTS + 2):
                            if r < SLOTS:
                                pe.wait_ge(minned, s * SLOTS + max(r - RING + 1, 0) + 1)
                                gather_slot(pe, s, r, hot, hot_ready, slot_ready, pad, minus, gat[r % RING][:])
                            if r >= 2:
                                flip(s, r - 2)

                @block.vector
                def _(dve):
                    starts_free(dve, minned)
                    with dve.Fori(0, SORTS) as s:
                        top, low = MAXQ[:, bass.ds(s * SG, SG), :], MINQ[:, bass.ds(s * SG, SG), :]
                        ahead = RING - 1
                        for r in range(ahead):
                            hot_slot(dve, s, r, hot, hot_ready, slot_ready)
                        for r in range(SLOTS + 3):
                            if r + ahead < SLOTS:
                                hot_slot(dve, s, r + ahead, hot, hot_ready, slot_ready)
                            if r < SLOTS:
                                k = r % RING
                                dve.wait_ge(slot_ready[k], s * TURN + r // RING + 1)
                                if r == 0:
                                    nc.vector.tensor_copy(top, gat[k][:]).then_inc(maxed, 1)
                                else:
                                    dve.wait_ge(maxed, s * SLOTS + r)
                                    nc.vector.tensor_tensor(top, top, gat[k][:], ALU.max).then_inc(maxed, 1)
                            if r >= 3:
                                m = r - 3
                                k = m % RING
                                dve.wait_ge(flipped[k], s * TURN + m // RING + 1)
                                if m == 0:
                                    nc.vector.tensor_copy(low, gat[k][:]).then_inc(minned, 1)
                                else:
                                    dve.wait_ge(minned, s * SLOTS + m + 1)
                                    nc.vector.tensor_tensor(low, low, gat[k][:], ALU.min).then_inc(minned, 1)

        def stage_pna():
            sg = {n: sem("pn_" + n) for n in ("staged", "turned", "turn_copied", "formed", "biased", "squared", "atf",
                                             "agged", "msq", "pools", "root", "dv", "m_turned", "m_copied", "joined", "added")}
            h4, hT, PQO = take([N, QG, C]), take([N, 2, N]), take([N, QG, 3 * C])
            QQ, ATf, M4, MT = take([N, QG, C]), take([N, QG, N]), take([N, QG, 4 * C]), take([N, QG, 2, N])
            m2, q2, pm, sq, vv, mx, mn, o1, o2, o3, o4 = [take([N, QG, C]) for _ in range(11)]
            eps = take([N, 1])
            bc = [N, QG, C]
            with ExitStack() as ps:
                tp = ps.enter_context(nc.psum_tensor("pn_tp", [N, 2, 256], F32))
                pq = ps.enter_context(nc.psum_tensor("pn_pq", [N, 2, 512], F32))
                ag = ps.enter_context(nc.psum_tensor("pn_ag", [N, QG, N], F32))
                mt = ps.enter_context(nc.psum_tensor("pn_mt", [N, QG, 2, N], F32))
                jo = ps.enter_context(nc.psum_tensor("pn_jo", [N, 2, 512], F32))
                block = ps.enter_context(nc.Block())
                jv = jo[:, :, 0:6 * C].rearrange("p b (a s c) -> p b a s c", a=2, s=3)

                @block.gpsimd
                def _(pool):
                    P = nc.gpsimd
                    starts_free(pool, sg["pools"])
                    with pool.Fori(0, QUADS) as q:
                        quad = bass.ds(q * QG, QG)
                        pool.wait_ge(sg["turned"], q + 1)
                        P.tensor_copy(h4, H[:, quad, :]).then_inc(sg["staged"], 1)
                        pool.wait_ge(sg["biased"], q + 1)
                        pool.wait_ge(sg["dv"], q * 8 + 1)
                        P.tensor_tensor(pm, PQO[:, :, 0:C], share[:, quad].unsqueeze(2).broadcast_to(bc), ALU.mult).then_inc(sg["pools"], 1)
                        P.tensor_tensor(mx, PQO[:, :, 0:C], MAXQ[:, quad, :], ALU.add).then_inc(sg["pools"], 1)
                        P.tensor_tensor(mn, PQO[:, :, 0:C], MINQ[:, quad, :], ALU.add).then_inc(sg["pools"], 1)
                        pool.wait_ge(sg["msq"], q + 1)
                        P.tensor_tensor(vv, q2, sq, ALU.subtract).then_inc(sg["pools"], 1)

                @block.tensor
                def _(pe):
                    starts_free(pe, sg["turned"], sg["agged"], sg["m_turned"], sg["joined"])
                    with pe.Fori(0, QUADS) as q:
                        pe.wait_ge(sg["staged"], q + 1)
                        pe.wait_ge(sg["turn_copied"], q + 1)
                        for pair in range(2):
                            mm = nc.tensor.transpose(tp[:, pair, 0:N], h4[:, 2 * pair:2 * pair + 2, :].rearrange("p g c -> p (g c)"),
                                                     identf[:])
                        mm.then_inc(sg["turned"], 1)
                        pe.wait_ge(sg["turn_copied"], q + 2)
                        for g in range(QG):
                            side = slice((g % 2) * C, (g % 2) * C + C)
                            mm = nc.tensor.matmul(pq[:, g % 2, (g // 2) * 3 * C:(g // 2 + 1) * 3 * C], hT[side, g // 2, :],
                                                  wcat[side, :], start=True, stop=True)
                            mm.then_inc(sg["formed"], 1)
                        pe.wait_ge(sg["squared"], q + 2)
                        pe.wait_ge(sg["atf"], q + 2)
                        pe.wait_ge(sg["biased"], q + 1)
                        for g in range(QG):
                            nc.tensor.matmul(ag[:, g, 0:C], ATf[:, g, :], PQO[:, g, C:2 * C], start=True, stop=True)
                            mm = nc.tensor.matmul(ag[:, g, C:2 * C], ATf[:, g, :], QQ[:, g, :], start=True, stop=True)
                        mm.then_inc(sg["agged"], 1)
                        pe.wait_ge(sg["dv"], q * 8 + 7)
                        pe.wait_ge(sg["root"], q + 1)
                        pe.wait_ge(sg["m_copied"], q * 2 + 1)
                        for g in range(QG):
                            for k in range(2):
                                mm = nc.tensor.transpose(mt[:, g, k, :], M4[:, g, k * N:(k + 1) * N], identf[:])
                        mm.then_inc(sg["m_turned"], 1)
                        pe.wait_ge(sg["m_copied"], q * 2 + 3)
                        for g in range(QG):
                            for k in range(2):
                                mm = nc.tensor.matmul(jo[:, g // 2, (g % 2) * 3 * C:(g % 2 + 1) * 3 * C], MT[:, g, k, :],
                                                      wm[:, k].rearrange("p s c -> p (s c)"), start=(k == 0), stop=(k == 1))
                        mm.then_inc(sg["joined"], 1)

                @block.scalar
                def _(act):
                    S = nc.scalar
                    starts_free(act, sg["turn_copied"], sg["m_copied"], sg["squared"], sg["atf"])
                    act.wait_ge(sg["dv"], 1)
                    nc.scalar.preload_act_table(ACT.Sqrt)
                    with act.Fori(0, QUADS) as q:
                        quad = bass.ds(q * QG, QG)
                        act.wait_ge(sg["turned"], q + 2)
                        S.copy(hT, tp[:, :, 0:N]).then_inc(sg["turn_copied"], 1)
                        act.wait_ge(sg["agged"], q + 1)
                        S.copy(ATf, AT[:, quad, :]).then_inc(sg["atf"], 1)
                        act.wait_ge(sg["biased"], q + 1)
                        S.activation(QQ, PQO[:, :, C:2 * C], ACT.Square).then_inc(sg["squared"], 1)
                        act.wait_ge(sg["dv"], q * 8 + 3)
                        act.wait_ge(sg["pools"], q * 4 + 1)
                        S.activation(sq, m2, ACT.Square).then_inc(sg["msq"], 1)
                        act.wait_ge(sg["dv"], q * 8 + 8)
                        act.wait_ge(sg["m_turned"], q + 1)
                        S.activation(M4[:, :, 3 * C:4 * C], vv, ACT.Sqrt, bias=eps).then_inc(sg["root"], 1)
                        act.wait_ge(sg["m_turned"], q + 2)
                        act.wait_ge(sg["joined"], q + 1)
                        for half in range(2):
                            S.copy(MT[:, 2 * half:2 * half + 2], mt[:, 2 * half:2 * half + 2]).then_inc(sg["m_copied"], 1)

                @block.vector
                def _(dve):
                    V = nc.vector
                    dv = sg["dv"]

                    def wait_dv(q, k):
                        dve.wait_ge(dv, q * 8 + k + 1)
                    V.memset(eps, LN_EPS).then_inc(dv, 1)
                    starts_free(dve, sg["added"])
                    with dve.Fori(0, QUADS) as q:
                        quad = bass.ds(q * QG, QG)
                        dve.wait_ge(sg["formed"], q * 4 + 4)
                        wait_dv(q, 0)
                        V.tensor_tensor(PQO.rearrange("p (a b) c -> p b a c", b=2),
                                        pq[:, :, 0:6 * C].rearrange("p b (a c) -> p b a c", a=2),
                                        bias.unsqueeze(1).unsqueeze(1).broadcast_to([N, 2, 2, 3 * C]), ALU.add).then_inc(sg["biased"], 1)
                        dve.wait_ge(sg["agged"], q + 2)
                        rb = rdeg[:, quad].unsqueeze(2).broadcast_to(bc)
                        V.tensor_tensor(m2, ag[:, :, 0:C], rb, ALU.mult).then_inc(dv, 1)
                        V.tensor_tensor(q2, ag[:, :, C:2 * C], rb, ALU.mult).then_inc(dv, 1)
                        dve.wait_ge(sg["pools"], q * 4 + 4)
                        wait_dv(q, 2)
                        dve.wait_ge(sg["m_turned"], q + 1)
                        V.tensor_tensor(M4[:, :, 0:C], m2, pm, ALU.add).then_inc(dv, 1)
                        V.tensor_scalar(M4[:, :, C:2 * C], mx, -NEG_BIG, None, ALU.max).then_inc(dv, 1)
                        V.tensor_scalar(M4[:, :, 2 * C:3 * C], mn, NEG_BIG, None, ALU.min).then_inc(dv, 1)
                        V.tensor_tensor(o3, PQO[:, :, 2 * C:3 * C], X[:, quad, :], ALU.add).then_inc(dv, 1)
                        dve.wait_ge(sg["pools"], q * 4 + 5)
                        V.tensor_scalar(vv, vv, 0.0, None, ALU.max).then_inc(dv, 1)
                        dve.wait_ge(sg["joined"], q + 2)
                        o1v, o2v = [o.rearrange("p (b a) c -> p b a c", b=2) for o in (o1, o2)]
                        ampb = amp[:, quad].rearrange("p (b a) -> p b a", b=2).unsqueeze(3).broadcast_to([N, 2, 2, C])
                        attb = att[:, quad].rearrange("p (b a) -> p b a", b=2).unsqueeze(3).broadcast_to([N, 2, 2, C])
                        added = sg["added"]
                        dve.wait_ge(added, q * 4 + 1)
                        V.tensor_tensor(o1v, jv[:, :, :, 1, :], ampb, ALU.mult).then_inc(added, 1)
                        V.tensor_tensor(o2v, jv[:, :, :, 2, :], attb, ALU.mult).then_inc(added, 1)
                        V.tensor_tensor(o4.rearrange("p (b a) c -> p b a c", b=2), jv[:, :, :, 0, :],
                                        o3.rearrange("p (b a) c -> p b a c", b=2), ALU.add).then_inc(dv, 1)
                        dve.wait_ge(added, q * 4 + 3)
                        V.tensor_tensor(o1, o1, o2, ALU.add).then_inc(added, 1)
                        dve.wait_ge(added, q * 4 + 4)
                        wait_dv(q, 8)
                        V.tensor_tensor(X[:, quad, :], o1, o4, ALU.add).then_inc(added, 1)

        def stage_gcn():
            HID = W["L3_gnn_W1"].shape[0]
            loaded = sem("gc_loaded")
            staged, turned, turn_copied, atf = [sem("gc_" + n) for n in ("staged", "turned", "turn_copied", "atf")]
            msg_done, msg_ready, agg_done, act_ready, out_done, added = [sem("gc_" + n) for n in (
                "msg_done", "msg_ready", "agg_done", "act_ready", "out_done", "added")]
            h4, hT, ATf = take([N, QG, C]), take([N, 2, N]), take([N, QG, N])
            msg, hid = take([N, QG, HID]), take([N, QG, N])
            y1, y2 = take([N, QG, C]), take([N, QG, C])
            w0, wh = take([N, HID]), take([N, 2, HID])
            wo, bb, bo = take([N, C]), take([N, 3, HID]), take([N, C])
            bcm = [N, QG, HID]
            with ExitStack() as ps:
                tp = ps.enter_context(nc.psum_tensor("gc_tp", [N, 2, 256], F32))
                m0 = ps.enter_context(nc.psum_tensor("gc_m0", [N, 2, 512], F32))
                mp = ps.enter_context(nc.psum_tensor("gc_mp", [N, QG, HID], F32))
                ap = ps.enter_context(nc.psum_tensor("gc_ap", [N, QG, N], F32))
                op = ps.enter_context(nc.psum_tensor("gc_op", [N, 2, 256], F32))
                block = ps.enter_context(nc.Block())
                opv = op[:].rearrange("p a (g c) -> p (a g) c", c=C)[:, 0:QG, :]

                @block.sync
                def _(sp):
                    for side in (0, C):
                        sp.dma_start(w0[side:side + C, :], W["L3_gnn_W0"]).then_inc(loaded, 16)
                    for k in range(2):
                        sp.dma_start(wh[:, k, :], W[f"L3_gnn_W{k + 1}"]).then_inc(loaded, 16)
                    sp.dma_start(wo, W["L3_gnn_Wout"]).then_inc(loaded, 16)
                    for k in range(3):
                        sp.dma_start(bb[:, k, :], W[f"L3_gnn_b{k}"].partition_broadcast(N)).then_inc(loaded, 16)
                    sp.dma_start(bo, W["L3_gnn_bout"].partition_broadcast(N)).then_inc(loaded, 16)

                @block.gpsimd
                def _(pool):
                    with pool.Fori(0, QUADS) as q:
                        pool.wait_ge(turned, q + 1)
                        nc.gpsimd.tensor_copy(h4, H[:, bass.ds(q * QG, QG), :]).then_inc(staged, 1)

                @block.tensor
                def _(pe):
                    starts_free(pe, turned, agg_done, out_done)
                    pe.wait_ge(loaded, 144)
                    with pe.Fori(0, QUADS) as q:
                        pe.wait_ge(staged, q + 1)
                        pe.wait_ge(turn_copied, q + 1)
                        for pair in range(2):
                            mm = nc.tensor.transpose(tp[:, pair, 0:N], h4[:, 2 * pair:2 * pair + 2, :].rearrange("p g c -> p (g c)"),
                                                     identf[:])
                        mm.then_inc(turned, 1)
                        pe.wait_ge(turn_copied, q + 2)
                        for g in range(QG):
                            side = slice((g % 2) * C, (g % 2) * C + C)
                            mm = nc.tensor.matmul(m0[:, g % 2, (g // 2) * HID:(g // 2 + 1) * HID], hT[side, g // 2, :],
                                                  w0[side, :], start=True, stop=True)
                            mm.then_inc(msg_done, 1)
                        pe.wait_ge(atf, q + 1)
                        for layer in range(3):
                            if layer:
                                for g in range(QG):
                                    mm = nc.tensor.matmul(mp[:, g, :], hid[:, g, :], wh[:, layer - 1, :], start=True, stop=True)
                                mm.then_inc(msg_done, 1)
                            pe.wait_ge(msg_ready, q * 3 + layer + 1)
                            for g in range(QG):
                                mm = nc.tensor.matmul(ap[:, g, :], msg[:, g, :], ATf[:, g, :], start=True, stop=True)
                            mm.then_inc(agg_done, 1)
                            pe.wait_ge(act_ready, q * 3 + layer + 1)
                        pe.wait_ge(added, q * 3 + 1)
                        for g in range(QG):
                            mm = nc.tensor.matmul(opv[:, g, :], hid[:, g, :], wo, start=True, stop=True)
                        mm.then_inc(out_done, 1)

                @block.scalar
                def _(act):
                    starts_free(act, turn_copied)
                    with act.Fori(0, QUADS) as q:
                        act.wait_ge(turned, q + 2)
                        nc.scalar.copy(hT, tp[:, :, 0:N]).then_inc(turn_copied, 1)
                        nc.scalar.copy(ATf, AT[:, bass.ds(q * QG, QG), :]).then_inc(atf, 1)
                        for layer in range(3):
                            act.wait_ge(agg_done, q * 3 + layer + 2)
                            if layer == 0:
                                act.wait_ge(out_done, q + 1)
                            nc.scalar.activation(hid, ap[:], ACT.Relu).then_inc(act_ready, 1)

                @block.vector
                def _(dve):
                    V = nc.vector
                    starts_free(dve, added)
                    dve.wait_ge(loaded, 144)
                    with dve.Fori(0, QUADS) as q:
                        quad = bass.ds(q * QG, QG)
                        for layer in range(3):
                            dve.wait_ge(msg_done, q * 6 + 4 + layer)
                            dve.wait_ge(agg_done, q * 3 + layer + 1)
                            if layer == 0:
                                V.tensor_tensor(msg.rearrange("p (a b) c -> p b a c", b=2),
                                                m0[:, :, 0:2 * HID].rearrange("p b (a c) -> p b a c", a=2),
                                                bb[:, 0, :].unsqueeze(1).unsqueeze(1).broadcast_to([N, 2, 2, HID]),
                                                ALU.add).then_inc(msg_ready, 1)
                            else:
                                V.tensor_tensor(msg, mp[:], bb[:, layer, :].unsqueeze(1).broadcast_to(bcm), ALU.add).then_inc(msg_ready, 1)
                        dve.wait_ge(out_done, q + 2)
                        dve.wait_ge(added, q * 3 + 1)
                        V.tensor_tensor(y1, opv, bo.unsqueeze(1).broadcast_to([N, QG, C]), ALU.add).then_inc(added, 1)
                        dve.wait_ge(added, q * 3 + 2)
                        V.tensor_tensor(y2, y1, mask[:, quad].unsqueeze(2).broadcast_to([N, QG, C]), ALU.mult).then_inc(added, 1)
                        dve.wait_ge(added, q * 3 + 3)
                        V.tensor_tensor(X[:, quad, :], X[:, quad, :], y2, ALU.add).then_inc(added, 1)

        def stage_aggregation():
            nonlocal degree, rdeg, share, amp, att, wcat, wm, bias, MAXQ, MINQ
            used[0] = 0
            degree, rdeg, share, amp, att = [take([N, B]) for _ in range(5)]
            wcat, wm, bias = take([N, 3 * C]), take([N, 2, 3, C]), take([N, 3 * C])
            MAXQ, MINQ = take([N, B, C]), take([N, B, C])
            base = used[0]
            for stage in (load_pna, stage_degrees, stage_neighbour_terms, stage_extremes,
                          lambda: stage_general("xg_", False), stage_pna):
                used[0] = base
                stage()

        degree = rdeg = share = amp = att = wcat = wm = bias = MAXQ = MINQ = None

        def stage_attention():
            nonlocal x2, uw, ox, coef, cu, ncu, cox, hcox, selfl, SUMS
            used[0] = 0
            x2, uw, ox, coef, cu, ncu, cox, hcox, selfl = [take([N, B]) for _ in range(9)]
            SUMS = take([N, B, C + 2])
            base = used[0]
            for stage in (stage_columns, stage_pairs, stage_expmap):
                used[0] = base
                stage()

        x2 = uw = ox = coef = cu = ncu = cox = hcox = selfl = SUMS = None

        def stage_store():
            stored = sem("stored")
            with nc.Block() as block:
                @block.sync
                def _(sp):
                    sp.dma_start(out.rearrange("g i c -> i g c"), X[:]).then_inc(stored, 16)
                    sp.wait_ge(stored, 16)

        stage_constants()
        stage_positions("thin_", True)
        stage_norm(0, True)
        stage_quantiles()
        used[0] = 0
        stage_general("qg_", True)
        stage_mlp()
        end_layer()
        stage_norm(1, False)
        stage_attention()
        end_layer()
        stage_positions("pna_", False)
        stage_norm(2, False)
        stage_aggregation()
        stage_norm(3, False)
        used[0] = 0
        stage_gcn()
        stage_store()
        end_layer()


def kernel(**inputs):
    import numpy as _np
    import concourse.bacc as _bacc
    from concourse import mybir as _mybir
    from concourse.bass_utils import run_bass_kernel_spmd as _run

    nc = _bacc.Bacc("TRN2", target_bir_lowering=False, num_devices=1)
    arrays, weights = {}, {}
    for name in inputs:
        a = _np.ascontiguousarray(inputs[name])
        if a.dtype == _np.bool_:
            a = a.view(_np.uint8)
        arrays[f"in_{name}_dram"] = a
        weights[name] = nc.dram_tensor(f"in_{name}_dram", a.shape, _mybir.dt.from_np(a.dtype), kind="ExternalInput").ap()
    x, adj, nodemask = (weights.pop(n) for n in ("x", "adj", "nodemask"))
    out = nc.dram_tensor("out_0_dram", x.shape, _mybir.dt.float32, kind="ExternalOutput").ap()
    build(nc, x, adj, nodemask, weights, out)
    r = _run(nc, [arrays], core_ids=[0])
    return r.results[0]["out_0_dram"]
```

```python
from contextlib import ExitStack

import concourse.bass as bass
from concourse import mybir

ALU = mybir.AluOpType
ACT = mybir.ActivationFunctionType
F32 = mybir.dt.float32
BF16 = mybir.dt.bfloat16
I32 = mybir.dt.int32
U8 = mybir.dt.uint8
AX = mybir.AxisListType.X

SLOTS = 20
RING = 5
QG = 4
SG = 8
BIG = 2.0 ** 100
ROUND = 2.0 ** 23
TAUS = ((0.25, 0.25), (0.5, 0.5), (0.75, 0.25))
TIERS = ((64, 64, 9, 3, 8, 2), (16, 48, 12, 4, 8, 2), (0, 16, 20, 10, 8, 2))
ORDERS = 16
PIECES = 4
MIN_NORM = 1e-15
ATANH_MAX = 1.0 - 2.0 ** -23
LN_EPS = 1e-5
CLAMP = 1000000.0
AVG_D_LOG = 4.86
NEG_BIG = 1000000000.0
BALL = 1.0 - 0.004

SELECTION = {
    9: (
          (6, 7), (4, 5), (2, 3), (5, 7), (0, 1), (0, 2), (4, 6), (1, 3), (5, 6), (0, 4), (1, 2), (3, 7),
          (4, 8), (2, 6), (1, 5), (2, 8), (1, 4), (3, 8), (2, 4), (3, 5), (6, 8), (5, 6), (3, 4)),
    12: (
          (0, 1), (4, 5), (2, 3), (9, 11), (8, 10), (6, 7), (0, 2), (4, 6), (1, 3), (8, 9), (7, 10), (0, 8),
          (5, 7), (2, 9), (1, 11), (3, 7), (10, 11), (3, 10), (7, 11), (1, 5), (0, 4), (6, 9), (9, 10), (5, 9),
          (7, 10), (2, 8), (1, 4), (7, 9), (4, 8), (5, 8), (2, 6), (3, 6), (3, 5), (1, 2), (2, 4), (6, 8),
          (7, 8), (3, 4), (5, 6)),
    20: (
          (2, 3), (4, 5), (0, 1), (6, 7), (14, 15), (10, 11), (18, 19), (8, 9), (9, 11), (5, 7), (0, 2),
          (12, 13), (8, 10), (1, 3), (12, 14), (13, 15), (8, 12), (13, 14), (11, 15), (4, 6), (0, 4), (9, 10),
          (10, 14), (16, 17), (17, 19), (5, 6), (1, 2), (9, 13), (2, 6), (3, 7), (1, 5), (3, 5), (3, 19),
          (11, 13), (2, 4), (1, 2), (16, 18), (17, 18), (10, 12), (2, 18), (9, 10), (2, 10), (13, 14), (0, 3),
          (7, 19), (5, 6), (5, 13), (1, 9), (11, 12), (3, 4), (0, 8), (5, 9), (4, 12), (7, 15), (6, 14), (4, 8),
          (3, 11), (14, 18), (6, 10), (10, 14), (2, 4), (1, 2), (7, 11), (8, 16), (7, 9), (11, 13), (3, 17),
          (2, 3), (13, 14), (10, 16), (12, 16), (9, 17), (4, 8), (14, 17), (11, 14), (16, 19), (3, 8), (5, 9),
          (6, 10), (13, 14), (14, 16), (6, 8), (9, 12), (13, 14), (11, 13), (7, 10), (7, 9), (3, 5), (10, 12),
          (7, 8), (3, 4), (11, 12), (9, 10), (5, 6), (15, 16)),
}


def layered(comparators):
    layers, depth = [], {}
    for a, b in comparators:
        at = max(depth.get(a, 0), depth.get(b, 0))
        if at == len(layers):
            layers.append([])
        layers[at].append((a, b))
        depth[a] = depth[b] = at + 1
    return layers


def live_halves(layers, outputs):
    live, kept = set(outputs), []
    for layer in reversed(layers):
        rows = [(a, b, a in live, b in live) for a, b in layer if a in live or b in live]
        for a, b, _, _ in rows:
            live |= {a, b}
        kept.insert(0, rows)
    return kept


class Steps:
    def __init__(self, eng, sem, per=0, turn=0):
        self.eng, self.sem, self.per, self.turn, self.k = eng, sem, per, turn, 0

    def __call__(self, ins):
        ins.then_inc(self.sem, 1)
        self.k += 1
        return ins

    def wait(self, back=0):
        if self.k > back:
            self.eng.wait_ge(self.sem, self.turn * self.per + self.k - back)

    def end(self):
        assert self.per == self.k, (self.per, self.k)


class Turns:
    def __init__(self, sem, per=1):
        self.sem, self.per = sem, per

    def begin(self, eng):
        eng.sem_inc(self.sem, 2 * self.per)

    def wait(self, eng, turn, k=None, behind=0):
        k = self.per if k is None else k
        eng.wait_ge(self.sem, (turn + (2 - behind)) * self.per + k if behind < 2 else turn * self.per + k)


def starts_free(eng, *sems):
    for s in sems:
        eng.sem_inc(s, 1)


def build(nc, x, adj, nodemask, W, out, stop=99):
    B, N, C = x.shape
    assert N == 128 and C == 64 and B % SG == 0
    HID = W["L0_gnn_W1"].shape[1]
    QUADS, SORTS = B // QG, B // SG
    with ExitStack() as ctx:
        def sb(name, shape, dt=F32):
            return ctx.enter_context(nc.sbuf_tensor(name, shape, dt))

        layer_sems = []

        def sem(name):
            layer_sems.append(nc.alloc_semaphore(name=name))
            return layer_sems[-1]

        def end_layer():
            nc.clear_and_free_semaphores(list(layer_sems))
            nc.all_engine_barrier()
            layer_sems.clear()

        X = sb("X", [N, B, C])
        H = sb("H", [N, B, C])
        AT = sb("AT", [N, B, N], BF16)
        POS = sb("POS", [N, B, N], BF16)
        PARTS = sb("PARTS", [N, 3, B, C], BF16)
        identf = sb("identf", [N, N])
        identb = sb("identb", [N, N], BF16)
        offdiag = sb("offdiag", [N, N], BF16)
        upper = sb("upper", [N, N], BF16)
        onesb = sb("onesb", [N, N], BF16)
        onesf = sb("onesf", [1, N])
        slot_no = sb("slot_no", [N, SLOTS])
        mask = sb("mask", [N, B])
        count = sb("count", [N, B])
        w1 = sb("w1", [2 * C, HID])
        b1 = sb("b1", [HID, 1])
        w2 = sb("w2", [HID, C])
        b2 = sb("b2", [1, C])
        ROOM = 29736
        room = sb("room", [N, ROOM])
        used = [0]

        def take(shape, dt=F32):
            size = 1
            for s in shape[1:]:
                size *= s
            words = size if dt == F32 or dt == I32 else size // 2
            a = used[0]
            used[0] += words
            assert used[0] <= ROOM, used[0]
            piece = room[0:shape[0], a:a + words]
            if dt != F32:
                piece = piece.bitcast(dt)
            names = "abcd"[:len(shape) - 1]
            if len(names) > 1:
                piece = piece.rearrange("p (" + " ".join(names) + ") -> p " + " ".join(names),
                                        **{n: s for n, s in zip(names, shape[1:])})
            return piece

        def stage_constants():
            used[0] = 0
            loaded, made, turned = sem("loaded"), sem("made"), sem("turned")
            mrow8, mrow = take([N, N // 4]), take([N, N])
            mrow8 = mrow8.bitcast(U8)
            with nc.psum_tensor("mT", [N, B], F32) as mT, nc.Block() as block:
                @block.sync
                def _(sp):
                    sp.dma_start(mrow8[0:B, :], nodemask).then_inc(loaded, 16)
                    sp.dma_start(X[:], x.rearrange("g i c -> i g c")).then_inc(loaded, 16)
                    sp.dma_start(w1[0:C, :], W["L0_gnn_W1"]).then_inc(loaded, 16)
                    sp.dma_start(w1[C:2 * C, :], W["L0_gnn_W1"]).then_inc(loaded, 16)
                    sp.dma_start(b1[:], W["L0_gnn_b1"].rearrange("(h a) -> h a", a=1)).then_inc(loaded, 16)
                    sp.dma_start(w2[:], W["L0_gnn_W2"]).then_inc(loaded, 16)
                    sp.dma_start(b2[:], W["L0_gnn_b2"].rearrange("(a c) -> a c", a=1)).then_inc(loaded, 16)
                    sp.wait_ge(loaded, 112)

                @block.gpsimd
                def _(pool):
                    step = Steps(pool, made)
                    step(nc.gpsimd.memset(onesf[:], 1.0))
                    step(nc.gpsimd.memset(onesb[:], 1.0))
                    step(nc.gpsimd.memset(identf[:], 0.0))
                    step.wait()
                    step(nc.gpsimd.affine_select(out=identf[:], in_=identf[:], compare_op=ALU.not_equal,
                                                 fill=1.0, base=0, pattern=[[-1, N]], channel_multiplier=1))
                    step(nc.gpsimd.affine_select(out=upper[:], in_=onesb[:], compare_op=ALU.is_ge,
                                                 fill=0.0, base=0, pattern=[[1, N]], channel_multiplier=-1))
                    step(nc.gpsimd.affine_select(out=offdiag[:], in_=onesb[:], compare_op=ALU.not_equal,
                                                 fill=0.0, base=0, pattern=[[-1, N]], channel_multiplier=1))
                    step(nc.gpsimd.iota(slot_no[:], pattern=[[1, SLOTS]], base=0, channel_multiplier=0,
                                        allow_small_or_imprecise_dtypes=True))
                    step.wait()
                    step(nc.gpsimd.tensor_copy(identb[:], identf[:]))
                    pool.wait_ge(loaded, 112)
                    step(nc.gpsimd.tensor_copy(mrow[0:B, :], mrow8[0:B, :]))

                @block.tensor
                def _(pe):
                    pe.wait_ge(made, 9)
                    nc.tensor.transpose(mT[:], mrow[0:B, :], identf[0:B, 0:B]).then_inc(turned, 1)

                @block.vector
                def _(dve):
                    dve.wait_ge(turned, 1)
                    nc.vector.tensor_copy(mask[:], mT[:]).then_inc(made, 1)

        def stage_positions(tag, thinned):
            used[0] = 0
            kept_ready, summed, step_done = sem(tag + "kept_ready"), sem(tag + "summed"), sem(tag + "step_done")
            if thinned:
                adj_in, adj_free, turned, at_ready = sem("adj_in"), sem("adj_free"), sem("adj_turned"), sem("at_ready")
                neigh_ready, ranked, rem_ready, rem_both = sem("neigh_ready"), sem("ranked"), sem("rem_ready"), sem("rem_both")
            A = take([N, QG, N])
            nat = take([N, QG, N], BF16)
            natT = take([N, QG, N], BF16)
            e1, e2 = take([N, QG, N]), take([N, QG, N])
            rem = take([N, QG, N], BF16)
            keepT = take([N, QG, N], BF16)
            small = [take([N, QG]) for _ in range(8)]
            with ExitStack() as ps:
                tA = ps.enter_context(nc.psum_tensor(tag + "tA", [N, QG, N], F32))
                rank = ps.enter_context(nc.psum_tensor(tag + "rank", [N, QG, N], F32))
                both = ps.enter_context(nc.psum_tensor(tag + "both", [N, QG, N], F32))
                cum = ps.enter_context(nc.psum_tensor(tag + "cum", [N, QG, N], F32))
                nv = ps.enter_context(nc.psum_tensor(tag + "nv", [N, QG], F32))
                block = ps.enter_context(nc.Block())
                bc = [N, QG, N]

                if thinned:
                    @block.sync
                    def _(sp):
                        with sp.Fori(0, QUADS) as q:
                            sp.wait_ge(adj_free, q + 1)
                            sp.dma_start(A, adj[bass.ds(q * QG, QG)].rearrange("g i j -> i g j")).then_inc(adj_in, 16)

                    @block.scalar
                    def _(act):
                        starts_free(act, at_ready)
                        with act.Fori(0, QUADS) as q:
                            act.wait_ge(turned, q + 1)
                            nc.scalar.copy(AT[:, bass.ds(q * QG, QG), :], tA[:]).then_inc(at_ready, 1)

                @block.tensor
                def _(pe):
                    with pe.Fori(0, QUADS) as q:
                        if thinned:
                            pe.wait_ge(adj_in, q * 16 + 16)
                            pe.wait_ge(at_ready, q + 1)
                            for g in range(QG):
                                mm = nc.tensor.transpose(tA[:, g, :], A[:, g, :], identf[:])
                            mm.then_inc(turned, 1)
                            pe.wait_ge(neigh_ready, q * 2 + 2)
                            for g in range(QG):
                                mm = nc.tensor.matmul(rank[:, g, :], natT[:, g, :], upper[:], start=True, stop=True)
                            mm.then_inc(ranked, 1)
                            pe.wait_ge(rem_ready, q + 1)
                            for g in range(QG):
                                nc.tensor.matmul(both[:, g, :], rem[:, g, :], identb[:], start=True, stop=False)
                                mm = nc.tensor.matmul(both[:, g, :], identb[:], rem[:, g, :], start=False, stop=True)
                            mm.then_inc(rem_both, 1)
                        else:
                            pe.wait_ge(kept_ready, q + 1)
                            nc.tensor.matmul(cum[:], upper[:], keepT, start=True, stop=True)
                            for g in range(QG):
                                mm = nc.tensor.matmul(nv[:, g:g + 1], keepT[:, g, :], onesb[:, 0:1], start=True, stop=True)
                            mm.then_inc(summed, 1)

                @block.vector
                def _(dve):
                    if thinned:
                        starts_free(dve, adj_free)
                    with dve.Fori(0, QUADS) as q:
                        quad = bass.ds(q * QG, QG)
                        step = Steps(dve, step_done, 13 if thinned else 1, q)
                        if thinned:
                            off = offdiag[:].unsqueeze(1).broadcast_to(bc)
                            dve.wait_ge(adj_in, q * 16 + 16)
                            nc.vector.scalar_tensor_tensor(out=nat, in0=A, scalar=0.0, in1=off,
                                                           op0=ALU.is_gt, op1=ALU.mult).then_inc(neigh_ready, 1)
                            dve.wait_ge(at_ready, q + 2)
                            nc.vector.scalar_tensor_tensor(out=natT, in0=AT[:, quad, :], scalar=0.0, in1=off,
                                                           op0=ALU.is_gt, op1=ALU.mult).then_inc(neigh_ready, 1)
                            dve.wait_ge(neigh_ready, q * 2 + 2)
                            dve.sem_inc(adj_free, 1)
                            dve.wait_ge(ranked, q + 1)
                            nb = rank[:, :, N - 1]
                            half, up, skip, cond, cm, sk1, sk2, sk0 = small
                            step(nc.vector.tensor_scalar(half, nb, 0.5, 0.25, ALU.mult, ALU.add))
                            step.wait()
                            step(nc.vector.tensor_scalar(up, half, ROUND, None, ALU.add))
                            step.wait()
                            step(nc.vector.tensor_scalar(skip, up, ROUND, None, ALU.subtract))
                            step(nc.vector.scalar_tensor_tensor(out=cond, in0=nb, scalar=10.5, in1=mask[:, quad],
                                                                op0=ALU.is_gt, op1=ALU.mult))
                            step.wait()
                            step(nc.vector.tensor_scalar(cm, cond, 1.0, None, ALU.subtract))
                            step(nc.vector.tensor_tensor(sk0, skip, cond, ALU.mult))
                            step.wait()
                            step(nc.vector.tensor_tensor(sk1, sk0, cm, ALU.add))
                            step.wait()
                            step(nc.vector.tensor_scalar(sk2, sk1, 2.0, None, ALU.mult))
                            step.wait()
                            step(nc.vector.tensor_tensor(e1, rank[:], sk1.unsqueeze(2).broadcast_to(bc), ALU.is_equal))
                            step(nc.vector.tensor_tensor(e2, rank[:], sk2.unsqueeze(2).broadcast_to(bc), ALU.is_equal))
                            step.wait()
                            step(nc.vector.tensor_tensor(e1, e1, e2, ALU.add))
                            step.wait()
                            nc.vector.tensor_tensor(rem, e1, nat, ALU.mult).then_inc(rem_ready, 1)
                            step(nc.vector.tensor_tensor(e2, nat, identb[:].unsqueeze(1).broadcast_to(bc), ALU.add))
                            step.wait()
                            dve.wait_ge(rem_both, q + 1)
                            nc.vector.scalar_tensor_tensor(out=POS[:, quad, :], in0=both[:], scalar=0.0, in1=e2,
                                                           op0=ALU.is_equal, op1=ALU.mult).then_inc(kept_ready, 1)
                            dve.wait_ge(kept_ready, q + 1)
                            step(nc.vector.tensor_reduce(count[:, quad], POS[:, quad, :], AX, ALU.add))
                            step.wait()
                            step.end()
                        else:
                            nc.vector.tensor_scalar(keepT, AT[:, quad, :], 0.0, None, ALU.is_gt).then_inc(kept_ready, 1)
                            dve.wait_ge(kept_ready, q + 1)
                            dve.wait_ge(summed, q + 1)
                            nc.vector.tensor_tensor(POS[:, quad, :], cum[:], keepT, ALU.mult)
                            step(nc.vector.tensor_copy(count[:, quad], nv[:]))
                            step.wait()
                            step.end()

        centred, squared, var_ready, root_ready, mean_ready, h_ready, norm_step = [
            ctx.enter_context(nc.semaphore(n)) for n in ("centred", "squared", "var", "root", "mean", "h", "norm_step")]

        def stage_norm(n, parts):
            used[0] = 0
            CH = B // 4
            if parts:
                hi_ready, r1_ready, mid_ready, r2_ready = [sem("norm_" + w) for w in ("hi", "r1", "mid", "r2")]
            mean, var, root, rstd = [take([N, B]) for _ in range(4)]
            eps = take([N, 1])
            xc, sq = take([N, B, C]), take([N, B, C])
            rest = take([N, B, C])
            bc = [N, CH, C]
            with nc.Block() as block:
                @block.gpsimd
                def _(pool):
                    with pool.Fori(0, 4) as t:
                        ch = bass.ds(t * CH, CH)
                        pool.wait_ge(mean_ready, t + 5 * n + 2)
                        nc.gpsimd.tensor_tensor(xc[:, ch], X[:, ch], mean[:, ch].unsqueeze(2).broadcast_to(bc),
                                                ALU.add).then_inc(centred, 1)
                    if parts:
                        with pool.Fori(0, 4) as t:
                            ch = bass.ds(t * CH, CH)
                            pool.wait_ge(hi_ready, t + 1)
                            nc.gpsimd.tensor_tensor(rest[:, ch], H[:, ch], PARTS[:, 0, ch], ALU.subtract).then_inc(r1_ready, 1)
                        with pool.Fori(0, 4) as t:
                            ch = bass.ds(t * CH, CH)
                            pool.wait_ge(mid_ready, t + 1)
                            nc.gpsimd.tensor_tensor(xc[:, ch], rest[:, ch], PARTS[:, 1, ch], ALU.subtract).then_inc(r2_ready, 1)

                @block.scalar
                def _(act):
                    with act.Fori(0, 4) as t:
                        ch = bass.ds(t * CH, CH)
                        act.wait_ge(centred, t + 4 * n + 1)
                        nc.scalar.activation(sq[:, ch], xc[:, ch], ACT.Square).then_inc(squared, 1)
                    act.wait_ge(var_ready, 4 * n + 4)
                    act.wait_ge(mean_ready, 5 * n + 1)
                    nc.scalar.activation(root, var, ACT.Sqrt, bias=eps, scale=1.0 / C).then_inc(root_ready, 1)
                    if parts:
                        with act.Fori(0, 4) as t:
                            ch = bass.ds(t * CH, CH)
                            act.wait_ge(h_ready, t + 4 * n + 1)
                            nc.scalar.copy(PARTS[:, 0, ch], H[:, ch]).then_inc(hi_ready, 1)
                        with act.Fori(0, 4) as t:
                            ch = bass.ds(t * CH, CH)
                            act.wait_ge(r1_ready, t + 1)
                            nc.scalar.copy(PARTS[:, 1, ch], rest[:, ch]).then_inc(mid_ready, 1)
                        with act.Fori(0, 4) as t:
                            ch = bass.ds(t * CH, CH)
                            act.wait_ge(r2_ready, t + 1)
                            nc.scalar.copy(PARTS[:, 2, ch], xc[:, ch])

                @block.vector
                def _(dve):
                    nc.vector.memset(eps, LN_EPS).then_inc(mean_ready, 1)
                    with dve.Fori(0, 4) as t:
                        ch = bass.ds(t * CH, CH)
                        nc.vector.tensor_reduce(root[:, ch], X[:, ch], AX, ALU.add).then_inc(norm_step, 1)
                        dve.wait_ge(norm_step, t + 5 * n + 1)
                        nc.vector.tensor_scalar(mean[:, ch], root[:, ch], -1.0 / C, None, ALU.mult).then_inc(mean_ready, 1)
                    with dve.Fori(0, 4) as t:
                        ch = bass.ds(t * CH, CH)
                        dve.wait_ge(squared, t + 4 * n + 1)
                        nc.vector.tensor_reduce(var[:, ch], sq[:, ch], AX, ALU.add).then_inc(var_ready, 1)
                    dve.wait_ge(root_ready, n + 1)
                    nc.vector.reciprocal(rstd, root).then_inc(norm_step, 1)
                    dve.wait_ge(norm_step, 5 * n + 5)
                    with dve.Fori(0, 4) as t:
                        ch = bass.ds(t * CH, CH)
                        nc.vector.scalar_tensor_tensor(out=H[:, ch], in0=xc[:, ch], scalar=0.0,
                                                       in1=rstd[:, ch].unsqueeze(2).broadcast_to(bc),
                                                       op0=ALU.max, op1=ALU.mult).then_inc(h_ready, 1)

        def hot_slot(dve, s, r, hot, hot_ready, slot_ready):
            k = r % RING
            if r >= RING:
                dve.wait_ge(slot_ready[k], s * (SLOTS // RING) + r // RING)
            nc.vector.tensor_scalar(hot[k], POS[:, bass.ds(s * SG, SG), :].rearrange("p g i -> p (g i)"), float(r + 1),
                                    None, ALU.is_equal).then_inc(hot_ready[k], 1)

        def gather_slot(pe, s, r, hot, hot_ready, slot_ready, pad, pad_sign, piece):
            k = r % RING
            pe.wait_ge(hot_ready[k], s * (SLOTS // RING) + r // RING + 1)
            nc.tensor.matmul(piece, pad_sign, pad[:, r, bass.ds(s * SG, SG)].unsqueeze(2).broadcast_to([N, SG, C]),
                             start=True, stop=True)
            for g in range(SG):
                for part in range(3):
                    mm = nc.tensor.matmul(piece[:, g, :], hot[k][:, g * N:(g + 1) * N],
                                          PARTS[:, part, bass.ds(s * SG + g, 1), :].rearrange("p a c -> p (a c)"),
                                          start=False, stop=True, skip_group_check=True)
            mm.then_inc(slot_ready[k], 1)

        def absent_slots(eng, step, pad):
            for r in range(SLOTS):
                step(eng.tensor_scalar(pad[:, r, :], count[:], float(r), BIG, ALU.is_le, ALU.mult))

        def stage_order():
            prepared, diag_ready, keyed, above_ready, ranked, placed_ready, moved, kept_ready, counted, placed = [
                sem("ord_" + n) for n in ("prepared", "diag", "keyed", "above", "ranked", "hot", "moved", "kept",
                                          "counted", "placed")]
            diag, above, P, keep = [take([N, SG, N], BF16) for _ in range(4)]
            key, number, back, order = take([N, B]), take([N, 1]), take([N, 1]), take([N, N])
            times, last = take([N, N], BF16), take([N, N], BF16)
            at, dist, size, hats = take([N, 1]), take([N, ORDERS]), take([N, ORDERS]), take([N, ORDERS])
            HALF = 4
            bc = [N, SG, N]
            with ExitStack() as ps:
                kb = ps.enter_context(nc.psum_tensor("ord_kb", [N, SG, N], F32))
                rb = ps.enter_context(nc.psum_tensor("ord_rb", [N, SG, N], F32))
                kp = ps.enter_context(nc.psum_tensor("ord_kp", [N, SG, N], F32))
                rc = ps.enter_context(nc.psum_tensor("ord_rc", [N, SG], F32))
                block = ps.enter_context(nc.Block())

                @block.gpsimd
                def _(pool):
                    step = Steps(pool, prepared)
                    for t, pattern, base, mult in ((number, [[0, 1]], 0, 1), (back, [[0, 1]], N - 1, -1),
                                                   (order, [[1, N]], 0, 0)):
                        step(nc.gpsimd.iota(t, pattern=pattern, base=base, channel_multiplier=mult,
                                            allow_small_or_imprecise_dtypes=True))
                    step(nc.gpsimd.memset(times, float(N)))
                    step(nc.gpsimd.memset(minus_big, -BIG))
                    step(nc.gpsimd.memset(big_share, BIG / N))
                    with pool.Fori(0, SORTS) as s:
                        pool.wait_ge(keyed, s + 1)
                        nc.gpsimd.tensor_tensor(diag, identb[:].unsqueeze(1).broadcast_to(bc),
                                                count[:, bass.ds(s * SG, SG)].unsqueeze(2).broadcast_to(bc),
                                                ALU.mult).then_inc(diag_ready, 1)

                @block.tensor
                def _(pe):
                    starts_free(pe, keyed)
                    pe.wait_ge(prepared, 8)
                    with pe.Fori(0, SORTS) as s:
                        pe.wait_ge(diag_ready, s + 1)
                        pe.wait_ge(placed, s * 2 + 1)
                        for h in range(0, SG, HALF):
                            nc.tensor.matmul(kb[:, h:h + HALF, :], times, diag[:, h:h + HALF, :], start=True, stop=False)
                            mm = nc.tensor.matmul(kb[:, h:h + HALF, :], onesb[:], last.unsqueeze(1).broadcast_to([N, HALF, N]),
                                                  start=False, stop=True)
                        mm.then_inc(keyed, 1)
                        pe.wait_ge(above_ready, s + 1)
                        for h in range(0, SG, HALF):
                            nc.tensor.matmul(rb[:, h:h + HALF, :], onesb[:], above[:, h:h + HALF, :], start=True, stop=True)
                        for g in range(SG):
                            mm = nc.tensor.matmul(rc[:, g:g + 1], above[:, g, :], onesb[:, 0:1], start=True, stop=True)
                        mm.then_inc(ranked, 1)
                        pe.wait_ge(placed_ready, s * 3 + 3)
                        pe.wait_ge(kept_ready, s + 1)
                        for g in range(SG):
                            mm = nc.tensor.matmul(kp[:, g, :], POS[:, bass.ds(s * SG + g, 1), :].rearrange("p a i -> p (a i)"),
                                                  P[:, g, :], start=True, stop=True)
                        mm.then_inc(moved, 1)
                        pe.wait_ge(kept_ready, s + 2)
                        for h in range(0, SG, HALF):
                            nc.tensor.matmul(kb[:, h:h + HALF, :], upper[:], keep[:, h:h + HALF, :], start=True, stop=True)
                            mm = nc.tensor.matmul(rb[:, h:h + HALF, :], onesb[:], keep[:, h:h + HALF, :], start=True, stop=True)
                        mm.then_inc(counted, 1)

                @block.scalar
                def _(act):
                    starts_free(act, kept_ready)
                    with act.Fori(0, SORTS) as s:
                        act.wait_ge(moved, s + 1)
                        act.wait_ge(placed, s * 2 + 1)
                        nc.scalar.copy(keep, kp[:]).then_inc(kept_ready, 1)

                @block.vector
                def _(dve):
                    V = nc.vector
                    starts_free(dve, placed)
                    dve.wait_ge(prepared, 6)
                    V.tensor_scalar(last, identb[:], back, None, ALU.mult).then_inc(prepared, 1)
                    V.tensor_scalar(key, count[:], float(N), back, ALU.mult, ALU.add).then_inc(prepared, 1)
                    dve.wait_ge(prepared, 8)
                    with dve.Fori(0, SORTS) as s:
                        turn = bass.ds(s * SG, SG)
                        dve.wait_ge(keyed, s + 2)
                        V.tensor_tensor(above, kb[:], key[:, turn].unsqueeze(2).broadcast_to(bc), ALU.is_lt).then_inc(above_ready, 1)
                        dve.wait_ge(ranked, s + 1)
                        V.tensor_tensor(P, order.unsqueeze(1).broadcast_to(bc), rc[:].unsqueeze(2).broadcast_to(bc),
                                        ALU.is_equal).then_inc(placed_ready, 1)
                        V.tensor_copy(RANK[:, turn], rc[:]).then_inc(placed_ready, 1)
                        V.tensor_scalar(PT[:, turn, :], rb[:], number, None, ALU.is_equal).then_inc(placed_ready, 1)
                        dve.wait_ge(counted, s + 1)
                        V.tensor_tensor(POS[:, turn, :], kb[:], keep, ALU.mult).then_inc(placed, 1)
                        V.tensor_scalar(COUNT1[:, bass.ds(s * (SG // 2), SG // 2)].rearrange("n p i e -> n p e i"),
                                        rb[:].rearrange("n (p e) i -> n p e i", e=2), number, None,
                                        ALU.is_equal).then_inc(placed, 1)
                    step = Steps(dve, prepared)
                    step.k = 8
                    for n, (tau, w) in enumerate(TAUS):
                        step(V.tensor_scalar(at, number, tau, -tau, ALU.mult, ALU.add))
                        step.wait()
                        step(V.tensor_scalar(dist, slot_no[:, 0:ORDERS], at, None, ALU.subtract))
                        step.wait()
                        step(V.scalar_tensor_tensor(out=size, in0=dist, scalar=-1.0, in1=dist, op0=ALU.mult, op1=ALU.max))
                        step.wait()
                        step(V.tensor_scalar(dist, size, -w, w, ALU.mult, ALU.add))
                        step.wait()
                        if n == 0:
                            step(V.tensor_scalar(hats, dist, 0.0, None, ALU.max))
                        else:
                            step(V.scalar_tensor_tensor(out=hats, in0=dist, scalar=0.0, in1=hats, op0=ALU.max, op1=ALU.add))
                        step.wait()
                    step(V.memset(WEIGHTS, 0.0))
                    step.wait()
                    step(V.tensor_copy(WEIGHTS[:, :, C:2 * C], hats.unsqueeze(2).broadcast_to([N, ORDERS, C])))

        def stage_quantiles(tier, first, width, slots, chunk, pairs, piece_pairs):
            tag = f"q{tier}_"
            used_orders = -(-3 * (slots - 1) // 4) + 1
            layers = live_halves(layered(SELECTION[slots]), range(used_orders))
            CHUNKS, BLOCKS = slots // chunk, pairs // piece_pairs
            TURNS, GRAPHS, COLS = B // (2 * pairs), 2 * pairs, pairs * width
            assert CHUNKS * chunk == slots and BLOCKS % PIECES == 0 and piece_pairs * chunk * width <= 512
            USES = CHUNKS * BLOCKS // PIECES
            hot_ready = [sem(f"{tag}hot_ready{h}") for h in range(CHUNKS)]
            gathered = [sem(f"{tag}gathered{k}") for k in range(PIECES)]
            copied = [sem(f"{tag}copied{k}") for k in range(PIECES)]
            sorting, first_read, spread, kept = [sem(tag + n) for n in ("sorting", "first_read", "spread", "kept")]
            weighted, summed, agg_copied = sem(tag + "weighted"), sem(tag + "summed"), sem(tag + "agg_copied")
            raw = take([N, slots, COLS])
            wires = take([N, slots + 2, COLS])
            hot = [take([N, GRAPHS, chunk, width], BF16) for _ in range(CHUNKS)]
            parts = take([N, 3, GRAPHS, C], BF16)
            om = take([N, used_orders, COLS], BF16)
            parts_ready = sem(tag + "parts_ready")

            HOME = [None] * slots
            plan, free = [], list(range(slots + 2))
            for layer in layers:
                rows = []
                for a, b, want_min, want_max in layer:
                    src = [("raw", w) if HOME[w] is None else ("wire", HOME[w]) for w in (a, b)]
                    low = free.pop(0) if want_min else None
                    high = None
                    if want_max:
                        high = free.pop(0) if HOME[b] is None else HOME[b]
                    elif HOME[b] is not None:
                        free.append(HOME[b])
                    if HOME[a] is not None:
                        free.append(HOME[a])
                    rows.append((src[0], src[1], low, high))
                    HOME[a], HOME[b] = low, high
                plan.append(rows)
            HALVES = sum((lo is not None) + (hi is not None) for rows in plan for _, _, lo, hi in rows)
            first_last = max(n for n, rows in enumerate(plan) for r in rows if "raw" in (r[0][0], r[1][0]))
            writes = [w for rows in plan for _, _, low, high in rows for w in (low, high) if w is not None]
            sum_order = sorted(range(used_orders), key=lambda m: writes.index(HOME[m]))

            with ExitStack() as ps:
                gat = [ps.enter_context(nc.psum_tensor(f"{tag}gat{b}", [N, piece_pairs, chunk, width], F32)) for b in range(PIECES)]
                omp = [ps.enter_context(nc.psum_tensor(f"{tag}om{b}", [N, pairs, width], F32)) for b in range(2)]
                agg = ps.enter_context(nc.psum_tensor(tag + "agg", [N, COLS], F32))
                block = ps.enter_context(nc.Block())

                @block.gpsimd
                def _(pool):
                    def load_parts(s):
                        for part in range(3):
                            nc.gpsimd.tensor_copy(parts[:, part], PARTS[:, part, bass.ds(s * GRAPHS, GRAPHS), :]).then_inc(parts_ready, 1)
                    load_parts(0)
                    with pool.Fori(0, TURNS - 1) as s:
                        for k in range(PIECES):
                            pool.wait_ge(gathered[k], (s + 1) * USES)
                        load_parts(s + 1)

                @block.tensor
                def _(pe):
                    def gather_turn(s):
                        pe.wait_ge(parts_ready, s * 3 + 3)
                        for h in range(CHUNKS):
                            pe.wait_ge(hot_ready[h], (s + 1) * chunk)
                            for b in range(BLOCKS):
                                n = h * BLOCKS + b
                                k = n % PIECES
                                pe.wait_ge(copied[k], s * USES + n // PIECES + 1)
                                nc.tensor.matmul(gat[k][:].rearrange("n p k w -> n (p k w)"), onesb[:],
                                                 big_share.broadcast_to([N, piece_pairs * chunk * width]),
                                                 start=True, stop=True)
                                for p in range(piece_pairs):
                                    for odd in range(2):
                                        g = (b * piece_pairs + p) * 2 + odd
                                        marks = hot[h][:, g, :, :].rearrange("n k w -> n (k w)")
                                        to = gat[k][odd * C:odd * C + C, p, :, :].rearrange("n k w -> n (k w)")
                                        nc.tensor.matmul(to, minus_big, marks, start=False, stop=True, skip_group_check=True)
                                        for part in range(3):
                                            mm = nc.tensor.matmul(
                                                to, parts[:, part, g, :], marks, start=False, stop=True, skip_group_check=True)
                                mm.then_inc(gathered[k], 1)

                    def spread_weights(s):
                        nodes = COUNT1[:, bass.ds(s * pairs, pairs), first:first + width, :]
                        for m in range(used_orders):
                            pe.wait_ge(kept, s * used_orders + max(m - 1, 0) + 1)
                            for odd in range(2):
                                mm = nc.tensor.matmul(omp[m % 2][:], WEIGHTS[:, m, (1 - odd) * C:(3 - odd) * C],
                                                      nodes[:, :, :, odd], start=(odd == 0), stop=(odd == 1))
                            mm.then_inc(spread, 1)

                    def sum_turn(s):
                        pe.wait_ge(agg_copied, s + 1)
                        for n, m in enumerate(sum_order):
                            pe.wait_ge(weighted, s * used_orders + n + 2)
                            nc.tensor.matmul(agg[:], identf[:], wires[:, HOME[m], :], start=(n == 0),
                                             stop=(n == used_orders - 1)).then_inc(summed, 1)

                    pe.sem_inc(summed, used_orders)
                    spread_weights(0)
                    gather_turn(0)
                    with pe.Fori(0, TURNS - 1) as s:
                        gather_turn(s + 1)
                        sum_turn(s)
                        spread_weights(s + 1)
                    sum_turn(TURNS - 1)

                @block.scalar
                def _(act):
                    def copy_turn(s):
                        act.wait_ge(first_read, s + 1)
                        for h in range(CHUNKS):
                            for b in range(BLOCKS):
                                n = h * BLOCKS + b
                                k = n % PIECES
                                act.wait_ge(gathered[k], s * USES + n // PIECES + 1)
                                nc.scalar.copy(raw[:, h * chunk:(h + 1) * chunk,
                                                   b * piece_pairs * width:(b + 1) * piece_pairs * width]
                                               .rearrange("n k (p w) -> n p k w", w=width), gat[k][:]).then_inc(copied[k], 1)

                    def keep_weights(s):
                        act.wait_ge(weighted, s * used_orders + 1)
                        for m in range(used_orders):
                            act.wait_ge(spread, s * used_orders + m + 1)
                            nc.scalar.copy(om[:, m, :], omp[m % 2][:].rearrange("n p w -> n (p w)")).then_inc(kept, 1)

                    def store_turn(s):
                        act.wait_ge(summed, (s + 2) * used_orders)
                        nc.scalar.copy(AGG[:, bass.ds(s * pairs, pairs), first:first + width],
                                       agg[:].rearrange("n (p w) -> n p w", w=width)).then_inc(agg_copied, 1)

                    starts_free(act, agg_copied, kept, *copied)
                    keep_weights(0)
                    copy_turn(0)
                    with act.Fori(0, TURNS - 1) as s:
                        copy_turn(s + 1)
                        store_turn(s)
                        keep_weights(s + 1)
                    store_turn(TURNS - 1)

                @block.vector
                def _(dve):
                    def mark(s, r):
                        h = r // chunk
                        nc.vector.tensor_scalar(hot[h][:, :, r % chunk, :],
                                                POS[:, bass.ds(s * GRAPHS, GRAPHS), first:first + width],
                                                float(r + 1), None, ALU.is_equal).then_inc(hot_ready[h], 1)

                    def sort_turn(s, ahead):
                        step = Steps(dve, sorting, HALVES, s)
                        for k in range(PIECES):
                            dve.wait_ge(copied[k], (s + 1) * USES + 1)
                        unwritten = [HOME[m] for m in sum_order]
                        marks = list(range(slots)) if ahead else []
                        for n, rows in enumerate(plan):
                            before = 0
                            for (ka, a), (kb, b), low, high in rows:
                                step.wait(before)
                                before = (low is not None) + (high is not None)
                                va = raw[:, a, :] if ka == "raw" else wires[:, a, :]
                                vb = raw[:, b, :] if kb == "raw" else wires[:, b, :]
                                for w in (low, high):
                                    if w in unwritten:
                                        dve.wait_ge(summed, s * used_orders + used_orders - len(unwritten) + 1)
                                        unwritten.remove(w)
                                if low is not None:
                                    step(nc.vector.tensor_tensor(wires[:, low, :], va, vb, ALU.min))
                                if high is not None:
                                    step(nc.vector.tensor_tensor(wires[:, high, :], va, vb, ALU.max))
                                if n > 0 and marks:
                                    mark(s + 1, marks.pop(0))
                            step.wait()
                            if n == first_last:
                                dve.sem_inc(first_read, 1)
                        for r in marks:
                            mark(s + 1, r)
                        step.end()
                        dve.wait_ge(kept, (s + 1) * used_orders + 1)
                        for m in sum_order:
                            w = wires[:, HOME[m], :]
                            nc.vector.tensor_tensor(w, w, om[:, m, :], ALU.mult).then_inc(weighted, 1)

                    starts_free(dve, first_read, weighted)
                    for r in range(slots):
                        mark(0, r)
                    with dve.Fori(0, TURNS - 1) as s:
                        sort_turn(s, True)
                    sort_turn(TURNS - 1, False)

        def stage_return():
            def turns(name, per=1):
                return Turns(sem("ret_" + name), per)
            staged, turned, copied, returned, added = turns("staged", 2), turns("turned"), turns("copied"), turns("returned"), turns("added")
            a4 = [take([N, 2, N]) for _ in range(2)]
            p4 = [take([N, QG, N]) for _ in range(2)]
            t4 = [take([N, QG, C]) for _ in range(2)]
            with ExitStack() as ps:
                tp = [ps.enter_context(nc.psum_tensor(f"ret_tp{u}", [N, 2, N], F32)) for u in range(2)]
                rp = [ps.enter_context(nc.psum_tensor(f"ret_rp{u}", [N, QG, C], F32)) for u in range(2)]
                block = ps.enter_context(nc.Block())

                @block.gpsimd
                def _(pool):
                    staged.begin(pool)
                    with pool.Fori(0, QUADS // 2) as i:
                        for u in range(2):
                            q = i * 2 + u
                            turned.wait(pool, q, behind=2)
                            nc.gpsimd.tensor_copy(a4[u], AGG[:, bass.ds(q * 2, 2), :]).then_inc(staged.sem, 1)
                            returned.wait(pool, q, behind=2)
                            nc.gpsimd.tensor_copy(p4[u], PT[:, bass.ds(q * QG, QG), :]).then_inc(staged.sem, 1)

                @block.tensor
                def _(pe):
                    def turn(i, u):
                        q = i * 2 + u
                        staged.wait(pe, q, 1)
                        copied.wait(pe, q, behind=2)
                        for pair in range(2):
                            mm = nc.tensor.transpose(tp[u][:, pair, :], a4[u][:, pair, :], identf[:])
                        mm.then_inc(turned.sem, 1)

                    def put_back(i, u):
                        q = i * 2 + u
                        staged.wait(pe, q)
                        copied.wait(pe, q)
                        added.wait(pe, q, behind=2)
                        for g in range(QG):
                            mm = nc.tensor.matmul(rp[u][:, g, :], p4[u][:, g, :], t4[u][:, g, :], start=True, stop=True)
                        mm.then_inc(returned.sem, 1)

                    turned.begin(pe)
                    returned.begin(pe)
                    with pe.Fori(0, QUADS // 2) as i:
                        turn(i, 0)
                        turn(i, 1)
                        put_back(i, 0)
                        put_back(i, 1)

                @block.scalar
                def _(act):
                    copied.begin(act)
                    with act.Fori(0, QUADS // 2) as i:
                        for u in range(2):
                            q = i * 2 + u
                            turned.wait(act, q)
                            returned.wait(act, q, behind=2)
                            nc.scalar.copy(t4[u].rearrange("n g c -> n (g c)"),
                                           tp[u][:].rearrange("n p c -> n (p c)")).then_inc(copied.sem, 1)

                @block.vector
                def _(dve):
                    added.begin(dve)
                    with dve.Fori(0, QUADS // 2) as i:
                        for u in range(2):
                            q = i * 2 + u
                            hs = H[:, bass.ds(q * QG, QG), :]
                            returned.wait(dve, q)
                            nc.vector.tensor_tensor(hs, hs, rp[u][:], ALU.add).then_inc(added.sem, 1)

        def stage_first():
            nonlocal PT, COUNT1, AGG, RANK, WEIGHTS, minus_big, big_share
            used[0] = 0
            PT, AGG = take([N, B, N], BF16), take([N, B // 2, N])
            COUNT1 = AGG.rearrange("n p i -> n (p i)").bitcast(BF16).rearrange("n (p i e) -> n p i e", i=N, e=2)
            RANK, WEIGHTS = take([N, B]), take([N, ORDERS, 3 * C], BF16)
            minus_big, big_share = take([N, C], BF16), take([N, 2], BF16)[:, 0:1]
            base = used[0]
            stages = [stage_order] + [lambda t=t, tier=tier: stage_quantiles(t, *tier) for t, tier in enumerate(TIERS)]
            for stage in stages + [stage_return, lambda: stage_general("qg_", True)]:
                used[0] = base
                stage()

        PT = COUNT1 = AGG = RANK = WEIGHTS = minus_big = big_share = None

        def stage_general(tag, quantiles):
            flag_step, flagged = sem(tag + "flag_step"), sem(tag + "flagged")
            value_ready, spread, pos_turned = sem(tag + "value_ready"), sem(tag + "spread"), sem(tag + "pos_turned")
            chain, rounds = sem(tag + "chain"), sem(tag + "rounds")
            room_a, room_b = take([N, N, C]), take([N, N, C])
            value, part = take([N, C]), take([N, C])
            absent, order = take([N, N]), take([N, N])
            cnt, top = take([N, 1]), take([N, 1])
            excess, late, turn_back = take([N, B]), take([N, B]), take([N, N])
            part_ready, returned = sem(tag + "part_ready"), sem(tag + "returned")
            FLAG = 8 if quantiles else 3
            over, flag = take([N, 2], BF16), take([N, 1], I32)
            at, dist, hats = take([N, 1]), take([N, N]), take([N, N])
            scratch = nc.dram_tensor(tag + "scratch", [N, C], F32, kind="Internal").ap()
            PAIRS = N // 2
            with ExitStack() as ps:
                fp = ps.enter_context(nc.psum_tensor(tag + "fp", [N, 2], F32))
                pt = ps.enter_context(nc.psum_tensor(tag + "pt", [N, N], F32))
                back = ps.enter_context(nc.psum_tensor(tag + "back", [N, C], F32))
                block = ps.enter_context(nc.Block())

                @block.gpsimd
                def _(pool):
                    nc.gpsimd.iota(order, pattern=[[1, N]], base=0, channel_multiplier=0,
                                   allow_small_or_imprecise_dtypes=True).then_inc(value_ready, 1)

                @block.sync
                def _(sp):
                    sp.wait_ge(flag_step, FLAG + 1)
                    crowded = sp.value_load(flag[0:1, 0:1])
                    with sp.If(crowded > 0):
                        with sp.Fori(0, B) as g:
                            sp.wait_ge(value_ready, g + 2)
                            sp.dma_start(scratch, value).then_inc(spread, 16)
                            sp.wait_ge(spread, g * 32 + 16)
                            sp.dma_start(room_a.rearrange("p j c -> p (j c)"),
                                         scratch.rearrange("j c -> (j c)").partition_broadcast(N)).then_inc(spread, 16)

                @block.tensor
                def _(pe):
                    pe.wait_ge(flag_step, FLAG)
                    nc.tensor.matmul(fp[0:1, 0:1], over[:, 0:1], onesb[:, 0:1], start=True, stop=True).then_inc(flagged, 1)
                    pe.wait_ge(flag_step, FLAG + 1)
                    crowded = pe.value_load(flag[0:1, 0:1])
                    with pe.If(crowded > 0):
                        with pe.Fori(0, B) as g:
                            pe.wait_ge(value_ready, g + 2)
                            nc.tensor.matmul(pt[:], POS[:, bass.ds(g, 1), :].rearrange("p a i -> p (a i)"), identb[:],
                                             start=True, stop=True).then_inc(pos_turned, 1)
                            if quantiles:
                                pe.wait_ge(part_ready, g + 1)
                                nc.tensor.matmul(back[:], turn_back, part, start=True, stop=True).then_inc(returned, 1)

                @block.vector
                def _(dve):
                    V = nc.vector
                    fs = Steps(dve, flag_step)
                    fs(V.memset(over, 0.0))
                    if quantiles:
                        (start2, _, slots2, *_), (start1, _, slots1, *_), (_, _, slots0, *_) = TIERS
                        fs(V.tensor_scalar(excess, count[:], float(slots0), None, ALU.subtract))
                        for start, fewer in ((start1, slots0 - slots1), (start2, slots1 - slots2)):
                            fs(V.tensor_scalar(late, RANK, start - 0.5, float(fewer), ALU.is_gt, ALU.mult))
                            fs.wait()
                            fs(V.tensor_tensor(excess, excess, late, ALU.add))
                            fs.wait()
                        fs(V.tensor_reduce(top, excess, AX, ALU.max))
                    else:
                        fs(V.tensor_reduce(top, count[:], AX, ALU.max))
                    fs.wait()
                    fs(V.tensor_scalar(over[:, 0:1], top, 0.0 if quantiles else float(SLOTS), None, ALU.is_gt))
                    dve.wait_ge(flagged, 1)
                    fs(V.tensor_copy(flag[0:1, :], fp[0:1, 0:1]))
                    fs.wait()
                    crowded = dve.value_load(flag[0:1, 0:1])
                    with dve.If(crowded > 0):
                        dve.wait_ge(value_ready, 1)
                        with dve.Fori(0, B) as g:
                            step = Steps(dve, chain, 27 if quantiles else 8, g)

                            def do(ins):
                                step(ins)
                                step.wait()

                            def graph(t):
                                return t[:, bass.ds(g, 1), :].rearrange("p a c -> p (a c)")
                            do(V.tensor_tensor(part, PARTS[:, 0, bass.ds(g, 1), :].rearrange("p a c -> p (a c)"),
                                               PARTS[:, 1, bass.ds(g, 1), :].rearrange("p a c -> p (a c)"), ALU.add))
                            V.tensor_tensor(value, part, PARTS[:, 2, bass.ds(g, 1), :].rearrange("p a c -> p (a c)"),
                                            ALU.add).then_inc(value_ready, 1)
                            dve.wait_ge(value_ready, g + 2)
                            dve.wait_ge(pos_turned, g + 1)
                            do(V.tensor_scalar(absent, pt[:], 0.0, BIG, ALU.is_equal, ALU.mult))
                            dve.wait_ge(spread, g * 32 + 32)
                            padding = absent.unsqueeze(2).broadcast_to([N, N, C])
                            if not quantiles:
                                do(V.tensor_tensor(room_b, room_a, padding, ALU.subtract))
                                do(V.tensor_reduce(value, room_b.rearrange("p j c -> p c j"), AX, ALU.max))
                                do(V.tensor_copy(graph(MAXQ), value))
                                do(V.tensor_tensor(room_b, room_a, padding, ALU.add))
                                do(V.tensor_reduce(value, room_b.rearrange("p j c -> p c j"), AX, ALU.min))
                                do(V.tensor_copy(graph(MINQ), value))
                                step.end()
                            else:
                                step(V.tensor_scalar(dist, pt[:], 0.0, None, ALU.is_gt))
                                step(V.tensor_copy(turn_back, graph(PT)))
                                do(V.tensor_tensor(room_a, room_a, padding, ALU.max))
                                step(V.tensor_reduce(cnt, dist, AX, ALU.add))
                                with dve.Fori(0, PAIRS) as r:
                                    ev, od = [t.rearrange("p (k e) c -> p k e c", e=2) for t in (room_a, room_b)]
                                    V.tensor_tensor(od[:, :, 0, :], ev[:, :, 0, :], ev[:, :, 1, :], ALU.min).then_inc(rounds, 1)
                                    V.tensor_tensor(od[:, :, 1, :], ev[:, :, 0, :], ev[:, :, 1, :], ALU.max).then_inc(rounds, 1)
                                    dve.wait_ge(rounds, g * (PAIRS * 6) + r * 6 + 2)
                                    up, down = room_b[:, 1:N - 1].rearrange("p (k e) c -> p k e c", e=2), room_a[:, 1:N - 1].rearrange("p (k e) c -> p k e c", e=2)
                                    V.tensor_tensor(down[:, :, 0, :], up[:, :, 0, :], up[:, :, 1, :], ALU.min).then_inc(rounds, 1)
                                    V.tensor_tensor(down[:, :, 1, :], up[:, :, 0, :], up[:, :, 1, :], ALU.max).then_inc(rounds, 1)
                                    V.tensor_copy(room_a[:, 0, :], room_b[:, 0, :]).then_inc(rounds, 1)
                                    V.tensor_copy(room_a[:, N - 1, :], room_b[:, N - 1, :]).then_inc(rounds, 1)
                                    dve.wait_ge(rounds, g * (PAIRS * 6) + r * 6 + 6)
                                step.wait()
                                for n, (tau, w) in enumerate(TAUS):
                                    do(V.tensor_scalar(at, cnt, -tau, tau, ALU.mult, ALU.add))
                                    do(V.tensor_scalar(dist, order, at, None, ALU.add))
                                    do(V.scalar_tensor_tensor(out=absent, in0=dist, scalar=-1.0, in1=dist, op0=ALU.mult, op1=ALU.max))
                                    do(V.tensor_scalar(dist, absent, -w, w, ALU.mult, ALU.add))
                                    do(V.tensor_scalar(dist, dist, 0.0, None, ALU.max))
                                    if n == 0:
                                        do(V.tensor_copy(hats, dist))
                                    else:
                                        do(V.tensor_tensor(hats, hats, dist, ALU.add))
                                do(V.tensor_tensor(room_a, room_a, hats.unsqueeze(2).broadcast_to([N, N, C]), ALU.mult))
                                V.tensor_reduce(part, room_a.rearrange("p j c -> p c j"), AX, ALU.add).then_inc(part_ready, 1)
                                dve.wait_ge(returned, g + 1)
                                do(V.tensor_tensor(value, value, back[:], ALU.add))
                                do(V.tensor_copy(graph(H), value))
                                step.end()

        def stage_mlp():
            used[0] = 0
            staged, turned, out_ready, hid_done, hid_ready, y_done, stepped, masked = [sem("mlp_" + n) for n in (
                "staged", "turned", "out_ready", "hid_done", "hid_ready", "y_done", "stepped", "masked")]
            h4, oT, hid, ym = take([N, QG, C]), take([N, QG // 2, N]), take([N, QG // 2, 2, N]), take([N, QG, C])
            with ExitStack() as ps:
                tp = ps.enter_context(nc.psum_tensor("mlp_tp", [N, QG // 2, N], F32))
                hp = ps.enter_context(nc.psum_tensor("mlp_hp", [N, 2, QG, N], F32))
                yp = ps.enter_context(nc.psum_tensor("mlp_yp", [N, QG, C], F32))
                block = ps.enter_context(nc.Block())

                @block.gpsimd
                def _(pool):
                    with pool.Fori(0, QUADS) as q:
                        pool.wait_ge(turned, q + 1)
                        nc.gpsimd.tensor_copy(h4, H[:, bass.ds(q * QG, QG), :]).then_inc(staged, 1)

                @block.tensor
                def _(pe):
                    starts_free(pe, turned, y_done)
                    with pe.Fori(0, QUADS) as q:
                        pe.wait_ge(staged, q + 1)
                        pe.wait_ge(out_ready, q + 1)
                        for pair in range(QG // 2):
                            mm = nc.tensor.transpose(tp[:, pair, :], h4[:, 2 * pair:2 * pair + 2, :].rearrange("p g c -> p (g c)"),
                                                     identf[:])
                        mm.then_inc(turned, 1)
                        pe.wait_ge(out_ready, q + 2)
                        pe.wait_ge(hid_ready, q * 2 + 1)
                        for odd in range(2):
                            side = slice(odd * C, odd * C + C)
                            mm = nc.tensor.matmul(hp[:, odd, 0:QG // 2, :], w1[side, :], oT[side], start=True, stop=True)
                        mm.then_inc(hid_done, 1)
                        pe.wait_ge(hid_ready, q * 2 + 3)
                        pe.wait_ge(masked, q + 1)
                        for g in range(QG):
                            nc.tensor.matmul(yp[:, g, :], hid[:, g // 2, g % 2, :], w2[:], start=True, stop=False)
                            mm = nc.tensor.matmul(yp[:, g, :], onesf[:], b2[:], start=False, stop=True)
                        mm.then_inc(y_done, 1)

                @block.scalar
                def _(act):
                    starts_free(act, out_ready, hid_ready)
                    with act.Fori(0, QUADS) as q:
                        act.wait_ge(turned, q + 2)
                        nc.scalar.copy(oT, tp[:]).then_inc(out_ready, 1)
                        act.wait_ge(hid_done, q + 1)
                        act.wait_ge(y_done, q + 1)
                        for odd in range(2):
                            nc.scalar.activation(hid[:, :, odd, :], hp[:, odd, 0:QG // 2, :], ACT.Relu,
                                                 bias=b1[:]).then_inc(hid_ready, 1)

                @block.vector
                def _(dve):
                    starts_free(dve, masked, stepped)
                    with dve.Fori(0, QUADS) as q:
                        quad = bass.ds(q * QG, QG)
                        dve.wait_ge(y_done, q + 2)
                        dve.wait_ge(stepped, q + 1)
                        nc.vector.tensor_tensor(ym, yp[:], mask[:, quad].unsqueeze(2).broadcast_to([N, QG, C]),
                                                ALU.mult).then_inc(masked, 1)
                        dve.wait_ge(masked, q + 2)
                        nc.vector.tensor_tensor(X[:, quad, :], X[:, quad, :], ym, ALU.add).then_inc(stepped, 1)

        def stage_columns():
            loaded, squared, multiplied = sem("att_loaded"), sem("att_squared"), sem("att_multiplied")
            col, act_done = sem("att_col"), sem("att_act")
            sq, hw = take([N, B, C]), take([N, B, C])
            wrow, bcol = take([N, 2 * C]), take([N, 1])
            sd, t1, am, dn, rd, sa, na, rt, zc, zm, lp, lm, at, rz, one = [take([N, B]) for _ in range(15)]
            with nc.Block() as block:
                @block.sync
                def _(sp):
                    sp.dma_start(wrow, W["L1_gnn_att_W"].rearrange("k o -> o k").partition_broadcast(N)
                                 .rearrange("p o k -> p (o k)")).then_inc(loaded, 16)
                    sp.dma_start(bcol, W["L1_gnn_att_b"].partition_broadcast(N)).then_inc(loaded, 16)

                @block.gpsimd
                def _(pool):
                    pool.wait_ge(loaded, 32)
                    nc.gpsimd.tensor_tensor(hw, H[:], wrow[:, 0:C].unsqueeze(1).broadcast_to([N, B, C]),
                                            ALU.mult).then_inc(multiplied, 1)

                @block.scalar
                def _(act):
                    nc.scalar.activation(sq, H[:], ACT.Square).then_inc(squared, 1)
                    act.wait_ge(col, 7)
                    nc.scalar.activation(rt, x2, ACT.Sqrt).then_inc(act_done, 1)
                    act.wait_ge(col, 18)
                    nc.scalar.activation(lp, zm, ACT.Ln, bias=one[:, 0:1]).then_inc(act_done, 1)
                    nc.scalar.activation(lm, zm, ACT.Ln, bias=one[:, 0:1], scale=-1.0).then_inc(act_done, 1)

                @block.vector
                def _(dve):
                    V = nc.vector
                    step = Steps(dve, col)
                    step(V.memset(one, 1.0))
                    dve.wait_ge(squared, 1)
                    step(V.tensor_reduce(x2, sq, AX, ALU.add))
                    dve.wait_ge(multiplied, 1)
                    step(V.tensor_reduce(sd, hw, AX, ALU.add))
                    step.wait()
                    step(V.tensor_tensor(sq, H[:], wrow[:, C:2 * C].unsqueeze(1).broadcast_to([N, B, C]), ALU.mult))
                    step.wait()
                    step(V.tensor_reduce(uw, sq, AX, ALU.add))
                    step(V.tensor_scalar(ox, x2, -1.0, 1.0, ALU.mult, ALU.add))
                    step(V.tensor_scalar(t1, x2, -2.0, 1.0, ALU.mult, ALU.add))
                    step.wait()
                    step(V.tensor_tensor(am, t1, x2, ALU.add))
                    step(V.tensor_tensor(dn, x2, x2, ALU.mult))
                    step(V.tensor_scalar(coef, ox, MIN_NORM, None, ALU.max))
                    step.wait()
                    step(V.tensor_tensor(sa, ox, am, ALU.subtract))
                    step(V.tensor_tensor(dn, dn, t1, ALU.add))
                    step.wait()
                    step(V.tensor_scalar(dn, dn, MIN_NORM, None, ALU.max))
                    step.wait()
                    step(V.reciprocal(rd, dn))
                    step.wait()
                    step(V.tensor_tensor(sa, sa, rd, ALU.mult))
                    step.wait()
                    step(V.scalar_tensor_tensor(out=na, in0=sa, scalar=-1.0, in1=sa, op0=ALU.mult, op1=ALU.max))
                    step.wait()
                    dve.wait_ge(act_done, 1)
                    step(V.tensor_tensor(zc, na, rt, ALU.mult))
                    step.wait()
                    step(V.tensor_scalar(zm, zc, MIN_NORM, ATANH_MAX, ALU.max, ALU.min))
                    step(V.tensor_scalar(na, zc, MIN_NORM, None, ALU.max))
                    step.wait()
                    step(V.reciprocal(rz, na))
                    dve.wait_ge(act_done, 3)
                    step(V.tensor_tensor(at, lp, lm, ALU.subtract))
                    step.wait()
                    step(V.tensor_tensor(at, at, rz, ALU.mult))
                    step(V.tensor_tensor(sa, sa, sd, ALU.mult))
                    step(V.tensor_tensor(cu, coef, uw, ALU.mult))
                    step(V.tensor_tensor(cox, coef, ox, ALU.mult))
                    step.wait()
                    step(V.tensor_tensor(at, at, sa, ALU.mult))
                    step(V.tensor_scalar(ncu, cu, -0.5, None, ALU.mult))
                    step(V.tensor_scalar(hcox, cox, 0.5, None, ALU.mult))
                    step.wait()
                    step(V.tensor_tensor(at, at, coef, ALU.mult))
                    step.wait()
                    step(V.tensor_scalar(selfl, at, 0.5, bcol, ALU.mult, ALU.add))
                    step.wait()

        def stage_pairs():
            def turns(name, per=1):
                return Turns(sem("pr_" + name), per)
            built, turned, copied, formed = turns("built", 10), turns("turned", 4), turns("copied", 4), turns("formed", 3)
            clamped, lns, sums, exps = turns("clamped", 2), turns("lns", 2), turns("sums", 2), turns("exps", 2)
            zmin, lnz, ks, lg, sig = turns("zmin"), turns("lnz", 2), turns("ks", 2), turns("lg", 2), turns("sig", 3)
            weighed, w_turned, w_masked, summed, stored = (turns("weighed"), turns("w_turned"), turns("w_masked"),
                                                           turns("summed"), turns("stored"))
            ready = sem("pr_ready")
            R = C + 3
            left = [[take([N, QG, R + 1]) for _ in range(4)] for _ in range(2)]
            turnT = [[take([N, QG, N]) for _ in range(4)] for _ in range(2)]
            a_, b_, s_, t_ = [[take([N, QG, N]) for _ in range(2)] for _ in range(4)]
            wT = [take([N, QG, N]) for _ in range(2)]
            one = take([N, 1])
            ends = take([N, B, 2])
            HALF = QUADS // 2
            with ExitStack() as ps:
                tp = [ps.enter_context(nc.psum_tensor(f"pr_tp{k}", [N, QG, N], F32)) for k in range(2)]
                gg = [ps.enter_context(nc.psum_tensor(f"pr_gg{k}", [N, QG, N], F32)) for k in range(2)]
                den, d2, wt, so = [ps.enter_context(nc.psum_tensor("pr_" + n, [N, QG, N], F32)) for n in ("den", "d2", "wt", "so")]
                block = ps.enter_context(nc.Block())

                @block.gpsimd
                def _(pool):
                    P = nc.gpsimd

                    def build(q, u):
                        J, D, E, G = left[u]
                        quad = bass.ds(q * QG, QG)

                        def c(t):
                            return t[:, quad].unsqueeze(2)
                        turned.wait(pool, q, behind=2)

                        def put(ins):
                            ins.then_inc(built.sem, 1)
                        put(P.tensor_copy(J[:, :, 0:C], H[:, quad, :]))
                        put(P.tensor_copy(J[:, :, C + 1:C + 2], c(x2)))
                        put(P.tensor_copy(J[:, :, C + 2:C + 3], c(uw)))
                        built.wait(pool, q, 1)
                        put(P.tensor_tensor(G[:, :, 0:C], J[:, :, 0:C], c(cu).broadcast_to([N, QG, C]), ALU.mult))
                        put(P.tensor_scalar(D[:, :, 0:C], J[:, :, 0:C], -2.0, None, ALU.mult))
                        put(P.tensor_copy(D[:, :, C + 1:C + 2], c(x2)))
                        put(P.tensor_scalar(E[:, :, 0:C], J[:, :, 0:C], -2.0, None, ALU.mult))
                        put(P.tensor_copy(E[:, :, C:C + 1], c(x2)))
                        put(P.tensor_copy(G[:, :, C:C + 2], c(ncu).broadcast_to([N, QG, 2])))
                        put(P.tensor_copy(G[:, :, C + 2:C + 3], c(hcox)))

                    def add_logs(q, u):
                        lns.wait(pool, q)
                        P.tensor_tensor(s_[u], b_[u], a_[u], ALU.subtract).then_inc(sums.sem, 1)
                        P.tensor_tensor(t_[u], a_[u], b_[u], ALU.add).then_inc(sums.sem, 1)

                    def artanh_over_z(q, u):
                        lnz.wait(pool, q)
                        P.tensor_tensor(a_[u], a_[u], b_[u], ALU.subtract).then_inc(ks.sem, 1)
                        ks.wait(pool, q, 1)
                        P.tensor_tensor(t_[u], a_[u], t_[u], ALU.mult).then_inc(ks.sem, 1)

                    def weigh(q, u):
                        sig.wait(pool, q)
                        P.tensor_tensor(a_[u], s_[u], t_[u], ALU.mult).then_inc(weighed.sem, 1)

                    for t in (built, sums, ks, weighed):
                        t.begin(pool)
                    for t in left[0] + left[1] + [ends]:
                        P.memset(t, 1.0).then_inc(ready, 1)
                    pool.wait_ge(ready, 9)
                    P.tensor_copy(ends[:, :, 1], x2).then_inc(ready, 1)
                    build(0, 0)
                    build(1, 1)

                    def two_quads(q, ahead):
                        add_logs(q, 0)
                        add_logs(q + 1, 1)
                        if ahead:
                            build(q + 2, 0)
                        artanh_over_z(q, 0)
                        artanh_over_z(q + 1, 1)
                        if ahead:
                            build(q + 3, 1)
                        weigh(q, 0)
                        weigh(q + 1, 1)
                    with pool.Fori(0, HALF - 1) as i:
                        two_quads(i * 2, True)
                    two_quads(QUADS - 2, False)

                @block.tensor
                def _(pe):
                    def form(q, u):
                        built.wait(pe, q)
                        for k, t in enumerate(left[u]):
                            if k < 2:
                                copied.wait(pe, q, 4, behind=1)
                            else:
                                copied.wait(pe, q, k - 1)
                            for g in range(QG):
                                mm = nc.tensor.transpose(tp[k % 2][0:R, g, :], t[:, g, 0:R], identf[:])
                            mm.then_inc(turned.sem, 1)
                        copied.wait(pe, q)
                        clamped.wait(pe, q, behind=1)
                        lg.wait(pe, q, 1, behind=2)
                        for k, (o, K) in enumerate(((den, C + 2), (d2, C + 2), (gg[u], C + 3))):
                            for g in range(QG):
                                mm = nc.tensor.matmul(o[:, g, :], turnT[u][k + 1][0:K, g, :], turnT[u][0][0:K, g, :],
                                                      start=True, stop=True)
                            mm.then_inc(formed.sem, 1)

                    def turn_weights(q, u):
                        weighed.wait(pe, q)
                        w_masked.wait(pe, q, behind=1)
                        for g in range(QG):
                            mm = nc.tensor.transpose(wt[:, g, :], a_[u][:, g, :], identf[:])
                        mm.then_inc(w_turned.sem, 1)

                    def sum_neighbours(q, u):
                        w_masked.wait(pe, q)
                        stored.wait(pe, q, behind=1)
                        for g in range(QG):
                            graph = bass.ds(q * QG + g, 1)
                            nc.tensor.matmul(so[:, g, 0:C], wT[u][:, g, :], H[:, graph, :].rearrange("p a c -> p (a c)"),
                                             start=True, stop=True)
                            mm = nc.tensor.matmul(so[:, g, C:C + 2], wT[u][:, g, :], ends[:, graph, :].rearrange("p a c -> p (a c)"),
                                                  start=True, stop=True)
                        mm.then_inc(summed.sem, 1)

                    for t in (turned, formed, w_turned, summed):
                        t.begin(pe)
                    pe.wait_ge(ready, 10)
                    form(0, 0)
                    form(1, 1)

                    def two_quads(q, ahead):
                        for u in range(2):
                            if ahead:
                                form(q + 2 + u, u)
                            turn_weights(q + u, u)
                            sum_neighbours(q + u, u)
                    with pe.Fori(0, HALF - 1) as i:
                        two_quads(i * 2, True)
                    two_quads(QUADS - 2, False)

                @block.scalar
                def _(act):
                    A = nc.scalar.activation

                    def copy_columns(q, u):
                        for k in range(4):
                            turned.wait(act, q, k + 1)
                            if k == 0:
                                formed.wait(act, q, behind=2)
                            nc.scalar.copy(turnT[u][k][0:R], tp[k % 2][0:R]).then_inc(copied.sem, 1)

                    def logs(q, u):
                        clamped.wait(act, q)
                        A(a_[u], a_[u], ACT.Ln).then_inc(lns.sem, 1)
                        A(b_[u], b_[u], ACT.Ln).then_inc(lns.sem, 1)

                    def roots(q, u):
                        sums.wait(act, q)
                        A(s_[u], s_[u], ACT.Exp, scale=0.5).then_inc(exps.sem, 1)
                        A(t_[u], t_[u], ACT.Exp, scale=-0.5).then_inc(exps.sem, 1)

                    def artanh_logs(q, u):
                        zmin.wait(act, q)
                        A(a_[u], s_[u], ACT.Ln, bias=one).then_inc(lnz.sem, 1)
                        A(b_[u], s_[u], ACT.Ln, bias=one, scale=-1.0).then_inc(lnz.sem, 1)

                    def sigmoid(q, u):
                        lg.wait(act, q)
                        lnz.wait(act, q)
                        A(s_[u], b_[u], ACT.Exp, scale=-1.0).then_inc(sig.sem, 1)
                        sig.wait(act, q, 1)
                        A(b_[u], s_[u], ACT.Ln, bias=one).then_inc(sig.sem, 1)
                        sig.wait(act, q, 2)
                        A(s_[u], b_[u], ACT.Exp, scale=-1.0).then_inc(sig.sem, 1)

                    def store(q, u):
                        summed.wait(act, q)
                        nc.scalar.mul(SUMS[:, bass.ds(q * QG, QG), :], so[:, :, 0:C + 2], 0.5).then_inc(stored.sem, 1)

                    for t in (copied, lns, exps, lnz, sig, stored):
                        t.begin(act)
                    act.wait_ge(ready, 10)
                    nc.scalar.activation(one, left[0][0][:, 0, C:C + 1], ACT.Copy)
                    nc.scalar.preload_act_table_set("natural_log_exp_and_others")
                    copy_columns(0, 0)
                    copy_columns(1, 1)

                    def two_quads(q, ahead):
                        for part in (logs, roots, artanh_logs):
                            part(q, 0)
                            part(q + 1, 1)
                        for u in range(2):
                            sigmoid(q + u, u)
                            if ahead:
                                copy_columns(q + 2 + u, u)
                            store(q + u, u)
                    with act.Fori(0, HALF - 1) as i:
                        two_quads(i * 2, True)
                    two_quads(QUADS - 2, False)

                @block.vector
                def _(dve):
                    V = nc.vector

                    def clamp(q, u):
                        formed.wait(dve, q)
                        w_turned.wait(dve, q, behind=2)
                        V.tensor_scalar(a_[u], den[:], MIN_NORM, None, ALU.max).then_inc(clamped.sem, 1)
                        V.tensor_scalar(b_[u], d2[:], 1e-18, None, ALU.max).then_inc(clamped.sem, 1)

                    def bound(q, u):
                        exps.wait(dve, q)
                        V.tensor_scalar(s_[u], s_[u], ATANH_MAX, None, ALU.min).then_inc(zmin.sem, 1)

                    def logits(q, u):
                        ks.wait(dve, q)
                        V.tensor_tensor(b_[u], gg[u][:], t_[u], ALU.mult).then_inc(lg.sem, 1)
                        lg.wait(dve, q, 1)
                        V.scalar_tensor_tensor(out=b_[u], in0=b_[u], scalar=-40.0,
                                               in1=selfl[:, bass.ds(q * QG, QG)].unsqueeze(2).broadcast_to([N, QG, N]),
                                               op0=ALU.max, op1=ALU.add).then_inc(lg.sem, 1)

                    def mask_weights(q, u):
                        w_turned.wait(dve, q)
                        summed.wait(dve, q, behind=2)
                        V.tensor_tensor(wT[u], wt[:], AT[:, bass.ds(q * QG, QG), :], ALU.mult).then_inc(w_masked.sem, 1)

                    for t in (clamped, zmin, lg, w_masked):
                        t.begin(dve)
                    clamp(0, 0)
                    clamp(1, 1)

                    def two_quads(q, ahead):
                        for part in (bound, logits):
                            part(q, 0)
                            part(q + 1, 1)
                        for u in range(2):
                            if ahead:
                                clamp(q + 2 + u, u)
                            mask_weights(q + u, u)
                    with dve.Fori(0, HALF - 1) as i:
                        two_quads(i * 2, True)
                    two_quads(QUADS - 2, False)

        def stage_expmap():
            step_v, pooled, acted = sem("ex_step"), sem("ex_pool"), sem("ex_act")
            cols = [take([N, B]) for _ in range(20)]
            dot, wa, c1, un2, xu, nn, la, th, kk, y2, xy, a1, dn, ca, cb, rn, nr, ff, i1, i2 = cols
            a, u, t, p = [take([N, B, C]) for _ in range(4)]
            S = SUMS[:, :, 0:C]
            bc = [N, B, C]

            def b(c):
                return c.unsqueeze(2).broadcast_to(bc)
            with nc.Block() as block:
                @block.gpsimd
                def _(pool):
                    pool.wait_ge(step_v, 5)
                    nc.gpsimd.tensor_tensor(p, H[:], b(c1), ALU.mult).then_inc(pooled, 1)
                    pool.wait_ge(step_v, 8)
                    nc.gpsimd.tensor_tensor(p, H[:], u, ALU.mult).then_inc(pooled, 1)
                    pool.wait_ge(step_v, 29)
                    nc.gpsimd.tensor_tensor(p, H[:], b(ca), ALU.mult).then_inc(pooled, 1)

                @block.scalar
                def _(act):
                    act.wait_ge(step_v, 8)
                    nc.scalar.activation(a, u, ACT.Square).then_inc(acted, 1)
                    act.wait_ge(step_v, 10)
                    nc.scalar.activation(nn, un2, ACT.Sqrt).then_inc(acted, 1)
                    act.wait_ge(step_v, 13)
                    nc.scalar.activation(th, la, ACT.Tanh).then_inc(acted, 1)
                    act.wait_ge(step_v, 30)
                    nc.scalar.activation(a, u, ACT.Square).then_inc(acted, 1)
                    act.wait_ge(step_v, 32)
                    nc.scalar.activation(nr, rn, ACT.Sqrt).then_inc(acted, 1)

                @block.vector
                def _(dve):
                    V = nc.vector
                    step = Steps(dve, step_v)

                    def do(ins):
                        step(ins)
                        step.wait()
                    do(V.tensor_tensor(a, H[:], S, ALU.mult))
                    do(V.tensor_reduce(dot, a, AX, ALU.add))
                    do(V.scalar_tensor_tensor(out=wa, in0=dot, scalar=-2.0, in1=SUMS[:, :, C], op0=ALU.mult, op1=ALU.add))
                    do(V.tensor_tensor(wa, wa, SUMS[:, :, C + 1], ALU.add))
                    do(V.scalar_tensor_tensor(out=c1, in0=wa, scalar=-1.0, in1=coef, op0=ALU.mult, op1=ALU.mult))
                    do(V.tensor_tensor(t, S, b(cox), ALU.mult))
                    dve.wait_ge(pooled, 1)
                    do(V.tensor_tensor(u, t, p, ALU.add))
                    do(V.tensor_scalar(u, u, CLAMP, -CLAMP, ALU.min, ALU.max))
                    dve.wait_ge(acted, 1)
                    do(V.tensor_reduce(un2, a, AX, ALU.add))
                    do(V.tensor_scalar(un2, un2, MIN_NORM * MIN_NORM, None, ALU.max))
                    dve.wait_ge(acted, 2)
                    do(V.reciprocal(la, coef))
                    do(V.tensor_tensor(la, la, nn, ALU.mult))
                    do(V.reciprocal(i1, nn))
                    dve.wait_ge(pooled, 2)
                    do(V.tensor_reduce(xu, p, AX, ALU.add))
                    dve.wait_ge(acted, 3)
                    do(V.tensor_tensor(kk, th, i1, ALU.mult))
                    do(V.tensor_reduce(y2, a, AX, ALU.add))
                    do(V.tensor_tensor(y2, y2, kk, ALU.mult))
                    do(V.tensor_tensor(y2, y2, kk, ALU.mult))
                    do(V.tensor_tensor(xy, xu, kk, ALU.mult))
                    do(V.tensor_scalar(xy, xy, 2.0, 1.0, ALU.mult, ALU.add))
                    do(V.tensor_tensor(a1, xy, y2, ALU.add))
                    do(V.tensor_tensor(dn, x2, y2, ALU.mult))
                    do(V.tensor_tensor(dn, dn, xy, ALU.add))
                    do(V.tensor_scalar(dn, dn, MIN_NORM, None, ALU.max))
                    do(V.reciprocal(i2, dn))
                    do(V.tensor_tensor(cb, ox, kk, ALU.mult))
                    do(V.tensor_tensor(cb, cb, i2, ALU.mult))
                    do(V.tensor_tensor(t, u, b(cb), ALU.mult))
                    do(V.tensor_tensor(ca, a1, i2, ALU.mult))
                    dve.wait_ge(pooled, 3)
                    do(V.tensor_tensor(u, t, p, ALU.add))
                    dve.wait_ge(acted, 4)
                    do(V.tensor_reduce(rn, a, AX, ALU.add))
                    do(V.tensor_scalar(rn, rn, MIN_NORM * MIN_NORM, None, ALU.max))
                    dve.wait_ge(acted, 5)
                    do(V.reciprocal(ff, nr))
                    do(V.tensor_scalar(ff, ff, BALL, 1.0, ALU.mult, ALU.min))
                    do(V.tensor_tensor(t, u, b(ff), ALU.mult))
                    do(V.tensor_tensor(X[:], X[:], t, ALU.add))

        def stage_degrees():
            summed, copied, col, logged = sem("dg_summed"), sem("dg_copied"), sem("dg_col"), sem("dg_logged")
            one, t = take([N, 1]), take([N, B])
            with nc.psum_tensor("dg", [N, B], F32) as dg, nc.Block() as block:
                @block.tensor
                def _(pe):
                    with pe.Fori(0, B) as g:
                        nc.tensor.matmul(dg[:, bass.ds(g, 1)], AT[:, bass.ds(g, 1), :].rearrange("p a i -> p (a i)"),
                                         onesb[:, 0:1], start=True, stop=True).then_inc(summed, 1)

                @block.scalar
                def _(act):
                    act.wait_ge(col, 2)
                    nc.scalar.activation(t, degree, ACT.Ln, bias=one).then_inc(logged, 1)

                @block.vector
                def _(dve):
                    V = nc.vector
                    step = Steps(dve, col)

                    def do(ins):
                        step(ins)
                        step.wait()
                    do(V.memset(one, 1.0))
                    dve.wait_ge(summed, B)
                    do(V.tensor_copy(degree, dg[:]))
                    do(V.tensor_scalar(rdeg, degree, 1.0, None, ALU.max))
                    do(V.reciprocal(rdeg, rdeg))
                    do(V.tensor_tensor(share, degree, rdeg, ALU.mult))
                    dve.wait_ge(logged, 1)
                    do(V.tensor_scalar(amp, t, 1.0 / AVG_D_LOG, None, ALU.mult))
                    do(V.tensor_scalar(t, t, LN_EPS, None, ALU.max))
                    do(V.reciprocal(t, t))
                    do(V.tensor_scalar(att, t, AVG_D_LOG, None, ALU.mult))

        def load_pna():
            loaded = sem("pna_loaded")
            with nc.Block() as block:
                @block.sync
                def _(sp):
                    for side in (0, C):
                        rows = slice(side, side + C)
                        sp.dma_start(wcat[rows, 0:C], W["L2_gnn_W_pre"][0:C, :]).then_inc(loaded, 16)
                        sp.dma_start(wcat[rows, C:2 * C], W["L2_gnn_W_pre"][C:2 * C, :]).then_inc(loaded, 16)
                        sp.dma_start(wcat[rows, 2 * C:3 * C], W["L2_gnn_W_post"][0:C, :]).then_inc(loaded, 16)
                    for k in range(2):
                        sp.dma_start(wm[:, k], W["L2_gnn_W_post"][C:, :].rearrange("(s k p) c -> k p s c", k=2, p=N)[k])\
                          .then_inc(loaded, 16)
                    sp.dma_start(bias[:, 0:C], W["L2_gnn_b_pre"].partition_broadcast(N)).then_inc(loaded, 16)
                    sp.dma_start(bias[:, 2 * C:3 * C], W["L2_gnn_b_post"].partition_broadcast(N)).then_inc(loaded, 16)
                    sp.wait_ge(loaded, 160)

                @block.gpsimd
                def _(pool):
                    nc.gpsimd.memset(bias[:, C:2 * C], 0.0)

        def stage_neighbour_terms():
            staged, turned, turn_copied, formed, q_ready, hi, r1, mid, r2, lo = [sem("nt_" + n) for n in (
                "staged", "turned", "turn_copied", "formed", "q_ready", "hi", "r1", "mid", "r2", "lo")]
            h4, hT, Q, ra, rb = take([N, QG, C]), take([N, 2, N]), take([N, QG, C]), take([N, QG, C]), take([N, QG, C])
            pt = [take([N, QG, C], BF16) for _ in range(2)]
            with ExitStack() as ps:
                tp = ps.enter_context(nc.psum_tensor("nt_tp", [N, 2, N], F32))
                qp = ps.enter_context(nc.psum_tensor("nt_qp", [N, 2, 512], F32))
                block = ps.enter_context(nc.Block())

                @block.gpsimd
                def _(pool):
                    with pool.Fori(0, QUADS) as q:
                        quad = bass.ds(q * QG, QG)
                        pool.wait_ge(turned, q + 1)
                        nc.gpsimd.tensor_copy(h4, H[:, quad, :]).then_inc(staged, 1)
                        pool.wait_ge(hi, q + 1)
                        nc.gpsimd.tensor_tensor(ra, Q, pt[0], ALU.subtract).then_inc(r1, 1)
                        pool.wait_ge(mid, q + 1)
                        nc.gpsimd.tensor_tensor(rb, ra, pt[1], ALU.subtract).then_inc(r2, 1)

                @block.tensor
                def _(pe):
                    starts_free(pe, turned)
                    with pe.Fori(0, QUADS) as q:
                        pe.wait_ge(staged, q + 1)
                        pe.wait_ge(turn_copied, q + 1)
                        for pair in range(2):
                            mm = nc.tensor.transpose(tp[:, pair, :], h4[:, 2 * pair:2 * pair + 2, :].rearrange("p g c -> p (g c)"),
                                                     identf[:])
                        mm.then_inc(turned, 1)
                        pe.wait_ge(turn_copied, q + 2)
                        pe.wait_ge(q_ready, q + 1)
                        for g in range(QG):
                            side = slice((g % 2) * C, (g % 2) * C + C)
                            mm = nc.tensor.matmul(qp[:, g % 2, (g // 2) * C:(g // 2 + 1) * C], hT[side, g // 2, :],
                                                  wcat[side, C:2 * C], start=True, stop=True)
                            mm.then_inc(formed, 1)

                @block.scalar
                def _(act):
                    starts_free(act, turn_copied, q_ready)
                    with act.Fori(0, QUADS) as q:
                        quad = bass.ds(q * QG, QG)
                        act.wait_ge(turned, q + 2)
                        nc.scalar.copy(hT, tp[:]).then_inc(turn_copied, 1)
                        act.wait_ge(formed, q * 4 + 4)
                        act.wait_ge(lo, q + 1)
                        nc.scalar.copy(Q.rearrange("p (a b) c -> p b a c", b=2),
                                       qp[:, :, 0:2 * C].rearrange("p b (a c) -> p b a c", a=2)).then_inc(q_ready, 1)
                        act.wait_ge(q_ready, q + 2)
                        nc.scalar.copy(pt[0], Q).then_inc(hi, 1)
                        act.wait_ge(r1, q + 1)
                        nc.scalar.copy(pt[1], ra).then_inc(mid, 1)
                        act.wait_ge(r2, q + 1)
                        nc.scalar.copy(PARTS[:, 2, quad, :], rb)

                @block.vector
                def _(dve):
                    starts_free(dve, lo)
                    with dve.Fori(0, QUADS) as q:
                        quad = bass.ds(q * QG, QG)
                        dve.wait_ge(hi, q + 1)
                        nc.vector.tensor_copy(PARTS[:, 0, quad, :], pt[0])
                        dve.wait_ge(mid, q + 1)
                        nc.vector.tensor_copy(PARTS[:, 1, quad, :], pt[1]).then_inc(lo, 1)

        def stage_extremes():
            hot_ready = [sem(f"x_hot_ready{k}") for k in range(RING)]
            slot_ready = [sem(f"x_slot_ready{k}") for k in range(RING)]
            flipped = [sem(f"x_flipped{k}") for k in range(RING)]
            prep, maxed, minned = sem("x_prep"), sem("x_maxed"), sem("x_minned")
            hot = [take([N, SG * N], BF16) for _ in range(RING)]
            pad = take([N, SLOTS, B], BF16)
            minus, twice = take([N, N], BF16), take([N, N], BF16)
            TURN = SLOTS // RING
            with ExitStack() as ps:
                gat = [ps.enter_context(nc.psum_tensor(f"x_gat{b}", [N, SG, C], F32)) for b in range(RING)]
                block = ps.enter_context(nc.Block())

                @block.gpsimd
                def _(pool):
                    step = Steps(pool, prep)
                    step(nc.gpsimd.tensor_scalar(minus, identb[:], -1.0, None, ALU.mult))
                    step(nc.gpsimd.tensor_scalar(twice, identb[:], 2.0, None, ALU.mult))
                    absent_slots(nc.gpsimd, step, pad)

                @block.tensor
                def _(pe):
                    def flip(s, r):
                        k = r % RING
                        pe.wait_ge(maxed, s * SLOTS + r + 1)
                        nc.tensor.matmul(gat[k][:], twice, pad[:, r, bass.ds(s * SG, SG)].unsqueeze(2).broadcast_to([N, SG, C]),
                                         start=False, stop=True, skip_group_check=True).then_inc(flipped[k], 1)
                    pe.wait_ge(prep, SLOTS + 2)
                    with pe.Fori(0, SORTS) as s:
                        for r in range(SLOTS + 2):
                            if r < SLOTS:
                                pe.wait_ge(minned, s * SLOTS + max(r - RING + 1, 0) + 1)
                                gather_slot(pe, s, r, hot, hot_ready, slot_ready, pad, minus, gat[r % RING][:])
                            if r >= 2:
                                flip(s, r - 2)

                @block.vector
                def _(dve):
                    starts_free(dve, minned)
                    with dve.Fori(0, SORTS) as s:
                        top, low = MAXQ[:, bass.ds(s * SG, SG), :], MINQ[:, bass.ds(s * SG, SG), :]
                        ahead = RING - 1
                        for r in range(ahead):
                            hot_slot(dve, s, r, hot, hot_ready, slot_ready)
                        for r in range(SLOTS + 3):
                            if r + ahead < SLOTS:
                                hot_slot(dve, s, r + ahead, hot, hot_ready, slot_ready)
                            if r < SLOTS:
                                k = r % RING
                                dve.wait_ge(slot_ready[k], s * TURN + r // RING + 1)
                                if r == 0:
                                    nc.vector.tensor_copy(top, gat[k][:]).then_inc(maxed, 1)
                                else:
                                    dve.wait_ge(maxed, s * SLOTS + r)
                                    nc.vector.tensor_tensor(top, top, gat[k][:], ALU.max).then_inc(maxed, 1)
                            if r >= 3:
                                m = r - 3
                                k = m % RING
                                dve.wait_ge(flipped[k], s * TURN + m // RING + 1)
                                if m == 0:
                                    nc.vector.tensor_copy(low, gat[k][:]).then_inc(minned, 1)
                                else:
                                    dve.wait_ge(minned, s * SLOTS + m + 1)
                                    nc.vector.tensor_tensor(low, low, gat[k][:], ALU.min).then_inc(minned, 1)

        def stage_pna():
            def turns(name, per=1):
                return Turns(sem("pn_" + name), per)
            staged, turned, copied, formed, biased = turns("staged"), turns("turned"), turns("copied"), turns("formed", QG), turns("biased")
            squared, widened, summed, scaled, msq = turns("squared"), turns("widened"), turns("summed"), turns("scaled", 2), turns("msq")
            parts, varied, floored, filled, rooted = turns("parts", 3), turns("varied"), turns("floored"), turns("filled", 4), turns("rooted")
            m_turned, m_copied, joined, added = turns("m_turned"), turns("m_copied", 2), turns("joined"), turns("added", 5)
            ready = sem("pn_ready")
            h4, QQ, m2, q2, pm, sq, vv, mx, mn, o1, o2, o3, o4 = [[take([N, QG, C]) for _ in range(2)] for _ in range(13)]
            hT = [take([N, 2, N]) for _ in range(2)]
            PQO = [take([N, QG, 3 * C]) for _ in range(2)]
            ATf = [take([N, QG, N]) for _ in range(2)]
            M4 = [take([N, QG, 4 * C]) for _ in range(2)]
            MT = [take([N, QG, 2, N]) for _ in range(2)]
            eps = take([N, 1])
            bc = [N, QG, C]
            with ExitStack() as ps:
                tp = ps.enter_context(nc.psum_tensor("pn_tp", [N, 2, 256], F32))
                pq = ps.enter_context(nc.psum_tensor("pn_pq", [N, 2, 512], F32))
                ag = ps.enter_context(nc.psum_tensor("pn_ag", [N, QG, N], F32))
                mt = ps.enter_context(nc.psum_tensor("pn_mt", [N, QG, 2, N], F32))
                jo = ps.enter_context(nc.psum_tensor("pn_jo", [N, 2, 512], F32))
                block = ps.enter_context(nc.Block())
                jv = jo[:, :, 0:6 * C].rearrange("p b (a s c) -> p b a s c", a=2, s=3)

                @block.gpsimd
                def _(pool):
                    P = nc.gpsimd

                    def stage(q, u):
                        turned.wait(pool, q, behind=2)
                        P.tensor_copy(h4[u], H[:, bass.ds(q * QG, QG), :]).then_inc(staged.sem, 1)

                    def own_terms(q, u):
                        quad = bass.ds(q * QG, QG)
                        biased.wait(pool, q)
                        filled.wait(pool, q, behind=2)
                        P.tensor_tensor(pm[u], PQO[u][:, :, 0:C], share[:, quad].unsqueeze(2).broadcast_to(bc), ALU.mult).then_inc(parts.sem, 1)
                        P.tensor_tensor(mx[u], PQO[u][:, :, 0:C], MAXQ[:, quad, :], ALU.add).then_inc(parts.sem, 1)
                        P.tensor_tensor(mn[u], PQO[u][:, :, 0:C], MINQ[:, quad, :], ALU.add).then_inc(parts.sem, 1)

                    def variance(q, u):
                        msq.wait(pool, q)
                        rooted.wait(pool, q, behind=2)
                        P.tensor_tensor(vv[u], q2[u], sq[u], ALU.subtract).then_inc(varied.sem, 1)

                    staged.begin(pool)
                    parts.begin(pool)
                    varied.begin(pool)
                    stage(0, 0)
                    stage(1, 1)

                    def two_quads(q, ahead):
                        for u in range(2):
                            if ahead:
                                stage(q + 2 + u, u)
                        own_terms(q, 0)
                        own_terms(q + 1, 1)
                        variance(q, 0)
                        variance(q + 1, 1)
                    with pool.Fori(0, QUADS // 2 - 1) as i:
                        two_quads(i * 2, True)
                    two_quads(QUADS - 2, False)

                @block.tensor
                def _(pe):
                    def turn(q, u):
                        staged.wait(pe, q)
                        copied.wait(pe, q, behind=1)
                        for pair in range(2):
                            mm = nc.tensor.transpose(tp[:, pair, 0:N], h4[u][:, 2 * pair:2 * pair + 2, :].rearrange("p g c -> p (g c)"),
                                                     identf[:])
                        mm.then_inc(turned.sem, 1)

                    def form(q, u):
                        copied.wait(pe, q)
                        biased.wait(pe, q, behind=1)
                        for g in range(QG):
                            side = slice((g % 2) * C, (g % 2) * C + C)
                            mm = nc.tensor.matmul(pq[:, g % 2, (g // 2) * 3 * C:(g // 2 + 1) * 3 * C], hT[u][side, g // 2, :],
                                                  wcat[side, :], start=True, stop=True)
                            mm.then_inc(formed.sem, 1)

                    def aggregate(q, u):
                        squared.wait(pe, q)
                        widened.wait(pe, q)
                        scaled.wait(pe, q, behind=1)
                        for g in range(QG):
                            nc.tensor.matmul(ag[:, g, 0:C], ATf[u][:, g, :], PQO[u][:, g, C:2 * C], start=True, stop=True)
                            mm = nc.tensor.matmul(ag[:, g, C:2 * C], ATf[u][:, g, :], QQ[u][:, g, :], start=True, stop=True)
                        mm.then_inc(summed.sem, 1)

                    def turn_aggregates(q, u):
                        filled.wait(pe, q)
                        rooted.wait(pe, q)
                        m_copied.wait(pe, q, behind=1)
                        for g in range(QG):
                            for k in range(2):
                                mm = nc.tensor.transpose(mt[:, g, k, :], M4[u][:, g, k * N:(k + 1) * N], identf[:])
                        mm.then_inc(m_turned.sem, 1)

                    def join(q, u):
                        m_copied.wait(pe, q)
                        added.wait(pe, q, 3, behind=1)
                        for g in range(QG):
                            for k in range(2):
                                mm = nc.tensor.matmul(jo[:, g // 2, (g % 2) * 3 * C:(g % 2 + 1) * 3 * C], MT[u][:, g, k, :],
                                                      wm[:, k].rearrange("p s c -> p (s c)"), start=(k == 0), stop=(k == 1))
                        mm.then_inc(joined.sem, 1)

                    for t in (turned, formed, summed, m_turned, joined):
                        t.begin(pe)
                    for u in range(2):
                        turn(u, u)
                        form(u, u)

                    def two_quads(q, ahead):
                        for u in range(2):
                            aggregate(q + u, u)
                            if ahead:
                                turn(q + 2 + u, u)
                        for u in range(2):
                            turn_aggregates(q + u, u)
                            if ahead:
                                form(q + 2 + u, u)
                        for u in range(2):
                            join(q + u, u)
                    with pe.Fori(0, QUADS // 2 - 1) as i:
                        two_quads(i * 2, True)
                    two_quads(QUADS - 2, False)

                @block.scalar
                def _(act):
                    S = nc.scalar

                    def copy_in(q, u):
                        turned.wait(act, q)
                        formed.wait(act, q, behind=2)
                        S.copy(hT[u], tp[:, :, 0:N]).then_inc(copied.sem, 1)

                    def widen(q, u):
                        summed.wait(act, q, behind=2)
                        S.copy(ATf[u], AT[:, bass.ds(q * QG, QG), :]).then_inc(widened.sem, 1)
                        biased.wait(act, q)
                        S.activation(QQ[u], PQO[u][:, :, C:2 * C], ACT.Square).then_inc(squared.sem, 1)

                    def square_mean(q, u):
                        scaled.wait(act, q)
                        varied.wait(act, q, behind=2)
                        S.activation(sq[u], m2[u], ACT.Square).then_inc(msq.sem, 1)

                    def root(q, u):
                        floored.wait(act, q)
                        m_turned.wait(act, q, behind=2)
                        S.activation(M4[u][:, :, 3 * C:4 * C], vv[u], ACT.Sqrt, bias=eps).then_inc(rooted.sem, 1)

                    def copy_aggregates(q, u):
                        m_turned.wait(act, q)
                        joined.wait(act, q, behind=2)
                        for half in range(2):
                            S.copy(MT[u][:, 2 * half:2 * half + 2], mt[:, 2 * half:2 * half + 2]).then_inc(m_copied.sem, 1)

                    for t in (copied, widened, squared, msq, rooted, m_copied):
                        t.begin(act)
                    act.wait_ge(ready, 1)
                    S.preload_act_table(ACT.Sqrt)
                    for u in range(2):
                        copy_in(u, u)
                        widen(u, u)

                    def two_quads(q, ahead):
                        for u in range(2):
                            square_mean(q + u, u)
                            if ahead:
                                copy_in(q + 2 + u, u)
                        for u in range(2):
                            root(q + u, u)
                            copy_aggregates(q + u, u)
                            if ahead:
                                widen(q + 2 + u, u)
                    with act.Fori(0, QUADS // 2 - 1) as i:
                        two_quads(i * 2, True)
                    two_quads(QUADS - 2, False)

                @block.vector
                def _(dve):
                    V = nc.vector

                    def add_bias(q, u):
                        formed.wait(dve, q)
                        filled.wait(dve, q, behind=2)
                        summed.wait(dve, q, behind=2)
                        V.tensor_tensor(PQO[u].rearrange("p (a b) c -> p b a c", b=2),
                                        pq[:, :, 0:6 * C].rearrange("p b (a c) -> p b a c", a=2),
                                        bias.unsqueeze(1).unsqueeze(1).broadcast_to([N, 2, 2, 3 * C]), ALU.add).then_inc(biased.sem, 1)

                    def scale(q, u):
                        rb = rdeg[:, bass.ds(q * QG, QG)].unsqueeze(2).broadcast_to(bc)
                        summed.wait(dve, q)
                        varied.wait(dve, q, behind=2)
                        V.tensor_tensor(m2[u], ag[:, :, 0:C], rb, ALU.mult).then_inc(scaled.sem, 1)
                        V.tensor_tensor(q2[u], ag[:, :, C:2 * C], rb, ALU.mult).then_inc(scaled.sem, 1)

                    def fill(q, u):
                        quad = bass.ds(q * QG, QG)
                        parts.wait(dve, q)
                        scaled.wait(dve, q)
                        m_turned.wait(dve, q, behind=2)
                        V.tensor_tensor(M4[u][:, :, 0:C], m2[u], pm[u], ALU.add).then_inc(filled.sem, 1)
                        V.tensor_scalar(M4[u][:, :, C:2 * C], mx[u], -NEG_BIG, None, ALU.max).then_inc(filled.sem, 1)
                        V.tensor_scalar(M4[u][:, :, 2 * C:3 * C], mn[u], NEG_BIG, None, ALU.min).then_inc(filled.sem, 1)
                        added.wait(dve, q, behind=2)
                        V.tensor_tensor(o3[u], PQO[u][:, :, 2 * C:3 * C], X[:, quad, :], ALU.add).then_inc(filled.sem, 1)
                        varied.wait(dve, q)
                        V.tensor_scalar(vv[u], vv[u], 0.0, None, ALU.max).then_inc(floored.sem, 1)

                    def finish(q, u):
                        quad = bass.ds(q * QG, QG)
                        joined.wait(dve, q)
                        added.wait(dve, q, behind=1)
                        o1v, o2v, o3v, o4v = [o[u].rearrange("p (b a) c -> p b a c", b=2) for o in (o1, o2, o3, o4)]
                        ampb, attb = [t[:, quad].rearrange("p (b a) -> p b a", b=2).unsqueeze(3).broadcast_to([N, 2, 2, C])
                                      for t in (amp, att)]
                        V.tensor_tensor(o1v, jv[:, :, :, 1, :], ampb, ALU.mult).then_inc(added.sem, 1)
                        V.tensor_tensor(o2v, jv[:, :, :, 2, :], attb, ALU.mult).then_inc(added.sem, 1)
                        V.tensor_tensor(o4v, jv[:, :, :, 0, :], o3v, ALU.add).then_inc(added.sem, 1)
                        added.wait(dve, q, 2)
                        V.tensor_tensor(o1[u], o1[u], o2[u], ALU.add).then_inc(added.sem, 1)
                        added.wait(dve, q, 4)
                        V.tensor_tensor(X[:, quad, :], o1[u], o4[u], ALU.add).then_inc(added.sem, 1)

                    V.memset(eps, LN_EPS).then_inc(ready, 1)
                    for t in (biased, scaled, filled, floored, added):
                        t.begin(dve)
                    add_bias(0, 0)
                    add_bias(1, 1)

                    def two_quads(q, ahead):
                        for u in range(2):
                            scale(q + u, u)
                        for u in range(2):
                            fill(q + u, u)
                        for u in range(2):
                            if ahead:
                                add_bias(q + 2 + u, u)
                        for u in range(2):
                            finish(q + u, u)
                    with dve.Fori(0, QUADS // 2 - 1) as i:
                        two_quads(i * 2, True)
                    two_quads(QUADS - 2, False)

        def stage_gcn():
            HID = W["L3_gnn_W1"].shape[0]
            LAYERS = 3
            loaded, even_done = sem("gc_loaded"), sem("gc_even_done")

            def turns(name, per=1):
                return Turns(sem("gc_" + name), per)
            staged, turned, copied = turns("staged"), turns("turned"), turns("copied", 2)
            messaged, biased, summed, rectified = [[turns(f"{n}{u}_", LAYERS) for u in range(2)]
                                                   for n in ("messaged", "biased", "summed", "rectified")]
            joined, added = turns("joined"), turns("added", 3)
            h4 = [take([N, QG, C]) for _ in range(2)]
            hT = [take([N, 2, N]) for _ in range(2)]
            ATf = [take([N, QG, N]) for _ in range(2)]
            msg = [take([N, QG, HID]) for _ in range(2)]
            hid = [take([N, QG, N]) for _ in range(2)]
            y1 = [take([N, QG, C]) for _ in range(2)]
            y2 = [take([N, QG, C]) for _ in range(2)]
            w0, wh = take([N, HID]), take([N, 2, HID])
            wo, bb, bo = take([N, C]), take([N, 3, HID]), take([N, C])
            with ExitStack() as ps:
                tp = ps.enter_context(nc.psum_tensor("gc_tp", [N, 2, 256], F32))
                m0 = ps.enter_context(nc.psum_tensor("gc_m0", [N, 2, 512], F32))
                mp = [ps.enter_context(nc.psum_tensor(f"gc_mp{u}", [N, QG, HID], F32)) for u in range(2)]
                ap = [ps.enter_context(nc.psum_tensor(f"gc_ap{u}", [N, QG, N], F32)) for u in range(2)]
                op = ps.enter_context(nc.psum_tensor("gc_op", [N, 2 * QG, C], F32))
                block = ps.enter_context(nc.Block())

                @block.sync
                def _(sp):
                    for side in (0, C):
                        sp.dma_start(w0[side:side + C, :], W["L3_gnn_W0"]).then_inc(loaded, 16)
                    for k in range(2):
                        sp.dma_start(wh[:, k, :], W[f"L3_gnn_W{k + 1}"]).then_inc(loaded, 16)
                    sp.dma_start(wo, W["L3_gnn_Wout"]).then_inc(loaded, 16)
                    for k in range(3):
                        sp.dma_start(bb[:, k, :], W[f"L3_gnn_b{k}"].partition_broadcast(N)).then_inc(loaded, 16)
                    sp.dma_start(bo, W["L3_gnn_bout"].partition_broadcast(N)).then_inc(loaded, 16)

                @block.gpsimd
                def _(pool):
                    staged.begin(pool)
                    with pool.Fori(0, QUADS // 2) as i:
                        for u in range(2):
                            q = i * 2 + u
                            turned.wait(pool, q, behind=2)
                            nc.gpsimd.tensor_copy(h4[u], H[:, bass.ds(q * QG, QG), :]).then_inc(staged.sem, 1)

                @block.tensor
                def _(pe):
                    def turn(i, u):
                        q = i * 2 + u
                        staged.wait(pe, q)
                        copied.wait(pe, q, behind=1)
                        for pair in range(2):
                            mm = nc.tensor.transpose(tp[:, pair, 0:N], h4[u][:, 2 * pair:2 * pair + 2, :].rearrange("p g c -> p (g c)"),
                                                     identf[:])
                        mm.then_inc(turned.sem, 1)

                    def first_message(i, u):
                        q = i * 2 + u
                        copied.wait(pe, q)
                        biased[1 - u].wait(pe, i, 1, behind=1 - u)
                        for g in range(QG):
                            side = slice((g % 2) * C, (g % 2) * C + C)
                            mm = nc.tensor.matmul(m0[:, g % 2, (g // 2) * HID:(g // 2 + 1) * HID], hT[u][side, g // 2, :],
                                                  w0[side, :], start=True, stop=True)
                            if g == QG - 2:
                                mm.then_inc(even_done, 1)
                        mm.then_inc(messaged[u].sem, 1)

                    def message(i, u, layer):
                        q = i * 2 + u
                        rectified[u].wait(pe, i, layer)
                        if layer == 1:
                            biased[u].wait(pe, i, behind=1)
                        else:
                            biased[u].wait(pe, i, layer)
                        for g in range(QG):
                            mm = nc.tensor.matmul(mp[u][:, g, :], hid[u][:, g, :], wh[:, layer - 1, :], start=True, stop=True)
                        mm.then_inc(messaged[u].sem, 1)

                    def aggregate(i, u, layer):
                        q = i * 2 + u
                        biased[u].wait(pe, i, layer + 1)
                        if layer == 0:
                            rectified[u].wait(pe, i, behind=1)
                        else:
                            rectified[u].wait(pe, i, layer)
                        for g in range(QG):
                            mm = nc.tensor.matmul(ap[u][:, g, :], msg[u][:, g, :], ATf[u][:, g, :], start=True, stop=True)
                        mm.then_inc(summed[u].sem, 1)

                    def join(i, u):
                        q = i * 2 + u
                        rectified[u].wait(pe, i)
                        added.wait(pe, q, 1, behind=1)
                        for g in range(QG):
                            mm = nc.tensor.matmul(op[:, g, :], hid[u][:, g, :], wo, start=True, stop=True)
                        mm.then_inc(joined.sem, 1)

                    for t in [turned, joined] + messaged + summed:
                        t.begin(pe)
                    pe.sem_inc(even_done, 1)
                    pe.wait_ge(loaded, 144)
                    turn(0, 0)
                    turn(0, 1)

                    def two_quads(i, ahead):
                        first_message(i, 0)
                        first_message(i, 1)
                        aggregate(i, 0, 0)
                        aggregate(i, 1, 0)
                        for layer in range(1, LAYERS):
                            message(i, 0, layer)
                            message(i, 1, layer)
                            if ahead and layer == LAYERS - 1:
                                turn(i + 1, 0)
                            aggregate(i, 0, layer)
                            aggregate(i, 1, layer)
                        join(i, 0)
                        join(i, 1)
                        if ahead:
                            turn(i + 1, 1)
                    with pe.Fori(0, QUADS // 2 - 1) as i:
                        two_quads(i, True)
                    two_quads(QUADS // 2 - 1, False)

                @block.scalar
                def _(act):
                    def copy_in(i, u):
                        q = i * 2 + u
                        turned.wait(act, q)
                        messaged[u].wait(act, i, 1, behind=1)
                        nc.scalar.copy(hT[u], tp[:, :, 0:N]).then_inc(copied.sem, 1)
                        summed[u].wait(act, i, behind=1)
                        nc.scalar.copy(ATf[u], AT[:, bass.ds(q * QG, QG), :]).then_inc(copied.sem, 1)

                    def rectify(i, u, layer):
                        q = i * 2 + u
                        summed[u].wait(act, i, layer + 1)
                        if layer == 0:
                            joined.wait(act, q, behind=2)
                        nc.scalar.activation(hid[u], ap[u][:], ACT.Relu).then_inc(rectified[u].sem, 1)

                    for t in [copied] + rectified:
                        t.begin(act)
                    copy_in(0, 0)
                    copy_in(0, 1)

                    def two_quads(i, ahead):
                        for layer in range(LAYERS):
                            rectify(i, 0, layer)
                            if ahead and layer == LAYERS - 1:
                                copy_in(i + 1, 0)
                            rectify(i, 1, layer)
                        if ahead:
                            copy_in(i + 1, 1)
                    with act.Fori(0, QUADS // 2 - 1) as i:
                        two_quads(i, True)
                    two_quads(QUADS // 2 - 1, False)

                @block.vector
                def _(dve):
                    V = nc.vector

                    def add_bias(i, u, layer):
                        q = i * 2 + u
                        messaged[u].wait(dve, i, layer + 1)
                        if layer == 0:
                            dve.wait_ge(even_done, q + 2)
                            summed[u].wait(dve, i, behind=1)
                            V.tensor_tensor(msg[u].rearrange("p (a b) c -> p b a c", b=2),
                                            m0[:, :, 0:2 * HID].rearrange("p b (a c) -> p b a c", a=2),
                                            bb[:, 0, :].unsqueeze(1).unsqueeze(1).broadcast_to([N, 2, 2, HID]),
                                            ALU.add).then_inc(biased[u].sem, 1)
                        else:
                            summed[u].wait(dve, i, layer)
                            V.tensor_tensor(msg[u], mp[u][:], bb[:, layer, :].unsqueeze(1).broadcast_to([N, QG, HID]),
                                            ALU.add).then_inc(biased[u].sem, 1)

                    def finish(i, u):
                        q = i * 2 + u
                        quad = bass.ds(q * QG, QG)
                        joined.wait(dve, q)
                        added.wait(dve, q, behind=1)
                        V.tensor_tensor(y1[u], op[:, 0:QG, :], bo.unsqueeze(1).broadcast_to([N, QG, C]), ALU.add).then_inc(added.sem, 1)
                        added.wait(dve, q, 1)
                        V.tensor_tensor(y2[u], y1[u], mask[:, quad].unsqueeze(2).broadcast_to([N, QG, C]), ALU.mult).then_inc(added.sem, 1)
                        added.wait(dve, q, 2)
                        V.tensor_tensor(X[:, quad, :], X[:, quad, :], y2[u], ALU.add).then_inc(added.sem, 1)

                    for t in [added] + biased:
                        t.begin(dve)
                    dve.wait_ge(loaded, 144)
                    with dve.Fori(0, QUADS // 2) as i:
                        for layer in range(LAYERS):
                            add_bias(i, 0, layer)
                            add_bias(i, 1, layer)
                        finish(i, 0)
                        finish(i, 1)

        def stage_aggregation():
            nonlocal degree, rdeg, share, amp, att, wcat, wm, bias, MAXQ, MINQ
            used[0] = 0
            degree, rdeg, share, amp, att = [take([N, B]) for _ in range(5)]
            wcat, wm, bias = take([N, 3 * C]), take([N, 2, 3, C]), take([N, 3 * C])
            MAXQ, MINQ = take([N, B, C]), take([N, B, C])
            base = used[0]
            for stage in (load_pna, stage_degrees, stage_neighbour_terms, stage_extremes,
                          lambda: stage_general("xg_", False), stage_pna):
                used[0] = base
                stage()

        degree = rdeg = share = amp = att = wcat = wm = bias = MAXQ = MINQ = None

        def stage_attention():
            nonlocal x2, uw, ox, coef, cu, ncu, cox, hcox, selfl, SUMS
            used[0] = 0
            x2, uw, ox, coef, cu, ncu, cox, hcox, selfl = [take([N, B]) for _ in range(9)]
            SUMS = take([N, B, C + 2])
            base = used[0]
            for stage in (stage_columns, stage_pairs, stage_expmap):
                used[0] = base
                stage()

        x2 = uw = ox = coef = cu = ncu = cox = hcox = selfl = SUMS = None

        def stage_store():
            stored = sem("stored")
            with nc.Block() as block:
                @block.sync
                def _(sp):
                    sp.dma_start(out.rearrange("g i c -> i g c"), X[:]).then_inc(stored, 16)
                    sp.wait_ge(stored, 16)

        stage_constants()
        stage_positions("thin_", True)
        stage_norm(0, True)
        stage_first()
        stage_mlp()
        end_layer()
        stage_norm(1, False)
        stage_attention()
        end_layer()
        stage_positions("pna_", False)
        stage_norm(2, False)
        stage_aggregation()
        stage_norm(3, False)
        used[0] = 0
        stage_gcn()
        stage_store()
        end_layer()


def kernel(**inputs):
    import numpy as _np
    import concourse.bacc as _bacc
    from concourse import mybir as _mybir
    from concourse.bass_utils import run_bass_kernel_spmd as _run

    nc = _bacc.Bacc("TRN2", target_bir_lowering=False, num_devices=1)
    arrays, weights = {}, {}
    for name in inputs:
        a = _np.ascontiguousarray(inputs[name])
        if a.dtype == _np.bool_:
            a = a.view(_np.uint8)
        arrays[f"in_{name}_dram"] = a
        weights[name] = nc.dram_tensor(f"in_{name}_dram", a.shape, _mybir.dt.from_np(a.dtype), kind="ExternalInput").ap()
    x, adj, nodemask = (weights.pop(n) for n in ("x", "adj", "nodemask"))
    out = nc.dram_tensor("out_0_dram", x.shape, _mybir.dt.float32, kind="ExternalOutput").ap()
    build(nc, x, adj, nodemask, weights, out)
    r = _run(nc, [arrays], core_ids=[0])
    return r.results[0]["out_0_dram"]
```

```python
from contextlib import ExitStack

import concourse.bass as bass
from concourse import mybir

ALU = mybir.AluOpType
ACT = mybir.ActivationFunctionType
F32 = mybir.dt.float32
BF16 = mybir.dt.bfloat16
I32 = mybir.dt.int32
U8 = mybir.dt.uint8
AX = mybir.AxisListType.X

SLOTS = 20
RING = 5
QG = 4
SG = 8
BIG = 2.0 ** 100
ROUND = 2.0 ** 23
TAUS = ((0.25, 0.25), (0.5, 0.5), (0.75, 0.25))
TIERS = ((64, 64, 9, 3, 8, 2), (16, 48, 12, 4, 8, 2), (0, 16, 20, 10, 8, 2))
ORDERS = 16
PIECES = 4
MIN_NORM = 1e-15
ATANH_MAX = 1.0 - 2.0 ** -23
LN_EPS = 1e-5
CLAMP = 1000000.0
AVG_D_LOG = 4.86
NEG_BIG = 1000000000.0
BALL = 1.0 - 0.004

SELECTION = {
    9: (
          (6, 7), (4, 5), (2, 3), (5, 7), (0, 1), (0, 2), (4, 6), (1, 3), (5, 6), (0, 4), (1, 2), (3, 7),
          (4, 8), (2, 6), (1, 5), (2, 8), (1, 4), (3, 8), (2, 4), (3, 5), (6, 8), (5, 6), (3, 4)),
    12: (
          (0, 1), (4, 5), (2, 3), (9, 11), (8, 10), (6, 7), (0, 2), (4, 6), (1, 3), (8, 9), (7, 10), (0, 8),
          (5, 7), (2, 9), (1, 11), (3, 7), (10, 11), (3, 10), (7, 11), (1, 5), (0, 4), (6, 9), (9, 10), (5, 9),
          (7, 10), (2, 8), (1, 4), (7, 9), (4, 8), (5, 8), (2, 6), (3, 6), (3, 5), (1, 2), (2, 4), (6, 8),
          (7, 8), (3, 4), (5, 6)),
    20: (
          (2, 3), (4, 5), (0, 1), (6, 7), (14, 15), (10, 11), (18, 19), (8, 9), (9, 11), (5, 7), (0, 2),
          (12, 13), (8, 10), (1, 3), (12, 14), (13, 15), (8, 12), (13, 14), (11, 15), (4, 6), (0, 4), (9, 10),
          (10, 14), (16, 17), (17, 19), (5, 6), (1, 2), (9, 13), (2, 6), (3, 7), (1, 5), (3, 5), (3, 19),
          (11, 13), (2, 4), (1, 2), (16, 18), (17, 18), (10, 12), (2, 18), (9, 10), (2, 10), (13, 14), (0, 3),
          (7, 19), (5, 6), (5, 13), (1, 9), (11, 12), (3, 4), (0, 8), (5, 9), (4, 12), (7, 15), (6, 14), (4, 8),
          (3, 11), (14, 18), (6, 10), (10, 14), (2, 4), (1, 2), (7, 11), (8, 16), (7, 9), (11, 13), (3, 17),
          (2, 3), (13, 14), (10, 16), (12, 16), (9, 17), (4, 8), (14, 17), (11, 14), (16, 19), (3, 8), (5, 9),
          (6, 10), (13, 14), (14, 16), (6, 8), (9, 12), (13, 14), (11, 13), (7, 10), (7, 9), (3, 5), (10, 12),
          (7, 8), (3, 4), (11, 12), (9, 10), (5, 6), (15, 16)),
}


def layered(comparators):
    layers, depth = [], {}
    for a, b in comparators:
        at = max(depth.get(a, 0), depth.get(b, 0))
        if at == len(layers):
            layers.append([])
        layers[at].append((a, b))
        depth[a] = depth[b] = at + 1
    return layers


def live_halves(layers, outputs):
    live, kept = set(outputs), []
    for layer in reversed(layers):
        rows = [(a, b, a in live, b in live) for a, b in layer if a in live or b in live]
        for a, b, _, _ in rows:
            live |= {a, b}
        kept.insert(0, rows)
    return kept


class Steps:
    def __init__(self, eng, sem, per=0, turn=0):
        self.eng, self.sem, self.per, self.turn, self.k = eng, sem, per, turn, 0

    def __call__(self, ins):
        ins.then_inc(self.sem, 1)
        self.k += 1
        return ins

    def wait(self, back=0):
        if self.k > back:
            self.eng.wait_ge(self.sem, self.turn * self.per + self.k - back)

    def end(self):
        assert self.per == self.k, (self.per, self.k)


class Turns:
    def __init__(self, sem, per=1):
        self.sem, self.per = sem, per

    def begin(self, eng):
        eng.sem_inc(self.sem, 2 * self.per)

    def wait(self, eng, turn, k=None, behind=0):
        k = self.per if k is None else k
        eng.wait_ge(self.sem, (turn + (2 - behind)) * self.per + k if behind < 2 else turn * self.per + k)


def starts_free(eng, *sems):
    for s in sems:
        eng.sem_inc(s, 1)


def build(nc, x, adj, nodemask, W, out, stop=99):
    B, N, C = x.shape
    assert N == 128 and C == 64 and B % SG == 0
    HID = W["L0_gnn_W1"].shape[1]
    QUADS, SORTS = B // QG, B // SG
    with ExitStack() as ctx:
        def sb(name, shape, dt=F32):
            return ctx.enter_context(nc.sbuf_tensor(name, shape, dt))

        layer_sems = []

        def sem(name):
            layer_sems.append(nc.alloc_semaphore(name=name))
            return layer_sems[-1]

        def end_layer():
            nc.clear_and_free_semaphores(list(layer_sems))
            nc.all_engine_barrier()
            layer_sems.clear()

        X = sb("X", [N, B, C])
        H = sb("H", [N, B, C])
        AT = sb("AT", [N, B, N], BF16)
        POS = sb("POS", [N, B, N], BF16)
        PARTS = sb("PARTS", [N, 3, B, C], BF16)
        identf = sb("identf", [N, N])
        identb = sb("identb", [N, N], BF16)
        offdiag = sb("offdiag", [N, N], BF16)
        upper = sb("upper", [N, N], BF16)
        onesb = sb("onesb", [N, N], BF16)
        onesf = sb("onesf", [1, N])
        slot_no = sb("slot_no", [N, SLOTS])
        mask = sb("mask", [N, B])
        count = sb("count", [N, B])
        w1 = sb("w1", [2 * C, HID])
        b1 = sb("b1", [HID, 1])
        w2 = sb("w2", [HID, C])
        b2 = sb("b2", [1, C])
        ROOM = 29736
        room = sb("room", [N, ROOM])
        used = [0]

        def take(shape, dt=F32):
            size = 1
            for s in shape[1:]:
                size *= s
            words = size if dt == F32 or dt == I32 else size // 2
            a = used[0]
            used[0] += words
            assert used[0] <= ROOM, used[0]
            piece = room[0:shape[0], a:a + words]
            if dt != F32:
                piece = piece.bitcast(dt)
            names = "abcd"[:len(shape) - 1]
            if len(names) > 1:
                piece = piece.rearrange("p (" + " ".join(names) + ") -> p " + " ".join(names),
                                        **{n: s for n, s in zip(names, shape[1:])})
            return piece

        def stage_constants():
            used[0] = 0
            loaded, made, turned = sem("loaded"), sem("made"), sem("turned")
            mrow8, mrow = take([N, N // 4]), take([N, N])
            mrow8 = mrow8.bitcast(U8)
            with nc.psum_tensor("mT", [N, B], F32) as mT, nc.Block() as block:
                @block.sync
                def _(sp):
                    sp.dma_start(mrow8[0:B, :], nodemask).then_inc(loaded, 16)
                    sp.dma_start(X[:], x.rearrange("g i c -> i g c")).then_inc(loaded, 16)
                    sp.dma_start(w1[0:C, :], W["L0_gnn_W1"]).then_inc(loaded, 16)
                    sp.dma_start(w1[C:2 * C, :], W["L0_gnn_W1"]).then_inc(loaded, 16)
                    sp.dma_start(b1[:], W["L0_gnn_b1"].rearrange("(h a) -> h a", a=1)).then_inc(loaded, 16)
                    sp.dma_start(w2[:], W["L0_gnn_W2"]).then_inc(loaded, 16)
                    sp.dma_start(b2[:], W["L0_gnn_b2"].rearrange("(a c) -> a c", a=1)).then_inc(loaded, 16)
                    sp.wait_ge(loaded, 112)

                @block.gpsimd
                def _(pool):
                    step = Steps(pool, made)
                    step(nc.gpsimd.memset(onesf[:], 1.0))
                    step(nc.gpsimd.memset(onesb[:], 1.0))
                    step(nc.gpsimd.memset(identf[:], 0.0))
                    step.wait()
                    step(nc.gpsimd.affine_select(out=identf[:], in_=identf[:], compare_op=ALU.not_equal,
                                                 fill=1.0, base=0, pattern=[[-1, N]], channel_multiplier=1))
                    step(nc.gpsimd.affine_select(out=upper[:], in_=onesb[:], compare_op=ALU.is_ge,
                                                 fill=0.0, base=0, pattern=[[1, N]], channel_multiplier=-1))
                    step(nc.gpsimd.affine_select(out=offdiag[:], in_=onesb[:], compare_op=ALU.not_equal,
                                                 fill=0.0, base=0, pattern=[[-1, N]], channel_multiplier=1))
                    step(nc.gpsimd.iota(slot_no[:], pattern=[[1, SLOTS]], base=0, channel_multiplier=0,
                                        allow_small_or_imprecise_dtypes=True))
                    step.wait()
                    step(nc.gpsimd.tensor_copy(identb[:], identf[:]))
                    pool.wait_ge(loaded, 112)
                    step(nc.gpsimd.tensor_copy(mrow[0:B, :], mrow8[0:B, :]))

                @block.tensor
                def _(pe):
                    pe.wait_ge(made, 9)
                    nc.tensor.transpose(mT[:], mrow[0:B, :], identf[0:B, 0:B]).then_inc(turned, 1)

                @block.vector
                def _(dve):
                    dve.wait_ge(turned, 1)
                    nc.vector.tensor_copy(mask[:], mT[:]).then_inc(made, 1)

        def stage_thinned():
            used[0] = 0

            def turns(name, per=1):
                return Turns(sem("th_" + name), per)
            adj_in, stepped = [sem(f"th_adj_in{u}") for u in range(2)], sem("th_stepped")
            turned, at_ready, prepared, ranked, rem_ready, rem_both, kept = (
                turns("turned"), turns("at"), turns("prepared", 3), turns("ranked"), turns("rem"), turns("both"), turns("kept"))
            A = [take([N, QG, N]) for _ in range(2)]
            nat, natT, own = [[take([N, QG, N], BF16) for _ in range(2)] for _ in range(3)]
            e1, e2, rem = take([N, QG, N]), take([N, QG, N]), take([N, QG, N], BF16)
            half, up, skip, cond, cm, sk1, sk2, sk0 = [take([N, QG]) for _ in range(8)]
            bc = [N, QG, N]
            with ExitStack() as ps:
                tA, rank, both = [ps.enter_context(nc.psum_tensor("th_" + n, [N, QG, N], F32)) for n in ("tA", "rank", "both")]
                block = ps.enter_context(nc.Block())

                @block.sync
                def _(sp):
                    def load(q, u):
                        sp.dma_start(A[u], adj[bass.ds(q * QG, QG)].rearrange("g i j -> i g j")).then_inc(adj_in[u], 16)
                    load(0, 0)
                    load(1, 1)
                    with sp.Fori(0, QUADS // 2 - 1) as i:
                        for u in range(2):
                            q = i * 2 + u
                            turned.wait(sp, q)
                            prepared.wait(sp, q, 1)
                            load(q + 2, u)

                @block.gpsimd
                def _(pool):
                    P = nc.gpsimd
                    prepared.begin(pool)
                    off, diagonal = [t[:].unsqueeze(1).broadcast_to(bc) for t in (offdiag, identb)]
                    with pool.Fori(0, QUADS // 2) as i:
                        for u in range(2):
                            q = i * 2 + u
                            kept.wait(pool, q, behind=2)
                            pool.wait_ge(adj_in[u], i * 16 + 16)
                            P.tensor_tensor(nat[u], A[u], off, ALU.mult).then_inc(prepared.sem, 1)
                            at_ready.wait(pool, q)
                            P.tensor_tensor(natT[u], AT[:, bass.ds(q * QG, QG), :], off, ALU.mult).then_inc(prepared.sem, 1)
                            prepared.wait(pool, q, 1)
                            P.tensor_tensor(own[u], nat[u], diagonal, ALU.add).then_inc(prepared.sem, 1)

                @block.scalar
                def _(act):
                    at_ready.begin(act)
                    with act.Fori(0, QUADS) as q:
                        turned.wait(act, q)
                        nc.scalar.copy(AT[:, bass.ds(q * QG, QG), :], tA[:]).then_inc(at_ready.sem, 1)

                @block.tensor
                def _(pe):
                    def turn(i, u):
                        q = i * 2 + u
                        pe.wait_ge(adj_in[u], i * 16 + 16)
                        at_ready.wait(pe, q, behind=1)
                        for g in range(QG):
                            mm = nc.tensor.transpose(tA[:, g, :], A[u][:, g, :], identf[:])
                        mm.then_inc(turned.sem, 1)

                    def thin(i, u, ahead):
                        q = i * 2 + u
                        prepared.wait(pe, q, 2)
                        rem_ready.wait(pe, q, behind=1)
                        for g in range(QG):
                            mm = nc.tensor.matmul(rank[:, g, :], natT[u][:, g, :], upper[:], start=True, stop=True)
                        mm.then_inc(ranked.sem, 1)
                        if ahead:
                            turn(i + u, 1 - u)
                        rem_ready.wait(pe, q)
                        kept.wait(pe, q, behind=1)
                        for g in range(QG):
                            nc.tensor.matmul(both[:, g, :], rem[:, g, :], identb[:], start=True, stop=False)
                            mm = nc.tensor.matmul(both[:, g, :], identb[:], rem[:, g, :], start=False, stop=True)
                        mm.then_inc(rem_both.sem, 1)

                    for t in (turned, ranked, rem_both):
                        t.begin(pe)
                    turn(0, 0)
                    with pe.Fori(0, QUADS // 2 - 1) as i:
                        thin(i, 0, True)
                        thin(i, 1, True)
                    thin(QUADS // 2 - 1, 0, True)
                    thin(QUADS // 2 - 1, 1, False)

                @block.vector
                def _(dve):
                    V = nc.vector
                    rem_ready.begin(dve)
                    kept.begin(dve)
                    with dve.Fori(0, QUADS // 2) as i:
                        for u in range(2):
                            q = i * 2 + u
                            quad = bass.ds(q * QG, QG)
                            step = Steps(dve, stepped, 12, q)
                            ranked.wait(dve, q)
                            nb = rank[:, :, N - 1]
                            step(V.tensor_scalar(half, nb, 0.5, 0.25, ALU.mult, ALU.add))
                            step(V.scalar_tensor_tensor(out=cond, in0=nb, scalar=10.5, in1=mask[:, quad],
                                                        op0=ALU.is_gt, op1=ALU.mult))
                            step.wait(1)
                            step(V.tensor_scalar(up, half, ROUND, None, ALU.add))
                            step.wait(1)
                            step(V.tensor_scalar(cm, cond, 1.0, None, ALU.subtract))
                            step.wait(1)
                            step(V.tensor_scalar(skip, up, ROUND, None, ALU.subtract))
                            step.wait()
                            step(V.tensor_tensor(sk0, skip, cond, ALU.mult))
                            step.wait()
                            step(V.tensor_tensor(sk1, sk0, cm, ALU.add))
                            step.wait()
                            step(V.tensor_scalar(sk2, sk1, 2.0, None, ALU.mult))
                            step(V.tensor_tensor(e1, rank[:], sk1.unsqueeze(2).broadcast_to(bc), ALU.is_equal))
                            step.wait(1)
                            step(V.tensor_tensor(e2, rank[:], sk2.unsqueeze(2).broadcast_to(bc), ALU.is_equal))
                            step.wait()
                            step(V.tensor_tensor(e1, e1, e2, ALU.add))
                            step.wait()
                            prepared.wait(dve, q)
                            V.tensor_tensor(rem, e1, nat[u], ALU.mult).then_inc(rem_ready.sem, 1)
                            rem_both.wait(dve, q)
                            V.scalar_tensor_tensor(out=POS[:, quad, :], in0=both[:], scalar=0.0, in1=own[u],
                                                   op0=ALU.is_equal, op1=ALU.mult).then_inc(kept.sem, 1)
                            kept.wait(dve, q)
                            step(V.tensor_reduce(count[:, quad], POS[:, quad, :], AX, ALU.add))
                            step.end()

        def stage_positions():
            used[0] = 0
            kept_ready, summed, placed = sem("pos_kept"), sem("pos_summed"), sem("pos_placed")
            keepT = take([N, SG, N], BF16)
            HALF = 4
            with nc.psum_tensor("cum", [N, SG, N], F32) as cum, nc.psum_tensor("nv", [N, SG], F32) as nv, nc.Block() as block:
                @block.tensor
                def _(pe):
                    with pe.Fori(0, SORTS) as s:
                        pe.wait_ge(kept_ready, s + 1)
                        for h in range(0, SG, HALF):
                            nc.tensor.matmul(cum[:, h:h + HALF, :], upper[:], keepT[:, h:h + HALF, :], start=True, stop=True)
                        for g in range(SG):
                            mm = nc.tensor.matmul(nv[:, g:g + 1], keepT[:, g, :], onesb[:, 0:1], start=True, stop=True)
                        mm.then_inc(summed, 1)

                @block.vector
                def _(dve):
                    V = nc.vector
                    with dve.Fori(0, SORTS) as s:
                        turn = bass.ds(s * SG, SG)
                        V.tensor_scalar(keepT, AT[:, turn, :], 0.0, None, ALU.is_gt).then_inc(kept_ready, 1)
                        dve.wait_ge(kept_ready, s + 1)
                        dve.wait_ge(summed, s + 1)
                        V.tensor_tensor(POS[:, turn, :], cum[:], keepT, ALU.mult).then_inc(placed, 1)
                        V.tensor_copy(count[:, turn], nv[:]).then_inc(placed, 1)
                        dve.wait_ge(placed, s * 2 + 2)

        centred, squared, var_ready, root_ready, mean_ready, h_ready, norm_step = [
            ctx.enter_context(nc.semaphore(n)) for n in ("centred", "squared", "var", "root", "mean", "h", "norm_step")]

        def stage_norm(n, parts):
            used[0] = 0
            CH = B // 4
            if parts:
                hi_ready, r1_ready, mid_ready, r2_ready = [sem("norm_" + w) for w in ("hi", "r1", "mid", "r2")]
            mean, var, root, rstd = [take([N, B]) for _ in range(4)]
            eps = take([N, 1])
            xc, sq = take([N, B, C]), take([N, B, C])
            rest = take([N, B, C])
            bc = [N, CH, C]
            with nc.Block() as block:
                @block.gpsimd
                def _(pool):
                    with pool.Fori(0, 4) as t:
                        ch = bass.ds(t * CH, CH)
                        pool.wait_ge(mean_ready, t + 5 * n + 2)
                        nc.gpsimd.tensor_tensor(xc[:, ch], X[:, ch], mean[:, ch].unsqueeze(2).broadcast_to(bc),
                                                ALU.add).then_inc(centred, 1)
                    if parts:
                        with pool.Fori(0, 4) as t:
                            ch = bass.ds(t * CH, CH)
                            pool.wait_ge(hi_ready, t + 1)
                            nc.gpsimd.tensor_tensor(rest[:, ch], H[:, ch], PARTS[:, 0, ch], ALU.subtract).then_inc(r1_ready, 1)
                        with pool.Fori(0, 4) as t:
                            ch = bass.ds(t * CH, CH)
                            pool.wait_ge(mid_ready, t + 1)
                            nc.gpsimd.tensor_tensor(xc[:, ch], rest[:, ch], PARTS[:, 1, ch], ALU.subtract).then_inc(r2_ready, 1)

                @block.scalar
                def _(act):
                    with act.Fori(0, 4) as t:
                        ch = bass.ds(t * CH, CH)
                        act.wait_ge(centred, t + 4 * n + 1)
                        nc.scalar.activation(sq[:, ch], xc[:, ch], ACT.Square).then_inc(squared, 1)
                    act.wait_ge(var_ready, 4 * n + 4)
                    act.wait_ge(mean_ready, 5 * n + 1)
                    nc.scalar.activation(root, var, ACT.Sqrt, bias=eps, scale=1.0 / C).then_inc(root_ready, 1)
                    if parts:
                        with act.Fori(0, 4) as t:
                            ch = bass.ds(t * CH, CH)
                            act.wait_ge(h_ready, t + 4 * n + 1)
                            nc.scalar.copy(PARTS[:, 0, ch], H[:, ch]).then_inc(hi_ready, 1)
                        with act.Fori(0, 4) as t:
                            ch = bass.ds(t * CH, CH)
                            act.wait_ge(r1_ready, t + 1)
                            nc.scalar.copy(PARTS[:, 1, ch], rest[:, ch]).then_inc(mid_ready, 1)
                        with act.Fori(0, 4) as t:
                            ch = bass.ds(t * CH, CH)
                            act.wait_ge(r2_ready, t + 1)
                            nc.scalar.copy(PARTS[:, 2, ch], xc[:, ch])

                @block.vector
                def _(dve):
                    nc.vector.memset(eps, LN_EPS).then_inc(mean_ready, 1)
                    with dve.Fori(0, 4) as t:
                        ch = bass.ds(t * CH, CH)
                        nc.vector.tensor_reduce(root[:, ch], X[:, ch], AX, ALU.add).then_inc(norm_step, 1)
                        dve.wait_ge(norm_step, t + 5 * n + 1)
                        nc.vector.tensor_scalar(mean[:, ch], root[:, ch], -1.0 / C, None, ALU.mult).then_inc(mean_ready, 1)
                    with dve.Fori(0, 4) as t:
                        ch = bass.ds(t * CH, CH)
                        dve.wait_ge(squared, t + 4 * n + 1)
                        nc.vector.tensor_reduce(var[:, ch], sq[:, ch], AX, ALU.add).then_inc(var_ready, 1)
                    dve.wait_ge(root_ready, n + 1)
                    nc.vector.reciprocal(rstd, root).then_inc(norm_step, 1)
                    dve.wait_ge(norm_step, 5 * n + 5)
                    with dve.Fori(0, 4) as t:
                        ch = bass.ds(t * CH, CH)
                        nc.vector.scalar_tensor_tensor(out=H[:, ch], in0=xc[:, ch], scalar=0.0,
                                                       in1=rstd[:, ch].unsqueeze(2).broadcast_to(bc),
                                                       op0=ALU.max, op1=ALU.mult).then_inc(h_ready, 1)

        def hot_slot(dve, s, r, hot, hot_ready, slot_ready):
            k = r % RING
            if r >= RING:
                dve.wait_ge(slot_ready[k], s * (SLOTS // RING) + r // RING)
            nc.vector.tensor_scalar(hot[k], POS[:, bass.ds(s * SG, SG), :].rearrange("p g i -> p (g i)"), float(r + 1),
                                    None, ALU.is_equal).then_inc(hot_ready[k], 1)

        def gather_slot(pe, s, r, hot, hot_ready, slot_ready, pad, pad_sign, piece):
            k = r % RING
            pe.wait_ge(hot_ready[k], s * (SLOTS // RING) + r // RING + 1)
            nc.tensor.matmul(piece, pad_sign, pad[:, r, bass.ds(s * SG, SG)].unsqueeze(2).broadcast_to([N, SG, C]),
                             start=True, stop=True)
            for g in range(SG):
                for part in range(3):
                    mm = nc.tensor.matmul(piece[:, g, :], hot[k][:, g * N:(g + 1) * N],
                                          PARTS[:, part, bass.ds(s * SG + g, 1), :].rearrange("p a c -> p (a c)"),
                                          start=False, stop=True, skip_group_check=True)
            mm.then_inc(slot_ready[k], 1)

        def absent_slots(eng, step, pad):
            for r in range(SLOTS):
                step(eng.tensor_scalar(pad[:, r, :], count[:], float(r), BIG, ALU.is_le, ALU.mult))

        def stage_order():
            prepared, diag_ready, keyed, above_ready, ranked, placed_ready, moved, kept_ready, counted, placed = [
                sem("ord_" + n) for n in ("prepared", "diag", "keyed", "above", "ranked", "hot", "moved", "kept",
                                          "counted", "placed")]
            diag, above, P, keep = [take([N, SG, N], BF16) for _ in range(4)]
            key, number, back, order = take([N, B]), take([N, 1]), take([N, 1]), take([N, N])
            times, last = take([N, N], BF16), take([N, N], BF16)
            at, dist, size, hats = take([N, 1]), take([N, ORDERS]), take([N, ORDERS]), take([N, ORDERS])
            HALF = 4
            bc = [N, SG, N]
            with ExitStack() as ps:
                kb = ps.enter_context(nc.psum_tensor("ord_kb", [N, SG, N], F32))
                rb = ps.enter_context(nc.psum_tensor("ord_rb", [N, SG, N], F32))
                kp = ps.enter_context(nc.psum_tensor("ord_kp", [N, SG, N], F32))
                rc = ps.enter_context(nc.psum_tensor("ord_rc", [N, SG], F32))
                block = ps.enter_context(nc.Block())

                @block.gpsimd
                def _(pool):
                    step = Steps(pool, prepared)
                    for t, pattern, base, mult in ((number, [[0, 1]], 0, 1), (back, [[0, 1]], N - 1, -1),
                                                   (order, [[1, N]], 0, 0)):
                        step(nc.gpsimd.iota(t, pattern=pattern, base=base, channel_multiplier=mult,
                                            allow_small_or_imprecise_dtypes=True))
                    step(nc.gpsimd.memset(times, float(N)))
                    step(nc.gpsimd.memset(minus_big, -BIG))
                    step(nc.gpsimd.memset(big_share, BIG / N))
                    with pool.Fori(0, SORTS) as s:
                        pool.wait_ge(keyed, s + 1)
                        nc.gpsimd.tensor_tensor(diag, identb[:].unsqueeze(1).broadcast_to(bc),
                                                count[:, bass.ds(s * SG, SG)].unsqueeze(2).broadcast_to(bc),
                                                ALU.mult).then_inc(diag_ready, 1)

                @block.tensor
                def _(pe):
                    starts_free(pe, keyed)
                    pe.wait_ge(prepared, 8)
                    with pe.Fori(0, SORTS) as s:
                        pe.wait_ge(diag_ready, s + 1)
                        pe.wait_ge(placed, s * 2 + 1)
                        for h in range(0, SG, HALF):
                            nc.tensor.matmul(kb[:, h:h + HALF, :], times, diag[:, h:h + HALF, :], start=True, stop=False)
                            mm = nc.tensor.matmul(kb[:, h:h + HALF, :], onesb[:], last.unsqueeze(1).broadcast_to([N, HALF, N]),
                                                  start=False, stop=True)
                        mm.then_inc(keyed, 1)
                        pe.wait_ge(above_ready, s + 1)
                        for h in range(0, SG, HALF):
                            nc.tensor.matmul(rb[:, h:h + HALF, :], onesb[:], above[:, h:h + HALF, :], start=True, stop=True)
                        for g in range(SG):
                            mm = nc.tensor.matmul(rc[:, g:g + 1], above[:, g, :], onesb[:, 0:1], start=True, stop=True)
                        mm.then_inc(ranked, 1)
                        pe.wait_ge(placed_ready, s * 3 + 3)
                        pe.wait_ge(kept_ready, s + 1)
                        for g in range(SG):
                            mm = nc.tensor.matmul(kp[:, g, :], POS[:, bass.ds(s * SG + g, 1), :].rearrange("p a i -> p (a i)"),
                                                  P[:, g, :], start=True, stop=True)
                        mm.then_inc(moved, 1)
                        pe.wait_ge(kept_ready, s + 2)
                        for h in range(0, SG, HALF):
                            nc.tensor.matmul(kb[:, h:h + HALF, :], upper[:], keep[:, h:h + HALF, :], start=True, stop=True)
                            mm = nc.tensor.matmul(rb[:, h:h + HALF, :], onesb[:], keep[:, h:h + HALF, :], start=True, stop=True)
                        mm.then_inc(counted, 1)

                @block.scalar
                def _(act):
                    starts_free(act, kept_ready)
                    with act.Fori(0, SORTS) as s:
                        act.wait_ge(moved, s + 1)
                        act.wait_ge(placed, s * 2 + 1)
                        nc.scalar.copy(keep, kp[:]).then_inc(kept_ready, 1)

                @block.vector
                def _(dve):
                    V = nc.vector
                    starts_free(dve, placed)
                    dve.wait_ge(prepared, 6)
                    V.tensor_scalar(last, identb[:], back, None, ALU.mult).then_inc(prepared, 1)
                    V.tensor_scalar(key, count[:], float(N), back, ALU.mult, ALU.add).then_inc(prepared, 1)
                    dve.wait_ge(prepared, 8)
                    with dve.Fori(0, SORTS) as s:
                        turn = bass.ds(s * SG, SG)
                        dve.wait_ge(keyed, s + 2)
                        V.tensor_tensor(above, kb[:], key[:, turn].unsqueeze(2).broadcast_to(bc), ALU.is_lt).then_inc(above_ready, 1)
                        dve.wait_ge(ranked, s + 1)
                        V.tensor_tensor(P, order.unsqueeze(1).broadcast_to(bc), rc[:].unsqueeze(2).broadcast_to(bc),
                                        ALU.is_equal).then_inc(placed_ready, 1)
                        V.tensor_copy(RANK[:, turn], rc[:]).then_inc(placed_ready, 1)
                        V.tensor_scalar(PT[:, turn, :], rb[:], number, None, ALU.is_equal).then_inc(placed_ready, 1)
                        dve.wait_ge(counted, s + 1)
                        V.tensor_tensor(POS[:, turn, :], kb[:], keep, ALU.mult).then_inc(placed, 1)
                        V.tensor_scalar(COUNT1[:, bass.ds(s * (SG // 2), SG // 2)].rearrange("n p i e -> n p e i"),
                                        rb[:].rearrange("n (p e) i -> n p e i", e=2), number, None,
                                        ALU.is_equal).then_inc(placed, 1)
                    step = Steps(dve, prepared)
                    step.k = 8
                    for n, (tau, w) in enumerate(TAUS):
                        step(V.tensor_scalar(at, number, tau, -tau, ALU.mult, ALU.add))
                        step.wait()
                        step(V.tensor_scalar(dist, slot_no[:, 0:ORDERS], at, None, ALU.subtract))
                        step.wait()
                        step(V.scalar_tensor_tensor(out=size, in0=dist, scalar=-1.0, in1=dist, op0=ALU.mult, op1=ALU.max))
                        step.wait()
                        step(V.tensor_scalar(dist, size, -w, w, ALU.mult, ALU.add))
                        step.wait()
                        if n == 0:
                            step(V.tensor_scalar(hats, dist, 0.0, None, ALU.max))
                        else:
                            step(V.scalar_tensor_tensor(out=hats, in0=dist, scalar=0.0, in1=hats, op0=ALU.max, op1=ALU.add))
                        step.wait()
                    step(V.memset(WEIGHTS, 0.0))
                    step.wait()
                    step(V.tensor_copy(WEIGHTS[:, :, C:2 * C], hats.unsqueeze(2).broadcast_to([N, ORDERS, C])))

        def stage_quantiles(tier, first, width, slots, chunk, pairs, piece_pairs):
            tag = f"q{tier}_"
            used_orders = -(-3 * (slots - 1) // 4) + 1
            layers = live_halves(layered(SELECTION[slots]), range(used_orders))
            CHUNKS, BLOCKS = slots // chunk, pairs // piece_pairs
            TURNS, GRAPHS, COLS = B // (2 * pairs), 2 * pairs, pairs * width
            assert CHUNKS * chunk == slots and BLOCKS % PIECES == 0 and piece_pairs * chunk * width <= 512
            USES = CHUNKS * BLOCKS // PIECES
            hot_ready = [sem(f"{tag}hot_ready{h}") for h in range(CHUNKS)]
            gathered = [sem(f"{tag}gathered{k}") for k in range(PIECES)]
            copied = [sem(f"{tag}copied{k}") for k in range(PIECES)]
            sorting, first_read, spread, kept = [sem(tag + n) for n in ("sorting", "first_read", "spread", "kept")]
            weighted, summed, agg_copied = sem(tag + "weighted"), sem(tag + "summed"), sem(tag + "agg_copied")
            raw = take([N, slots, COLS])
            wires = take([N, slots + 2, COLS])
            hot = [take([N, GRAPHS, chunk, width], BF16) for _ in range(CHUNKS)]
            parts = take([N, 3, GRAPHS, C], BF16)
            om = take([N, used_orders, COLS], BF16)
            parts_ready = sem(tag + "parts_ready")

            HOME = [None] * slots
            plan, free = [], list(range(slots + 2))
            for layer in layers:
                rows = []
                for a, b, want_min, want_max in layer:
                    src = [("raw", w) if HOME[w] is None else ("wire", HOME[w]) for w in (a, b)]
                    low = free.pop(0) if want_min else None
                    high = None
                    if want_max:
                        high = free.pop(0) if HOME[b] is None else HOME[b]
                    elif HOME[b] is not None:
                        free.append(HOME[b])
                    if HOME[a] is not None:
                        free.append(HOME[a])
                    rows.append((src[0], src[1], low, high))
                    HOME[a], HOME[b] = low, high
                plan.append(rows)
            HALVES = sum((lo is not None) + (hi is not None) for rows in plan for _, _, lo, hi in rows)
            first_last = max(n for n, rows in enumerate(plan) for r in rows if "raw" in (r[0][0], r[1][0]))
            writes = [w for rows in plan for _, _, low, high in rows for w in (low, high) if w is not None]
            sum_order = sorted(range(used_orders), key=lambda m: writes.index(HOME[m]))

            with ExitStack() as ps:
                gat = [ps.enter_context(nc.psum_tensor(f"{tag}gat{b}", [N, piece_pairs, chunk, width], F32)) for b in range(PIECES)]
                omp = [ps.enter_context(nc.psum_tensor(f"{tag}om{b}", [N, pairs, width], F32)) for b in range(2)]
                agg = ps.enter_context(nc.psum_tensor(tag + "agg", [N, COLS], F32))
                block = ps.enter_context(nc.Block())

                @block.gpsimd
                def _(pool):
                    def load_parts(s):
                        for part in range(3):
                            nc.gpsimd.tensor_copy(parts[:, part], PARTS[:, part, bass.ds(s * GRAPHS, GRAPHS), :]).then_inc(parts_ready, 1)
                    load_parts(0)
                    with pool.Fori(0, TURNS - 1) as s:
                        for k in range(PIECES):
                            pool.wait_ge(gathered[k], (s + 1) * USES)
                        load_parts(s + 1)

                @block.tensor
                def _(pe):
                    def gather_turn(s):
                        pe.wait_ge(parts_ready, s * 3 + 3)
                        for h in range(CHUNKS):
                            pe.wait_ge(hot_ready[h], (s + 1) * chunk)
                            for b in range(BLOCKS):
                                n = h * BLOCKS + b
                                k = n % PIECES
                                pe.wait_ge(copied[k], s * USES + n // PIECES + 1)
                                nc.tensor.matmul(gat[k][:].rearrange("n p k w -> n (p k w)"), onesb[:],
                                                 big_share.broadcast_to([N, piece_pairs * chunk * width]),
                                                 start=True, stop=True)
                                for p in range(piece_pairs):
                                    for odd in range(2):
                                        g = (b * piece_pairs + p) * 2 + odd
                                        marks = hot[h][:, g, :, :].rearrange("n k w -> n (k w)")
                                        to = gat[k][odd * C:odd * C + C, p, :, :].rearrange("n k w -> n (k w)")
                                        nc.tensor.matmul(to, minus_big, marks, start=False, stop=True, skip_group_check=True)
                                        for part in range(3):
                                            mm = nc.tensor.matmul(
                                                to, parts[:, part, g, :], marks, start=False, stop=True, skip_group_check=True)
                                mm.then_inc(gathered[k], 1)

                    def spread_weights(s):
                        nodes = COUNT1[:, bass.ds(s * pairs, pairs), first:first + width, :]
                        for m in range(used_orders):
                            pe.wait_ge(kept, s * used_orders + max(m - 1, 0) + 1)
                            for odd in range(2):
                                mm = nc.tensor.matmul(omp[m % 2][:], WEIGHTS[:, m, (1 - odd) * C:(3 - odd) * C],
                                                      nodes[:, :, :, odd], start=(odd == 0), stop=(odd == 1))
                            mm.then_inc(spread, 1)

                    def sum_turn(s):
                        pe.wait_ge(agg_copied, s + 1)
                        for n, m in enumerate(sum_order):
                            pe.wait_ge(weighted, s * used_orders + n + 2)
                            nc.tensor.matmul(agg[:], identf[:], wires[:, HOME[m], :], start=(n == 0),
                                             stop=(n == used_orders - 1)).then_inc(summed, 1)

                    pe.sem_inc(summed, used_orders)
                    spread_weights(0)
                    gather_turn(0)
                    with pe.Fori(0, TURNS - 1) as s:
                        gather_turn(s + 1)
                        sum_turn(s)
                        spread_weights(s + 1)
                    sum_turn(TURNS - 1)

                @block.scalar
                def _(act):
                    def copy_turn(s):
                        act.wait_ge(first_read, s + 1)
                        for h in range(CHUNKS):
                            for b in range(BLOCKS):
                                n = h * BLOCKS + b
                                k = n % PIECES
                                act.wait_ge(gathered[k], s * USES + n // PIECES + 1)
                                nc.scalar.copy(raw[:, h * chunk:(h + 1) * chunk,
                                                   b * piece_pairs * width:(b + 1) * piece_pairs * width]
                                               .rearrange("n k (p w) -> n p k w", w=width), gat[k][:]).then_inc(copied[k], 1)

                    def keep_weights(s):
                        act.wait_ge(weighted, s * used_orders + 1)
                        for m in range(used_orders):
                            act.wait_ge(spread, s * used_orders + m + 1)
                            nc.scalar.copy(om[:, m, :], omp[m % 2][:].rearrange("n p w -> n (p w)")).then_inc(kept, 1)

                    def store_turn(s):
                        act.wait_ge(summed, (s + 2) * used_orders)
                        nc.scalar.copy(AGG[:, bass.ds(s * pairs, pairs), first:first + width],
                                       agg[:].rearrange("n (p w) -> n p w", w=width)).then_inc(agg_copied, 1)

                    starts_free(act, agg_copied, kept, *copied)
                    keep_weights(0)
                    copy_turn(0)
                    with act.Fori(0, TURNS - 1) as s:
                        copy_turn(s + 1)
                        store_turn(s)
                        keep_weights(s + 1)
                    store_turn(TURNS - 1)

                @block.vector
                def _(dve):
                    def mark(s, r):
                        h = r // chunk
                        nc.vector.tensor_scalar(hot[h][:, :, r % chunk, :],
                                                POS[:, bass.ds(s * GRAPHS, GRAPHS), first:first + width],
                                                float(r + 1), None, ALU.is_equal).then_inc(hot_ready[h], 1)

                    def sort_turn(s, ahead):
                        step = Steps(dve, sorting, HALVES, s)
                        for k in range(PIECES):
                            dve.wait_ge(copied[k], (s + 1) * USES + 1)
                        unwritten = [HOME[m] for m in sum_order]
                        marks = list(range(slots)) if ahead else []
                        for n, rows in enumerate(plan):
                            before = 0
                            for (ka, a), (kb, b), low, high in rows:
                                step.wait(before)
                                before = (low is not None) + (high is not None)
                                va = raw[:, a, :] if ka == "raw" else wires[:, a, :]
                                vb = raw[:, b, :] if kb == "raw" else wires[:, b, :]
                                for w in (low, high):
                                    if w in unwritten:
                                        dve.wait_ge(summed, s * used_orders + used_orders - len(unwritten) + 1)
                                        unwritten.remove(w)
                                if low is not None:
                                    step(nc.vector.tensor_tensor(wires[:, low, :], va, vb, ALU.min))
                                if high is not None:
                                    step(nc.vector.tensor_tensor(wires[:, high, :], va, vb, ALU.max))
                                if n > 0 and marks:
                                    mark(s + 1, marks.pop(0))
                            step.wait()
                            if n == first_last:
                                dve.sem_inc(first_read, 1)
                        for r in marks:
                            mark(s + 1, r)
                        step.end()
                        dve.wait_ge(kept, (s + 1) * used_orders + 1)
                        for m in sum_order:
                            w = wires[:, HOME[m], :]
                            nc.vector.tensor_tensor(w, w, om[:, m, :], ALU.mult).then_inc(weighted, 1)

                    starts_free(dve, first_read, weighted)
                    for r in range(slots):
                        mark(0, r)
                    with dve.Fori(0, TURNS - 1) as s:
                        sort_turn(s, True)
                    sort_turn(TURNS - 1, False)

        def stage_return():
            def turns(name, per=1):
                return Turns(sem("ret_" + name), per)
            staged, turned, copied, returned, added = turns("staged", 2), turns("turned"), turns("copied"), turns("returned"), turns("added")
            a4 = [take([N, 2, N]) for _ in range(2)]
            p4 = [take([N, QG, N]) for _ in range(2)]
            t4 = [take([N, QG, C]) for _ in range(2)]
            with ExitStack() as ps:
                tp = [ps.enter_context(nc.psum_tensor(f"ret_tp{u}", [N, 2, N], F32)) for u in range(2)]
                rp = [ps.enter_context(nc.psum_tensor(f"ret_rp{u}", [N, QG, C], F32)) for u in range(2)]
                block = ps.enter_context(nc.Block())

                @block.gpsimd
                def _(pool):
                    staged.begin(pool)
                    with pool.Fori(0, QUADS // 2) as i:
                        for u in range(2):
                            q = i * 2 + u
                            turned.wait(pool, q, behind=2)
                            nc.gpsimd.tensor_copy(a4[u], AGG[:, bass.ds(q * 2, 2), :]).then_inc(staged.sem, 1)
                            returned.wait(pool, q, behind=2)
                            nc.gpsimd.tensor_copy(p4[u], PT[:, bass.ds(q * QG, QG), :]).then_inc(staged.sem, 1)

                @block.tensor
                def _(pe):
                    def turn(i, u):
                        q = i * 2 + u
                        staged.wait(pe, q, 1)
                        copied.wait(pe, q, behind=2)
                        for pair in range(2):
                            mm = nc.tensor.transpose(tp[u][:, pair, :], a4[u][:, pair, :], identf[:])
                        mm.then_inc(turned.sem, 1)

                    def put_back(i, u):
                        q = i * 2 + u
                        staged.wait(pe, q)
                        copied.wait(pe, q)
                        added.wait(pe, q, behind=2)
                        for g in range(QG):
                            mm = nc.tensor.matmul(rp[u][:, g, :], p4[u][:, g, :], t4[u][:, g, :], start=True, stop=True)
                        mm.then_inc(returned.sem, 1)

                    turned.begin(pe)
                    returned.begin(pe)
                    with pe.Fori(0, QUADS // 2) as i:
                        turn(i, 0)
                        turn(i, 1)
                        put_back(i, 0)
                        put_back(i, 1)

                @block.scalar
                def _(act):
                    copied.begin(act)
                    with act.Fori(0, QUADS // 2) as i:
                        for u in range(2):
                            q = i * 2 + u
                            turned.wait(act, q)
                            returned.wait(act, q, behind=2)
                            nc.scalar.copy(t4[u].rearrange("n g c -> n (g c)"),
                                           tp[u][:].rearrange("n p c -> n (p c)")).then_inc(copied.sem, 1)

                @block.vector
                def _(dve):
                    added.begin(dve)
                    with dve.Fori(0, QUADS // 2) as i:
                        for u in range(2):
                            q = i * 2 + u
                            hs = H[:, bass.ds(q * QG, QG), :]
                            returned.wait(dve, q)
                            nc.vector.tensor_tensor(hs, hs, rp[u][:], ALU.add).then_inc(added.sem, 1)

        def stage_first():
            nonlocal PT, COUNT1, AGG, RANK, WEIGHTS, minus_big, big_share
            used[0] = 0
            PT, AGG = take([N, B, N], BF16), take([N, B // 2, N])
            COUNT1 = AGG.rearrange("n p i -> n (p i)").bitcast(BF16).rearrange("n (p i e) -> n p i e", i=N, e=2)
            RANK, WEIGHTS = take([N, B]), take([N, ORDERS, 3 * C], BF16)
            minus_big, big_share = take([N, C], BF16), take([N, 2], BF16)[:, 0:1]
            base = used[0]
            stages = [stage_order] + [lambda t=t, tier=tier: stage_quantiles(t, *tier) for t, tier in enumerate(TIERS)]
            for stage in stages + [stage_return, lambda: stage_general("qg_", True)]:
                used[0] = base
                stage()

        PT = COUNT1 = AGG = RANK = WEIGHTS = minus_big = big_share = None

        def stage_general(tag, quantiles):
            flag_step, flagged = sem(tag + "flag_step"), sem(tag + "flagged")
            value_ready, spread, pos_turned = sem(tag + "value_ready"), sem(tag + "spread"), sem(tag + "pos_turned")
            chain, rounds = sem(tag + "chain"), sem(tag + "rounds")
            room_a, room_b = take([N, N, C]), take([N, N, C])
            value, part = take([N, C]), take([N, C])
            absent, order = take([N, N]), take([N, N])
            cnt, top = take([N, 1]), take([N, 1])
            excess, late, turn_back = take([N, B]), take([N, B]), take([N, N])
            part_ready, returned = sem(tag + "part_ready"), sem(tag + "returned")
            FLAG = 8 if quantiles else 3
            over, flag = take([N, 2], BF16), take([N, 1], I32)
            at, dist, hats = take([N, 1]), take([N, N]), take([N, N])
            scratch = nc.dram_tensor(tag + "scratch", [N, C], F32, kind="Internal").ap()
            PAIRS = N // 2
            with ExitStack() as ps:
                fp = ps.enter_context(nc.psum_tensor(tag + "fp", [N, 2], F32))
                pt = ps.enter_context(nc.psum_tensor(tag + "pt", [N, N], F32))
                back = ps.enter_context(nc.psum_tensor(tag + "back", [N, C], F32))
                block = ps.enter_context(nc.Block())

                @block.gpsimd
                def _(pool):
                    nc.gpsimd.iota(order, pattern=[[1, N]], base=0, channel_multiplier=0,
                                   allow_small_or_imprecise_dtypes=True).then_inc(value_ready, 1)

                @block.sync
                def _(sp):
                    sp.wait_ge(flag_step, FLAG + 1)
                    crowded = sp.value_load(flag[0:1, 0:1])
                    with sp.If(crowded > 0):
                        with sp.Fori(0, B) as g:
                            sp.wait_ge(value_ready, g + 2)
                            sp.dma_start(scratch, value).then_inc(spread, 16)
                            sp.wait_ge(spread, g * 32 + 16)
                            sp.dma_start(room_a.rearrange("p j c -> p (j c)"),
                                         scratch.rearrange("j c -> (j c)").partition_broadcast(N)).then_inc(spread, 16)

                @block.tensor
                def _(pe):
                    pe.wait_ge(flag_step, FLAG)
                    nc.tensor.matmul(fp[0:1, 0:1], over[:, 0:1], onesb[:, 0:1], start=True, stop=True).then_inc(flagged, 1)
                    pe.wait_ge(flag_step, FLAG + 1)
                    crowded = pe.value_load(flag[0:1, 0:1])
                    with pe.If(crowded > 0):
                        with pe.Fori(0, B) as g:
                            pe.wait_ge(value_ready, g + 2)
                            nc.tensor.matmul(pt[:], POS[:, bass.ds(g, 1), :].rearrange("p a i -> p (a i)"), identb[:],
                                             start=True, stop=True).then_inc(pos_turned, 1)
                            if quantiles:
                                pe.wait_ge(part_ready, g + 1)
                                nc.tensor.matmul(back[:], turn_back, part, start=True, stop=True).then_inc(returned, 1)

                @block.vector
                def _(dve):
                    V = nc.vector
                    fs = Steps(dve, flag_step)
                    fs(V.memset(over, 0.0))
                    if quantiles:
                        (start2, _, slots2, *_), (start1, _, slots1, *_), (_, _, slots0, *_) = TIERS
                        fs(V.tensor_scalar(excess, count[:], float(slots0), None, ALU.subtract))
                        for start, fewer in ((start1, slots0 - slots1), (start2, slots1 - slots2)):
                            fs(V.tensor_scalar(late, RANK, start - 0.5, float(fewer), ALU.is_gt, ALU.mult))
                            fs.wait()
                            fs(V.tensor_tensor(excess, excess, late, ALU.add))
                            fs.wait()
                        fs(V.tensor_reduce(top, excess, AX, ALU.max))
                    else:
                        fs(V.tensor_reduce(top, count[:], AX, ALU.max))
                    fs.wait()
                    fs(V.tensor_scalar(over[:, 0:1], top, 0.0 if quantiles else float(SLOTS), None, ALU.is_gt))
                    dve.wait_ge(flagged, 1)
                    fs(V.tensor_copy(flag[0:1, :], fp[0:1, 0:1]))
                    fs.wait()
                    crowded = dve.value_load(flag[0:1, 0:1])
                    with dve.If(crowded > 0):
                        dve.wait_ge(value_ready, 1)
                        with dve.Fori(0, B) as g:
                            step = Steps(dve, chain, 27 if quantiles else 8, g)

                            def do(ins):
                                step(ins)
                                step.wait()

                            def graph(t):
                                return t[:, bass.ds(g, 1), :].rearrange("p a c -> p (a c)")
                            do(V.tensor_tensor(part, PARTS[:, 0, bass.ds(g, 1), :].rearrange("p a c -> p (a c)"),
                                               PARTS[:, 1, bass.ds(g, 1), :].rearrange("p a c -> p (a c)"), ALU.add))
                            V.tensor_tensor(value, part, PARTS[:, 2, bass.ds(g, 1), :].rearrange("p a c -> p (a c)"),
                                            ALU.add).then_inc(value_ready, 1)
                            dve.wait_ge(value_ready, g + 2)
                            dve.wait_ge(pos_turned, g + 1)
                            do(V.tensor_scalar(absent, pt[:], 0.0, BIG, ALU.is_equal, ALU.mult))
                            dve.wait_ge(spread, g * 32 + 32)
                            padding = absent.unsqueeze(2).broadcast_to([N, N, C])
                            if not quantiles:
                                do(V.tensor_tensor(room_b, room_a, padding, ALU.subtract))
                                do(V.tensor_reduce(value, room_b.rearrange("p j c -> p c j"), AX, ALU.max))
                                do(V.tensor_copy(graph(MAXQ), value))
                                do(V.tensor_tensor(room_b, room_a, padding, ALU.add))
                                do(V.tensor_reduce(value, room_b.rearrange("p j c -> p c j"), AX, ALU.min))
                                do(V.tensor_copy(graph(MINQ), value))
                                step.end()
                            else:
                                step(V.tensor_scalar(dist, pt[:], 0.0, None, ALU.is_gt))
                                step(V.tensor_copy(turn_back, graph(PT)))
                                do(V.tensor_tensor(room_a, room_a, padding, ALU.max))
                                step(V.tensor_reduce(cnt, dist, AX, ALU.add))
                                with dve.Fori(0, PAIRS) as r:
                                    ev, od = [t.rearrange("p (k e) c -> p k e c", e=2) for t in (room_a, room_b)]
                                    V.tensor_tensor(od[:, :, 0, :], ev[:, :, 0, :], ev[:, :, 1, :], ALU.min).then_inc(rounds, 1)
                                    V.tensor_tensor(od[:, :, 1, :], ev[:, :, 0, :], ev[:, :, 1, :], ALU.max).then_inc(rounds, 1)
                                    dve.wait_ge(rounds, g * (PAIRS * 6) + r * 6 + 2)
                                    up, down = room_b[:, 1:N - 1].rearrange("p (k e) c -> p k e c", e=2), room_a[:, 1:N - 1].rearrange("p (k e) c -> p k e c", e=2)
                                    V.tensor_tensor(down[:, :, 0, :], up[:, :, 0, :], up[:, :, 1, :], ALU.min).then_inc(rounds, 1)
                                    V.tensor_tensor(down[:, :, 1, :], up[:, :, 0, :], up[:, :, 1, :], ALU.max).then_inc(rounds, 1)
                                    V.tensor_copy(room_a[:, 0, :], room_b[:, 0, :]).then_inc(rounds, 1)
                                    V.tensor_copy(room_a[:, N - 1, :], room_b[:, N - 1, :]).then_inc(rounds, 1)
                                    dve.wait_ge(rounds, g * (PAIRS * 6) + r * 6 + 6)
                                step.wait()
                                for n, (tau, w) in enumerate(TAUS):
                                    do(V.tensor_scalar(at, cnt, -tau, tau, ALU.mult, ALU.add))
                                    do(V.tensor_scalar(dist, order, at, None, ALU.add))
                                    do(V.scalar_tensor_tensor(out=absent, in0=dist, scalar=-1.0, in1=dist, op0=ALU.mult, op1=ALU.max))
                                    do(V.tensor_scalar(dist, absent, -w, w, ALU.mult, ALU.add))
                                    do(V.tensor_scalar(dist, dist, 0.0, None, ALU.max))
                                    if n == 0:
                                        do(V.tensor_copy(hats, dist))
                                    else:
                                        do(V.tensor_tensor(hats, hats, dist, ALU.add))
                                do(V.tensor_tensor(room_a, room_a, hats.unsqueeze(2).broadcast_to([N, N, C]), ALU.mult))
                                V.tensor_reduce(part, room_a.rearrange("p j c -> p c j"), AX, ALU.add).then_inc(part_ready, 1)
                                dve.wait_ge(returned, g + 1)
                                do(V.tensor_tensor(value, value, back[:], ALU.add))
                                do(V.tensor_copy(graph(H), value))
                                step.end()

        def stage_mlp():
            used[0] = 0
            staged, turned, out_ready, hid_done, hid_ready, y_done, stepped, masked = [sem("mlp_" + n) for n in (
                "staged", "turned", "out_ready", "hid_done", "hid_ready", "y_done", "stepped", "masked")]
            h8, oT, hid, ym = take([N, SG, C]), take([N, SG // 2, N]), take([N, SG // 2, 2, N]), take([N, SG, C])
            with ExitStack() as ps:
                tp = ps.enter_context(nc.psum_tensor("mlp_tp", [N, SG // 2, N], F32))
                hp = ps.enter_context(nc.psum_tensor("mlp_hp", [N, 2, SG, N], F32))
                yp = ps.enter_context(nc.psum_tensor("mlp_yp", [N, SG, C], F32))
                block = ps.enter_context(nc.Block())

                @block.gpsimd
                def _(pool):
                    with pool.Fori(0, SORTS) as s:
                        pool.wait_ge(turned, s + 1)
                        nc.gpsimd.tensor_copy(h8, H[:, bass.ds(s * SG, SG), :]).then_inc(staged, 1)

                @block.tensor
                def _(pe):
                    starts_free(pe, turned, y_done)
                    with pe.Fori(0, SORTS) as s:
                        pe.wait_ge(staged, s + 1)
                        pe.wait_ge(out_ready, s + 1)
                        for pair in range(SG // 2):
                            mm = nc.tensor.transpose(tp[:, pair, :], h8[:, 2 * pair:2 * pair + 2, :].rearrange("p g c -> p (g c)"),
                                                     identf[:])
                        mm.then_inc(turned, 1)
                        pe.wait_ge(out_ready, s + 2)
                        pe.wait_ge(hid_ready, s * 2 + 1)
                        for odd in range(2):
                            side = slice(odd * C, odd * C + C)
                            mm = nc.tensor.matmul(hp[:, odd, 0:SG // 2, :], w1[side, :], oT[side], start=True, stop=True)
                        mm.then_inc(hid_done, 1)
                        pe.wait_ge(hid_ready, s * 2 + 3)
                        pe.wait_ge(masked, s + 1)
                        for g in range(SG):
                            nc.tensor.matmul(yp[:, g, :], hid[:, g // 2, g % 2, :], w2[:], start=True, stop=False)
                            mm = nc.tensor.matmul(yp[:, g, :], onesf[:], b2[:], start=False, stop=True)
                        mm.then_inc(y_done, 1)

                @block.scalar
                def _(act):
                    starts_free(act, out_ready, hid_ready)
                    with act.Fori(0, SORTS) as s:
                        act.wait_ge(turned, s + 2)
                        nc.scalar.copy(oT, tp[:]).then_inc(out_ready, 1)
                        act.wait_ge(hid_done, s + 1)
                        act.wait_ge(y_done, s + 1)
                        for odd in range(2):
                            nc.scalar.activation(hid[:, :, odd, :], hp[:, odd, 0:SG // 2, :], ACT.Relu,
                                                 bias=b1[:]).then_inc(hid_ready, 1)

                @block.vector
                def _(dve):
                    starts_free(dve, masked, stepped)
                    with dve.Fori(0, SORTS) as s:
                        turn = bass.ds(s * SG, SG)
                        dve.wait_ge(y_done, s + 2)
                        dve.wait_ge(stepped, s + 1)
                        nc.vector.tensor_tensor(ym, yp[:], mask[:, turn].unsqueeze(2).broadcast_to([N, SG, C]),
                                                ALU.mult).then_inc(masked, 1)
                        dve.wait_ge(masked, s + 2)
                        nc.vector.tensor_tensor(X[:, turn, :], X[:, turn, :], ym, ALU.add).then_inc(stepped, 1)

        def stage_columns():
            loaded, squared, multiplied = sem("att_loaded"), sem("att_squared"), sem("att_multiplied")
            col, act_done = sem("att_col"), sem("att_act")
            sq, hw = take([N, B, C]), take([N, B, C])
            wrow, bcol = take([N, 2 * C]), take([N, 1])
            sd, t1, am, dn, rd, sa, na, rt, zc, zm, lp, lm, at, rz, one = [take([N, B]) for _ in range(15)]
            with nc.Block() as block:
                @block.sync
                def _(sp):
                    sp.dma_start(wrow, W["L1_gnn_att_W"].rearrange("k o -> o k").partition_broadcast(N)
                                 .rearrange("p o k -> p (o k)")).then_inc(loaded, 16)
                    sp.dma_start(bcol, W["L1_gnn_att_b"].partition_broadcast(N)).then_inc(loaded, 16)

                @block.gpsimd
                def _(pool):
                    pool.wait_ge(loaded, 32)
                    nc.gpsimd.tensor_tensor(hw, H[:], wrow[:, 0:C].unsqueeze(1).broadcast_to([N, B, C]),
                                            ALU.mult).then_inc(multiplied, 1)

                @block.scalar
                def _(act):
                    nc.scalar.activation(sq, H[:], ACT.Square).then_inc(squared, 1)
                    act.wait_ge(col, 7)
                    nc.scalar.activation(rt, x2, ACT.Sqrt).then_inc(act_done, 1)
                    act.wait_ge(col, 18)
                    nc.scalar.activation(lp, zm, ACT.Ln, bias=one[:, 0:1]).then_inc(act_done, 1)
                    nc.scalar.activation(lm, zm, ACT.Ln, bias=one[:, 0:1], scale=-1.0).then_inc(act_done, 1)

                @block.vector
                def _(dve):
                    V = nc.vector
                    step = Steps(dve, col)
                    step(V.memset(one, 1.0))
                    dve.wait_ge(squared, 1)
                    step(V.tensor_reduce(x2, sq, AX, ALU.add))
                    dve.wait_ge(multiplied, 1)
                    step(V.tensor_reduce(sd, hw, AX, ALU.add))
                    step.wait()
                    step(V.tensor_tensor(sq, H[:], wrow[:, C:2 * C].unsqueeze(1).broadcast_to([N, B, C]), ALU.mult))
                    step.wait()
                    step(V.tensor_reduce(uw, sq, AX, ALU.add))
                    step(V.tensor_scalar(ox, x2, -1.0, 1.0, ALU.mult, ALU.add))
                    step(V.tensor_scalar(t1, x2, -2.0, 1.0, ALU.mult, ALU.add))
                    step.wait()
                    step(V.tensor_tensor(am, t1, x2, ALU.add))
                    step(V.tensor_tensor(dn, x2, x2, ALU.mult))
                    step(V.tensor_scalar(coef, ox, MIN_NORM, None, ALU.max))
                    step.wait()
                    step(V.tensor_tensor(sa, ox, am, ALU.subtract))
                    step(V.tensor_tensor(dn, dn, t1, ALU.add))
                    step.wait()
                    step(V.tensor_scalar(dn, dn, MIN_NORM, None, ALU.max))
                    step.wait()
                    step(V.reciprocal(rd, dn))
                    step.wait()
                    step(V.tensor_tensor(sa, sa, rd, ALU.mult))
                    step.wait()
                    step(V.scalar_tensor_tensor(out=na, in0=sa, scalar=-1.0, in1=sa, op0=ALU.mult, op1=ALU.max))
                    step.wait()
                    dve.wait_ge(act_done, 1)
                    step(V.tensor_tensor(zc, na, rt, ALU.mult))
                    step.wait()
                    step(V.tensor_scalar(zm, zc, MIN_NORM, ATANH_MAX, ALU.max, ALU.min))
                    step(V.tensor_scalar(na, zc, MIN_NORM, None, ALU.max))
                    step.wait()
                    step(V.reciprocal(rz, na))
                    dve.wait_ge(act_done, 3)
                    step(V.tensor_tensor(at, lp, lm, ALU.subtract))
                    step.wait()
                    step(V.tensor_tensor(at, at, rz, ALU.mult))
                    step(V.tensor_tensor(sa, sa, sd, ALU.mult))
                    step(V.tensor_tensor(cu, coef, uw, ALU.mult))
                    step(V.tensor_tensor(cox, coef, ox, ALU.mult))
                    step.wait()
                    step(V.tensor_tensor(at, at, sa, ALU.mult))
                    step(V.tensor_scalar(ncu, cu, -0.5, None, ALU.mult))
                    step(V.tensor_scalar(hcox, cox, 0.5, None, ALU.mult))
                    step.wait()
                    step(V.tensor_tensor(at, at, coef, ALU.mult))
                    step.wait()
                    step(V.tensor_scalar(selfl, at, 0.5, bcol, ALU.mult, ALU.add))
                    step.wait()

        def stage_pairs():
            def turns(name, per=1):
                return Turns(sem("pr_" + name), per)
            built, turned, copied, formed = turns("built", 10), turns("turned", 4), turns("copied", 4), turns("formed", 3)
            clamped, lns, sums, exps = turns("clamped", 2), turns("lns", 2), turns("sums", 2), turns("exps", 2)
            zmin, lnz, ks, lg, sig = turns("zmin"), turns("lnz", 2), turns("ks", 2), turns("lg", 2), turns("sig", 3)
            weighed, w_turned, w_masked, summed, stored = (turns("weighed"), turns("w_turned"), turns("w_masked"),
                                                           turns("summed"), turns("stored"))
            ready = sem("pr_ready")
            R = C + 3
            left = [[take([N, QG, R + 1]) for _ in range(4)] for _ in range(2)]
            turnT = [[take([N, QG, N]) for _ in range(4)] for _ in range(2)]
            c_, d_, a_, b_, s_, t_ = [[take([N, QG, N]) for _ in range(2)] for _ in range(6)]
            wT = [take([N, QG, N]) for _ in range(2)]
            one = take([N, 1])
            ends = take([N, B, 2])
            HALF = QUADS // 2
            with ExitStack() as ps:
                tp = [ps.enter_context(nc.psum_tensor(f"pr_tp{k}", [N, QG, N], F32)) for k in range(2)]
                gg = [ps.enter_context(nc.psum_tensor(f"pr_gg{k}", [N, QG, N], F32)) for k in range(2)]
                den, d2, wt, so = [ps.enter_context(nc.psum_tensor("pr_" + n, [N, QG, N], F32)) for n in ("den", "d2", "wt", "so")]
                block = ps.enter_context(nc.Block())

                @block.gpsimd
                def _(pool):
                    P = nc.gpsimd

                    def build(q, u):
                        J, D, E, G = left[u]
                        quad = bass.ds(q * QG, QG)

                        def c(t):
                            return t[:, quad].unsqueeze(2)
                        turned.wait(pool, q, behind=2)

                        def put(ins):
                            ins.then_inc(built.sem, 1)
                        put(P.tensor_copy(J[:, :, 0:C], H[:, quad, :]))
                        put(P.tensor_copy(J[:, :, C + 1:C + 2], c(x2)))
                        put(P.tensor_copy(J[:, :, C + 2:C + 3], c(uw)))
                        built.wait(pool, q, 1)
                        put(P.tensor_tensor(G[:, :, 0:C], J[:, :, 0:C], c(cu).broadcast_to([N, QG, C]), ALU.mult))
                        put(P.tensor_scalar(D[:, :, 0:C], J[:, :, 0:C], -2.0, None, ALU.mult))
                        put(P.tensor_copy(D[:, :, C + 1:C + 2], c(x2)))
                        put(P.tensor_scalar(E[:, :, 0:C], J[:, :, 0:C], -2.0, None, ALU.mult))
                        put(P.tensor_copy(E[:, :, C:C + 1], c(x2)))
                        put(P.tensor_copy(G[:, :, C:C + 2], c(ncu).broadcast_to([N, QG, 2])))
                        put(P.tensor_copy(G[:, :, C + 2:C + 3], c(hcox)))

                    def add_logs(q, u):
                        weighed.wait(pool, q, behind=2)
                        lns.wait(pool, q)
                        P.tensor_tensor(s_[u], d_[u], c_[u], ALU.subtract).then_inc(sums.sem, 1)
                        P.tensor_tensor(t_[u], c_[u], d_[u], ALU.add).then_inc(sums.sem, 1)

                    def artanh_over_z(q, u):
                        lnz.wait(pool, q)
                        P.tensor_tensor(a_[u], a_[u], b_[u], ALU.subtract).then_inc(ks.sem, 1)
                        ks.wait(pool, q, 1)
                        P.tensor_tensor(t_[u], a_[u], t_[u], ALU.mult).then_inc(ks.sem, 1)

                    def weigh(q, u):
                        sig.wait(pool, q)
                        P.tensor_tensor(a_[u], s_[u], t_[u], ALU.mult).then_inc(weighed.sem, 1)

                    for t in (built, sums, ks, weighed):
                        t.begin(pool)
                    for t in left[0] + left[1] + [ends]:
                        P.memset(t, 1.0).then_inc(ready, 1)
                    pool.wait_ge(ready, 9)
                    P.tensor_copy(ends[:, :, 1], x2).then_inc(ready, 1)
                    build(0, 0)
                    build(1, 1)

                    def two_quads(q, ahead):
                        if ahead:
                            build(q + 2, 0)
                        add_logs(q, 0)
                        add_logs(q + 1, 1)
                        if ahead:
                            build(q + 3, 1)
                        artanh_over_z(q, 0)
                        artanh_over_z(q + 1, 1)
                        weigh(q, 0)
                        weigh(q + 1, 1)
                    with pool.Fori(0, HALF - 1) as i:
                        two_quads(i * 2, True)
                    two_quads(QUADS - 2, False)

                @block.tensor
                def _(pe):
                    def turn_columns(q, u):
                        built.wait(pe, q)
                        for k, t in enumerate(left[u]):
                            if k < 2:
                                copied.wait(pe, q, 4, behind=1)
                            else:
                                copied.wait(pe, q, k - 1)
                            for g in range(QG):
                                mm = nc.tensor.transpose(tp[k % 2][0:R, g, :], t[:, g, 0:R], identf[:])
                            mm.then_inc(turned.sem, 1)

                    def form(q, u):
                        copied.wait(pe, q)
                        clamped.wait(pe, q, behind=1)
                        for k, (o, K) in enumerate(((den, C + 2), (d2, C + 2), (gg[u], C + 3))):
                            if k == 2:
                                lg.wait(pe, q, 1, behind=2)
                            for g in range(QG):
                                mm = nc.tensor.matmul(o[:, g, :], turnT[u][k + 1][0:K, g, :], turnT[u][0][0:K, g, :],
                                                      start=True, stop=True)
                            mm.then_inc(formed.sem, 1)

                    def turn_weights(q, u):
                        weighed.wait(pe, q)
                        w_masked.wait(pe, q, behind=1)
                        for g in range(QG):
                            mm = nc.tensor.transpose(wt[:, g, :], a_[u][:, g, :], identf[:])
                        mm.then_inc(w_turned.sem, 1)

                    def sum_neighbours(q, u):
                        w_masked.wait(pe, q)
                        stored.wait(pe, q, behind=1)
                        for g in range(QG):
                            graph = bass.ds(q * QG + g, 1)
                            nc.tensor.matmul(so[:, g, 0:C], wT[u][:, g, :], H[:, graph, :].rearrange("p a c -> p (a c)"),
                                             start=True, stop=True)
                            mm = nc.tensor.matmul(so[:, g, C:C + 2], wT[u][:, g, :], ends[:, graph, :].rearrange("p a c -> p (a c)"),
                                                  start=True, stop=True)
                        mm.then_inc(summed.sem, 1)

                    for t in (turned, formed, w_turned, summed):
                        t.begin(pe)
                    pe.wait_ge(ready, 10)
                    turn_columns(0, 0)
                    form(0, 0)
                    turn_columns(1, 1)
                    form(1, 1)

                    def two_quads(q, ahead):
                        if ahead:
                            turn_columns(q + 2, 0)
                            form(q + 2, 0)
                            turn_columns(q + 3, 1)
                        for u in range(2):
                            turn_weights(q + u, u)
                            sum_neighbours(q + u, u)
                        if ahead:
                            form(q + 3, 1)
                    with pe.Fori(0, HALF - 1) as i:
                        two_quads(i * 2, True)
                    two_quads(QUADS - 2, False)

                @block.scalar
                def _(act):
                    A = nc.scalar.activation

                    def copy_columns(q, u, ks=range(4)):
                        for k in ks:
                            turned.wait(act, q, k + 1)
                            if k == 0:
                                formed.wait(act, q, behind=2)
                            nc.scalar.copy(turnT[u][k][0:R], tp[k % 2][0:R]).then_inc(copied.sem, 1)

                    def logs(q, u):
                        clamped.wait(act, q)
                        A(c_[u], c_[u], ACT.Ln).then_inc(lns.sem, 1)
                        A(d_[u], d_[u], ACT.Ln).then_inc(lns.sem, 1)

                    def roots(q, u):
                        sums.wait(act, q)
                        A(s_[u], s_[u], ACT.Exp, scale=0.5).then_inc(exps.sem, 1)
                        A(t_[u], t_[u], ACT.Exp, scale=-0.5).then_inc(exps.sem, 1)

                    def artanh_logs(q, u):
                        zmin.wait(act, q)
                        w_turned.wait(act, q, behind=2)
                        A(a_[u], s_[u], ACT.Ln, bias=one).then_inc(lnz.sem, 1)
                        A(b_[u], s_[u], ACT.Ln, bias=one, scale=-1.0).then_inc(lnz.sem, 1)

                    def sigmoid(q, u):
                        lg.wait(act, q)
                        lnz.wait(act, q)
                        A(s_[u], b_[u], ACT.Exp, scale=-1.0).then_inc(sig.sem, 1)
                        sig.wait(act, q, 1)
                        A(b_[u], s_[u], ACT.Ln, bias=one).then_inc(sig.sem, 1)
                        sig.wait(act, q, 2)
                        A(s_[u], b_[u], ACT.Exp, scale=-1.0).then_inc(sig.sem, 1)

                    def store(q, u):
                        summed.wait(act, q)
                        nc.scalar.mul(SUMS[:, bass.ds(q * QG, QG), :], so[:, :, 0:C + 2], 0.5).then_inc(stored.sem, 1)

                    for t in (copied, lns, exps, lnz, sig, stored):
                        t.begin(act)
                    act.wait_ge(ready, 10)
                    nc.scalar.activation(one, left[0][0][:, 0, C:C + 1], ACT.Copy)
                    nc.scalar.preload_act_table_set("natural_log_exp_and_others")
                    copy_columns(0, 0)
                    copy_columns(1, 1)
                    logs(0, 0)
                    logs(1, 1)

                    def two_quads(q, ahead):
                        if ahead:
                            copy_columns(q + 2, 0, (0, 1))
                        roots(q, 0)
                        roots(q + 1, 1)
                        if ahead:
                            copy_columns(q + 2, 0, (2, 3))
                        artanh_logs(q, 0)
                        artanh_logs(q + 1, 1)
                        if ahead:
                            copy_columns(q + 3, 1, (0, 1))
                        sigmoid(q, 0)
                        if ahead:
                            copy_columns(q + 3, 1, (2, 3))
                            logs(q + 2, 0)
                        sigmoid(q + 1, 1)
                        store(q, 0)
                        store(q + 1, 1)
                        if ahead:
                            logs(q + 3, 1)
                    with act.Fori(0, HALF - 1) as i:
                        two_quads(i * 2, True)
                    two_quads(QUADS - 2, False)

                @block.vector
                def _(dve):
                    V = nc.vector

                    def clamp(q, u):
                        formed.wait(dve, q, 2)
                        sums.wait(dve, q, behind=2)
                        V.tensor_scalar(c_[u], den[:], MIN_NORM, None, ALU.max).then_inc(clamped.sem, 1)
                        V.tensor_scalar(d_[u], d2[:], 1e-18, None, ALU.max).then_inc(clamped.sem, 1)

                    def bound(q, u):
                        exps.wait(dve, q)
                        V.tensor_scalar(s_[u], s_[u], ATANH_MAX, None, ALU.min).then_inc(zmin.sem, 1)

                    def logits(q, u):
                        ks.wait(dve, q)
                        formed.wait(dve, q)
                        V.tensor_tensor(b_[u], gg[u][:], t_[u], ALU.mult).then_inc(lg.sem, 1)
                        lg.wait(dve, q, 1)
                        V.scalar_tensor_tensor(out=b_[u], in0=b_[u], scalar=-40.0,
                                               in1=selfl[:, bass.ds(q * QG, QG)].unsqueeze(2).broadcast_to([N, QG, N]),
                                               op0=ALU.max, op1=ALU.add).then_inc(lg.sem, 1)

                    def mask_weights(q, u):
                        w_turned.wait(dve, q)
                        summed.wait(dve, q, behind=2)
                        V.tensor_tensor(wT[u], wt[:], AT[:, bass.ds(q * QG, QG), :], ALU.mult).then_inc(w_masked.sem, 1)

                    for t in (clamped, zmin, lg, w_masked):
                        t.begin(dve)
                    clamp(0, 0)
                    clamp(1, 1)

                    def two_quads(q, ahead):
                        bound(q, 0)
                        bound(q + 1, 1)
                        if ahead:
                            clamp(q + 2, 0)
                        logits(q, 0)
                        logits(q + 1, 1)
                        mask_weights(q, 0)
                        mask_weights(q + 1, 1)
                        if ahead:
                            clamp(q + 3, 1)
                    with dve.Fori(0, HALF - 1) as i:
                        two_quads(i * 2, True)
                    two_quads(QUADS - 2, False)

        def stage_expmap():
            step_v, pooled, acted = sem("ex_step"), sem("ex_pool"), sem("ex_act")
            cols = [take([N, B]) for _ in range(20)]
            dot, wa, c1, un2, xu, nn, la, th, kk, y2, xy, a1, dn, ca, cb, rn, nr, ff, i1, i2 = cols
            a, u, t, p = [take([N, B, C]) for _ in range(4)]
            S = SUMS[:, :, 0:C]
            bc = [N, B, C]

            def b(c):
                return c.unsqueeze(2).broadcast_to(bc)
            with nc.Block() as block:
                @block.gpsimd
                def _(pool):
                    pool.wait_ge(step_v, 5)
                    nc.gpsimd.tensor_tensor(p, H[:], b(c1), ALU.mult).then_inc(pooled, 1)
                    pool.wait_ge(step_v, 8)
                    nc.gpsimd.tensor_tensor(p, H[:], u, ALU.mult).then_inc(pooled, 1)
                    pool.wait_ge(step_v, 26)
                    nc.gpsimd.tensor_tensor(p, H[:], b(ca), ALU.mult).then_inc(pooled, 1)

                @block.scalar
                def _(act):
                    act.wait_ge(step_v, 8)
                    nc.scalar.activation(a, u, ACT.Square).then_inc(acted, 1)
                    act.wait_ge(step_v, 10)
                    nc.scalar.activation(nn, un2, ACT.Sqrt).then_inc(acted, 1)
                    act.wait_ge(step_v, 13)
                    nc.scalar.activation(th, la, ACT.Tanh).then_inc(acted, 1)
                    act.wait_ge(step_v, 30)
                    nc.scalar.activation(a, u, ACT.Square).then_inc(acted, 1)
                    act.wait_ge(step_v, 32)
                    nc.scalar.activation(nr, rn, ACT.Sqrt).then_inc(acted, 1)

                @block.vector
                def _(dve):
                    V = nc.vector
                    step = Steps(dve, step_v)

                    def do(ins):
                        step(ins)
                        step.wait()
                    do(V.tensor_tensor(a, H[:], S, ALU.mult))
                    do(V.tensor_reduce(dot, a, AX, ALU.add))
                    do(V.scalar_tensor_tensor(out=wa, in0=dot, scalar=-2.0, in1=SUMS[:, :, C], op0=ALU.mult, op1=ALU.add))
                    do(V.tensor_tensor(wa, wa, SUMS[:, :, C + 1], ALU.add))
                    do(V.scalar_tensor_tensor(out=c1, in0=wa, scalar=-1.0, in1=coef, op0=ALU.mult, op1=ALU.mult))
                    do(V.tensor_tensor(t, S, b(cox), ALU.mult))
                    dve.wait_ge(pooled, 1)
                    do(V.tensor_tensor(u, t, p, ALU.add))
                    do(V.tensor_scalar(u, u, CLAMP, -CLAMP, ALU.min, ALU.max))
                    dve.wait_ge(acted, 1)
                    do(V.tensor_reduce(un2, a, AX, ALU.add))
                    do(V.tensor_scalar(un2, un2, MIN_NORM * MIN_NORM, None, ALU.max))
                    dve.wait_ge(acted, 2)
                    do(V.reciprocal(la, coef))
                    do(V.tensor_tensor(la, la, nn, ALU.mult))
                    do(V.reciprocal(i1, nn))
                    dve.wait_ge(pooled, 2)
                    do(V.tensor_reduce(xu, p, AX, ALU.add))
                    dve.wait_ge(acted, 3)
                    do(V.tensor_tensor(kk, th, i1, ALU.mult))
                    do(V.tensor_reduce(y2, a, AX, ALU.add))
                    do(V.tensor_tensor(y2, y2, kk, ALU.mult))
                    do(V.tensor_tensor(y2, y2, kk, ALU.mult))
                    do(V.tensor_tensor(xy, xu, kk, ALU.mult))
                    do(V.tensor_scalar(xy, xy, 2.0, 1.0, ALU.mult, ALU.add))
                    do(V.tensor_tensor(a1, xy, y2, ALU.add))
                    do(V.tensor_tensor(dn, x2, y2, ALU.mult))
                    do(V.tensor_tensor(dn, dn, xy, ALU.add))
                    do(V.tensor_scalar(dn, dn, MIN_NORM, None, ALU.max))
                    do(V.reciprocal(i2, dn))
                    do(V.tensor_tensor(ca, a1, i2, ALU.mult))
                    do(V.tensor_tensor(cb, ox, kk, ALU.mult))
                    do(V.tensor_tensor(cb, cb, i2, ALU.mult))
                    do(V.tensor_tensor(t, u, b(cb), ALU.mult))
                    dve.wait_ge(pooled, 3)
                    do(V.tensor_tensor(u, t, p, ALU.add))
                    dve.wait_ge(acted, 4)
                    do(V.tensor_reduce(rn, a, AX, ALU.add))
                    do(V.tensor_scalar(rn, rn, MIN_NORM * MIN_NORM, None, ALU.max))
                    dve.wait_ge(acted, 5)
                    do(V.reciprocal(ff, nr))
                    do(V.tensor_scalar(ff, ff, BALL, 1.0, ALU.mult, ALU.min))
                    do(V.tensor_tensor(t, u, b(ff), ALU.mult))
                    do(V.tensor_tensor(X[:], X[:], t, ALU.add))

        def stage_degrees():
            summed, copied, col, logged = sem("dg_summed"), sem("dg_copied"), sem("dg_col"), sem("dg_logged")
            one, t = take([N, 1]), take([N, B])
            loaded = sem("pna_loaded")
            UNROLL = 8
            with nc.psum_tensor("dg", [N, B], F32) as dg, nc.Block() as block:
                @block.sync
                def _(sp):
                    for side in (0, C):
                        rows = slice(side, side + C)
                        sp.dma_start(wcat[rows, 0:C], W["L2_gnn_W_pre"][0:C, :]).then_inc(loaded, 16)
                        sp.dma_start(wcat[rows, C:2 * C], W["L2_gnn_W_pre"][C:2 * C, :]).then_inc(loaded, 16)
                        sp.dma_start(wcat[rows, 2 * C:3 * C], W["L2_gnn_W_post"][0:C, :]).then_inc(loaded, 16)
                    for k in range(2):
                        sp.dma_start(wm[:, k], W["L2_gnn_W_post"][C:, :].rearrange("(s k p) c -> k p s c", k=2, p=N)[k])\
                          .then_inc(loaded, 16)
                    sp.dma_start(bias[:, 0:C], W["L2_gnn_b_pre"].partition_broadcast(N)).then_inc(loaded, 16)
                    sp.dma_start(bias[:, 2 * C:3 * C], W["L2_gnn_b_post"].partition_broadcast(N)).then_inc(loaded, 16)
                    sp.wait_ge(loaded, 160)

                @block.gpsimd
                def _(pool):
                    nc.gpsimd.memset(bias[:, C:2 * C], 0.0)

                @block.tensor
                def _(pe):
                    with pe.Fori(0, B // UNROLL) as t:
                        for k in range(UNROLL):
                            g = t * UNROLL + k
                            mm = nc.tensor.matmul(dg[:, bass.ds(g, 1)], AT[:, bass.ds(g, 1), :].rearrange("p a i -> p (a i)"),
                                                  onesb[:, 0:1], start=True, stop=True)
                        mm.then_inc(summed, 1)

                @block.scalar
                def _(act):
                    act.wait_ge(col, 2)
                    nc.scalar.activation(t, degree, ACT.Ln, bias=one).then_inc(logged, 1)

                @block.vector
                def _(dve):
                    V = nc.vector
                    step = Steps(dve, col)

                    def do(ins):
                        step(ins)
                        step.wait()
                    do(V.memset(one, 1.0))
                    dve.wait_ge(summed, B // UNROLL)
                    do(V.tensor_copy(degree, dg[:]))
                    do(V.tensor_scalar(rdeg, degree, 1.0, None, ALU.max))
                    do(V.reciprocal(rdeg, rdeg))
                    do(V.tensor_tensor(share, degree, rdeg, ALU.mult))
                    dve.wait_ge(logged, 1)
                    do(V.tensor_scalar(amp, t, 1.0 / AVG_D_LOG, None, ALU.mult))
                    do(V.tensor_scalar(t, t, LN_EPS, None, ALU.max))
                    do(V.reciprocal(t, t))
                    do(V.tensor_scalar(att, t, AVG_D_LOG, None, ALU.mult))

        def stage_neighbour_terms():
            staged, turned, turn_copied, formed, q_ready, hi, r1, mid, r2, lo = [sem("nt_" + n) for n in (
                "staged", "turned", "turn_copied", "formed", "q_ready", "hi", "r1", "mid", "r2", "lo")]
            h8, hT, Q, ra, rb = take([N, SG, C]), take([N, SG // 2, N]), take([N, SG, C]), take([N, SG, C]), take([N, SG, C])
            pt = [take([N, SG, C], BF16) for _ in range(2)]
            with ExitStack() as ps:
                tp = ps.enter_context(nc.psum_tensor("nt_tp", [N, SG // 2, N], F32))
                qp = ps.enter_context(nc.psum_tensor("nt_qp", [N, 2, 512], F32))
                block = ps.enter_context(nc.Block())

                @block.gpsimd
                def _(pool):
                    with pool.Fori(0, SORTS) as s:
                        turn = bass.ds(s * SG, SG)
                        pool.wait_ge(turned, s + 1)
                        nc.gpsimd.tensor_copy(h8, H[:, turn, :]).then_inc(staged, 1)
                        pool.wait_ge(hi, s + 1)
                        nc.gpsimd.tensor_tensor(ra, Q, pt[0], ALU.subtract).then_inc(r1, 1)
                        pool.wait_ge(mid, s + 1)
                        nc.gpsimd.tensor_tensor(rb, ra, pt[1], ALU.subtract).then_inc(r2, 1)

                @block.tensor
                def _(pe):
                    starts_free(pe, turned)
                    with pe.Fori(0, SORTS) as s:
                        pe.wait_ge(staged, s + 1)
                        pe.wait_ge(turn_copied, s + 1)
                        for pair in range(SG // 2):
                            mm = nc.tensor.transpose(tp[:, pair, :], h8[:, 2 * pair:2 * pair + 2, :].rearrange("p g c -> p (g c)"),
                                                     identf[:])
                        mm.then_inc(turned, 1)
                        pe.wait_ge(turn_copied, s + 2)
                        pe.wait_ge(q_ready, s + 1)
                        for g in range(SG):
                            side = slice((g % 2) * C, (g % 2) * C + C)
                            mm = nc.tensor.matmul(qp[:, g % 2, (g // 2) * C:(g // 2 + 1) * C], hT[side, g // 2, :],
                                                  wcat[side, C:2 * C], start=True, stop=True)
                            mm.then_inc(formed, 1)

                @block.scalar
                def _(act):
                    starts_free(act, turn_copied, q_ready)
                    with act.Fori(0, SORTS) as s:
                        turn = bass.ds(s * SG, SG)
                        act.wait_ge(turned, s + 2)
                        nc.scalar.copy(hT, tp[:]).then_inc(turn_copied, 1)
                        act.wait_ge(formed, (s + 1) * SG)
                        act.wait_ge(lo, s + 1)
                        nc.scalar.copy(Q.rearrange("p (a b) c -> p b a c", b=2),
                                       qp[:, :, 0:SG // 2 * C].rearrange("p b (a c) -> p b a c", c=C)).then_inc(q_ready, 1)
                        act.wait_ge(q_ready, s + 2)
                        nc.scalar.copy(pt[0], Q).then_inc(hi, 1)
                        act.wait_ge(r1, s + 1)
                        nc.scalar.copy(pt[1], ra).then_inc(mid, 1)
                        act.wait_ge(r2, s + 1)
                        nc.scalar.copy(PARTS[:, 2, turn, :], rb)

                @block.vector
                def _(dve):
                    starts_free(dve, lo)
                    with dve.Fori(0, SORTS) as s:
                        turn = bass.ds(s * SG, SG)
                        dve.wait_ge(hi, s + 1)
                        nc.vector.tensor_copy(PARTS[:, 0, turn, :], pt[0])
                        dve.wait_ge(mid, s + 1)
                        nc.vector.tensor_copy(PARTS[:, 1, turn, :], pt[1]).then_inc(lo, 1)

        def stage_extremes():
            hot_ready = [sem(f"x_hot_ready{k}") for k in range(RING)]
            slot_ready = [sem(f"x_slot_ready{k}") for k in range(RING)]
            flipped = [sem(f"x_flipped{k}") for k in range(RING)]
            prep, maxed, minned = sem("x_prep"), sem("x_maxed"), sem("x_minned")
            hot = [take([N, SG * N], BF16) for _ in range(RING)]
            pad = take([N, SLOTS, B], BF16)
            minus, twice = take([N, N], BF16), take([N, N], BF16)
            TURN = SLOTS // RING
            with ExitStack() as ps:
                gat = [ps.enter_context(nc.psum_tensor(f"x_gat{b}", [N, SG, C], F32)) for b in range(RING)]
                block = ps.enter_context(nc.Block())

                @block.gpsimd
                def _(pool):
                    step = Steps(pool, prep)
                    step(nc.gpsimd.tensor_scalar(minus, identb[:], -1.0, None, ALU.mult))
                    step(nc.gpsimd.tensor_scalar(twice, identb[:], 2.0, None, ALU.mult))
                    absent_slots(nc.gpsimd, step, pad)

                @block.tensor
                def _(pe):
                    def flip(s, r):
                        k = r % RING
                        pe.wait_ge(maxed, s * SLOTS + r + 1)
                        nc.tensor.matmul(gat[k][:], twice, pad[:, r, bass.ds(s * SG, SG)].unsqueeze(2).broadcast_to([N, SG, C]),
                                         start=False, stop=True, skip_group_check=True).then_inc(flipped[k], 1)
                    pe.wait_ge(prep, SLOTS + 2)
                    with pe.Fori(0, SORTS) as s:
                        for r in range(SLOTS + 2):
                            if r < SLOTS:
                                pe.wait_ge(minned, s * SLOTS + max(r - RING + 1, 0) + 1)
                                gather_slot(pe, s, r, hot, hot_ready, slot_ready, pad, minus, gat[r % RING][:])
                            if r >= 2:
                                flip(s, r - 2)

                @block.vector
                def _(dve):
                    starts_free(dve, minned)
                    with dve.Fori(0, SORTS) as s:
                        top, low = MAXQ[:, bass.ds(s * SG, SG), :], MINQ[:, bass.ds(s * SG, SG), :]
                        ahead = RING - 1
                        for r in range(ahead):
                            hot_slot(dve, s, r, hot, hot_ready, slot_ready)
                        for r in range(SLOTS + 3):
                            if r + ahead < SLOTS:
                                hot_slot(dve, s, r + ahead, hot, hot_ready, slot_ready)
                            if r < SLOTS:
                                k = r % RING
                                dve.wait_ge(slot_ready[k], s * TURN + r // RING + 1)
                                if r == 0:
                                    nc.vector.tensor_copy(top, gat[k][:]).then_inc(maxed, 1)
                                else:
                                    dve.wait_ge(maxed, s * SLOTS + r)
                                    nc.vector.tensor_tensor(top, top, gat[k][:], ALU.max).then_inc(maxed, 1)
                            if r >= 3:
                                m = r - 3
                                k = m % RING
                                dve.wait_ge(flipped[k], s * TURN + m // RING + 1)
                                if m == 0:
                                    nc.vector.tensor_copy(low, gat[k][:]).then_inc(minned, 1)
                                else:
                                    dve.wait_ge(minned, s * SLOTS + m + 1)
                                    nc.vector.tensor_tensor(low, low, gat[k][:], ALU.min).then_inc(minned, 1)

        def stage_pna():
            def turns(name, per=1):
                return Turns(sem("pn_" + name), per)
            staged, turned, copied, formed, biased = turns("staged"), turns("turned"), turns("copied"), turns("formed", QG), turns("biased")
            squared, widened, summed, scaled, msq = turns("squared"), turns("widened"), turns("summed"), turns("scaled", 2), turns("msq")
            parts, varied, floored, filled, rooted = turns("parts", 3), turns("varied"), turns("floored"), turns("filled", 4), turns("rooted")
            m_turned, m_copied, joined, added = turns("m_turned"), turns("m_copied", 2), turns("joined"), turns("added", 5)
            ready = sem("pn_ready")
            h4, QQ, m2, q2, pm, sq, vv, mx, mn, o1, o2, o3, o4 = [[take([N, QG, C]) for _ in range(2)] for _ in range(13)]
            hT = [take([N, 2, N]) for _ in range(2)]
            PQO = [take([N, QG, 3 * C]) for _ in range(2)]
            ATf = [take([N, QG, N]) for _ in range(2)]
            M4 = [take([N, QG, 4 * C]) for _ in range(2)]
            MT = [take([N, QG, 2, N]) for _ in range(2)]
            eps = take([N, 1])
            bc = [N, QG, C]
            with ExitStack() as ps:
                tp = ps.enter_context(nc.psum_tensor("pn_tp", [N, 2, 256], F32))
                pq = ps.enter_context(nc.psum_tensor("pn_pq", [N, 2, 512], F32))
                ag = ps.enter_context(nc.psum_tensor("pn_ag", [N, QG, N], F32))
                mt = ps.enter_context(nc.psum_tensor("pn_mt", [N, QG, 2, N], F32))
                jo = ps.enter_context(nc.psum_tensor("pn_jo", [N, 2, 512], F32))
                block = ps.enter_context(nc.Block())
                jv = jo[:, :, 0:6 * C].rearrange("p b (a s c) -> p b a s c", a=2, s=3)

                @block.gpsimd
                def _(pool):
                    P = nc.gpsimd

                    def stage(q, u):
                        turned.wait(pool, q, behind=2)
                        P.tensor_copy(h4[u], H[:, bass.ds(q * QG, QG), :]).then_inc(staged.sem, 1)

                    def own_terms(q, u):
                        quad = bass.ds(q * QG, QG)
                        biased.wait(pool, q)
                        filled.wait(pool, q, behind=2)
                        P.tensor_tensor(pm[u], PQO[u][:, :, 0:C], share[:, quad].unsqueeze(2).broadcast_to(bc), ALU.mult).then_inc(parts.sem, 1)
                        P.tensor_tensor(mx[u], PQO[u][:, :, 0:C], MAXQ[:, quad, :], ALU.add).then_inc(parts.sem, 1)
                        P.tensor_tensor(mn[u], PQO[u][:, :, 0:C], MINQ[:, quad, :], ALU.add).then_inc(parts.sem, 1)

                    def variance(q, u):
                        msq.wait(pool, q)
                        rooted.wait(pool, q, behind=2)
                        P.tensor_tensor(vv[u], q2[u], sq[u], ALU.subtract).then_inc(varied.sem, 1)

                    staged.begin(pool)
                    parts.begin(pool)
                    varied.begin(pool)
                    stage(0, 0)
                    stage(1, 1)

                    def two_quads(q, ahead):
                        for u in range(2):
                            if ahead:
                                stage(q + 2 + u, u)
                        own_terms(q, 0)
                        own_terms(q + 1, 1)
                        variance(q, 0)
                        variance(q + 1, 1)
                    with pool.Fori(0, QUADS // 2 - 1) as i:
                        two_quads(i * 2, True)
                    two_quads(QUADS - 2, False)

                @block.tensor
                def _(pe):
                    def turn(q, u):
                        staged.wait(pe, q)
                        copied.wait(pe, q, behind=1)
                        for pair in range(2):
                            mm = nc.tensor.transpose(tp[:, pair, 0:N], h4[u][:, 2 * pair:2 * pair + 2, :].rearrange("p g c -> p (g c)"),
                                                     identf[:])
                        mm.then_inc(turned.sem, 1)

                    def form(q, u):
                        copied.wait(pe, q)
                        biased.wait(pe, q, behind=1)
                        for g in range(QG):
                            side = slice((g % 2) * C, (g % 2) * C + C)
                            mm = nc.tensor.matmul(pq[:, g % 2, (g // 2) * 3 * C:(g // 2 + 1) * 3 * C], hT[u][side, g // 2, :],
                                                  wcat[side, :], start=True, stop=True)
                            mm.then_inc(formed.sem, 1)

                    def aggregate(q, u):
                        squared.wait(pe, q)
                        widened.wait(pe, q)
                        scaled.wait(pe, q, behind=1)
                        for g in range(QG):
                            nc.tensor.matmul(ag[:, g, 0:C], ATf[u][:, g, :], PQO[u][:, g, C:2 * C], start=True, stop=True)
                            mm = nc.tensor.matmul(ag[:, g, C:2 * C], ATf[u][:, g, :], QQ[u][:, g, :], start=True, stop=True)
                        mm.then_inc(summed.sem, 1)

                    def turn_aggregates(q, u):
                        filled.wait(pe, q)
                        rooted.wait(pe, q)
                        m_copied.wait(pe, q, behind=1)
                        for g in range(QG):
                            for k in range(2):
                                mm = nc.tensor.transpose(mt[:, g, k, :], M4[u][:, g, k * N:(k + 1) * N], identf[:])
                        mm.then_inc(m_turned.sem, 1)

                    def join(q, u):
                        m_copied.wait(pe, q)
                        added.wait(pe, q, 3, behind=1)
                        for g in range(QG):
                            for k in range(2):
                                mm = nc.tensor.matmul(jo[:, g // 2, (g % 2) * 3 * C:(g % 2 + 1) * 3 * C], MT[u][:, g, k, :],
                                                      wm[:, k].rearrange("p s c -> p (s c)"), start=(k == 0), stop=(k == 1))
                        mm.then_inc(joined.sem, 1)

                    for t in (turned, formed, summed, m_turned, joined):
                        t.begin(pe)
                    for u in range(2):
                        turn(u, u)
                        form(u, u)

                    def two_quads(q, ahead):
                        for u in range(2):
                            aggregate(q + u, u)
                            if ahead:
                                turn(q + 2 + u, u)
                        for u in range(2):
                            turn_aggregates(q + u, u)
                            if ahead:
                                form(q + 2 + u, u)
                        for u in range(2):
                            join(q + u, u)
                    with pe.Fori(0, QUADS // 2 - 1) as i:
                        two_quads(i * 2, True)
                    two_quads(QUADS - 2, False)

                @block.scalar
                def _(act):
                    S = nc.scalar

                    def copy_in(q, u):
                        turned.wait(act, q)
                        formed.wait(act, q, behind=2)
                        S.copy(hT[u], tp[:, :, 0:N]).then_inc(copied.sem, 1)

                    def widen(q, u):
                        summed.wait(act, q, behind=2)
                        S.copy(ATf[u], AT[:, bass.ds(q * QG, QG), :]).then_inc(widened.sem, 1)
                        biased.wait(act, q)
                        S.activation(QQ[u], PQO[u][:, :, C:2 * C], ACT.Square).then_inc(squared.sem, 1)

                    def square_mean(q, u):
                        scaled.wait(act, q)
                        varied.wait(act, q, behind=2)
                        S.activation(sq[u], m2[u], ACT.Square).then_inc(msq.sem, 1)

                    def root(q, u):
                        floored.wait(act, q)
                        m_turned.wait(act, q, behind=2)
                        S.activation(M4[u][:, :, 3 * C:4 * C], vv[u], ACT.Sqrt, bias=eps).then_inc(rooted.sem, 1)

                    def copy_aggregates(q, u):
                        m_turned.wait(act, q)
                        joined.wait(act, q, behind=2)
                        for half in range(2):
                            S.copy(MT[u][:, 2 * half:2 * half + 2], mt[:, 2 * half:2 * half + 2]).then_inc(m_copied.sem, 1)

                    for t in (copied, widened, squared, msq, rooted, m_copied):
                        t.begin(act)
                    act.wait_ge(ready, 1)
                    S.preload_act_table(ACT.Sqrt)
                    for u in range(2):
                        copy_in(u, u)
                        widen(u, u)

                    def two_quads(q, ahead):
                        for u in range(2):
                            square_mean(q + u, u)
                            if ahead:
                                copy_in(q + 2 + u, u)
                        for u in range(2):
                            root(q + u, u)
                            copy_aggregates(q + u, u)
                            if ahead:
                                widen(q + 2 + u, u)
                    with act.Fori(0, QUADS // 2 - 1) as i:
                        two_quads(i * 2, True)
                    two_quads(QUADS - 2, False)

                @block.vector
                def _(dve):
                    V = nc.vector

                    def add_bias(q, u):
                        formed.wait(dve, q)
                        filled.wait(dve, q, behind=2)
                        summed.wait(dve, q, behind=2)
                        V.tensor_tensor(PQO[u].rearrange("p (a b) c -> p b a c", b=2),
                                        pq[:, :, 0:6 * C].rearrange("p b (a c) -> p b a c", a=2),
                                        bias.unsqueeze(1).unsqueeze(1).broadcast_to([N, 2, 2, 3 * C]), ALU.add).then_inc(biased.sem, 1)

                    def scale(q, u):
                        rb = rdeg[:, bass.ds(q * QG, QG)].unsqueeze(2).broadcast_to(bc)
                        summed.wait(dve, q)
                        varied.wait(dve, q, behind=2)
                        V.tensor_tensor(m2[u], ag[:, :, 0:C], rb, ALU.mult).then_inc(scaled.sem, 1)
                        V.tensor_tensor(q2[u], ag[:, :, C:2 * C], rb, ALU.mult).then_inc(scaled.sem, 1)

                    def fill(q, u):
                        quad = bass.ds(q * QG, QG)
                        parts.wait(dve, q)
                        scaled.wait(dve, q)
                        m_turned.wait(dve, q, behind=2)
                        V.tensor_tensor(M4[u][:, :, 0:C], m2[u], pm[u], ALU.add).then_inc(filled.sem, 1)
                        V.tensor_scalar(M4[u][:, :, C:2 * C], mx[u], -NEG_BIG, None, ALU.max).then_inc(filled.sem, 1)
                        V.tensor_scalar(M4[u][:, :, 2 * C:3 * C], mn[u], NEG_BIG, None, ALU.min).then_inc(filled.sem, 1)
                        added.wait(dve, q, behind=2)
                        V.tensor_tensor(o3[u], PQO[u][:, :, 2 * C:3 * C], X[:, quad, :], ALU.add).then_inc(filled.sem, 1)
                        varied.wait(dve, q)
                        V.tensor_scalar(vv[u], vv[u], 0.0, None, ALU.max).then_inc(floored.sem, 1)

                    def finish(q, u):
                        quad = bass.ds(q * QG, QG)
                        joined.wait(dve, q)
                        added.wait(dve, q, behind=1)
                        o1v, o2v, o3v, o4v = [o[u].rearrange("p (b a) c -> p b a c", b=2) for o in (o1, o2, o3, o4)]
                        ampb, attb = [t[:, quad].rearrange("p (b a) -> p b a", b=2).unsqueeze(3).broadcast_to([N, 2, 2, C])
                                      for t in (amp, att)]
                        V.tensor_tensor(o1v, jv[:, :, :, 1, :], ampb, ALU.mult).then_inc(added.sem, 1)
                        V.tensor_tensor(o2v, jv[:, :, :, 2, :], attb, ALU.mult).then_inc(added.sem, 1)
                        V.tensor_tensor(o4v, jv[:, :, :, 0, :], o3v, ALU.add).then_inc(added.sem, 1)
                        added.wait(dve, q, 2)
                        V.tensor_tensor(o1[u], o1[u], o2[u], ALU.add).then_inc(added.sem, 1)
                        added.wait(dve, q, 4)
                        V.tensor_tensor(X[:, quad, :], o1[u], o4[u], ALU.add).then_inc(added.sem, 1)

                    V.memset(eps, LN_EPS).then_inc(ready, 1)
                    for t in (biased, scaled, filled, floored, added):
                        t.begin(dve)
                    add_bias(0, 0)
                    add_bias(1, 1)

                    def two_quads(q, ahead):
                        for u in range(2):
                            scale(q + u, u)
                        for u in range(2):
                            fill(q + u, u)
                        for u in range(2):
                            if ahead:
                                add_bias(q + 2 + u, u)
                        for u in range(2):
                            finish(q + u, u)
                    with dve.Fori(0, QUADS // 2 - 1) as i:
                        two_quads(i * 2, True)
                    two_quads(QUADS - 2, False)

        def stage_gcn():
            HID = W["L3_gnn_W1"].shape[0]
            LAYERS = 3
            loaded, even_done = sem("gc_loaded"), sem("gc_even_done")

            def turns(name, per=1):
                return Turns(sem("gc_" + name), per)
            staged, turned, copied = turns("staged"), turns("turned"), turns("copied", 2)
            messaged, biased, summed, rectified = [[turns(f"{n}{u}_", LAYERS) for u in range(2)]
                                                   for n in ("messaged", "biased", "summed", "rectified")]
            joined, added = turns("joined"), turns("added", 3)
            h4 = [take([N, QG, C]) for _ in range(2)]
            hT = [take([N, 2, N]) for _ in range(2)]
            ATf = [take([N, QG, N]) for _ in range(2)]
            msg = [take([N, QG, HID]) for _ in range(2)]
            hid = [take([N, QG, N]) for _ in range(2)]
            y1 = [take([N, QG, C]) for _ in range(2)]
            y2 = [take([N, QG, C]) for _ in range(2)]
            w0, wh = take([N, HID]), take([N, 2, HID])
            wo, bb, bo = take([N, C]), take([N, 3, HID]), take([N, C])
            with ExitStack() as ps:
                tp = ps.enter_context(nc.psum_tensor("gc_tp", [N, 2, 256], F32))
                m0 = ps.enter_context(nc.psum_tensor("gc_m0", [N, 2, 512], F32))
                mp = [ps.enter_context(nc.psum_tensor(f"gc_mp{u}", [N, QG, HID], F32)) for u in range(2)]
                ap = [ps.enter_context(nc.psum_tensor(f"gc_ap{u}", [N, QG, N], F32)) for u in range(2)]
                op = ps.enter_context(nc.psum_tensor("gc_op", [N, 2 * QG, C], F32))
                block = ps.enter_context(nc.Block())

                @block.sync
                def _(sp):
                    for side in (0, C):
                        sp.dma_start(w0[side:side + C, :], W["L3_gnn_W0"]).then_inc(loaded, 16)
                    for k in range(2):
                        sp.dma_start(wh[:, k, :], W[f"L3_gnn_W{k + 1}"]).then_inc(loaded, 16)
                    sp.dma_start(wo, W["L3_gnn_Wout"]).then_inc(loaded, 16)
                    for k in range(3):
                        sp.dma_start(bb[:, k, :], W[f"L3_gnn_b{k}"].partition_broadcast(N)).then_inc(loaded, 16)
                    sp.dma_start(bo, W["L3_gnn_bout"].partition_broadcast(N)).then_inc(loaded, 16)

                @block.gpsimd
                def _(pool):
                    staged.begin(pool)
                    with pool.Fori(0, QUADS // 2) as i:
                        for u in range(2):
                            q = i * 2 + u
                            turned.wait(pool, q, behind=2)
                            nc.gpsimd.tensor_copy(h4[u], H[:, bass.ds(q * QG, QG), :]).then_inc(staged.sem, 1)

                @block.tensor
                def _(pe):
                    def turn(i, u):
                        q = i * 2 + u
                        staged.wait(pe, q)
                        copied.wait(pe, q, behind=1)
                        for pair in range(2):
                            mm = nc.tensor.transpose(tp[:, pair, 0:N], h4[u][:, 2 * pair:2 * pair + 2, :].rearrange("p g c -> p (g c)"),
                                                     identf[:])
                        mm.then_inc(turned.sem, 1)

                    def first_message(i, u):
                        q = i * 2 + u
                        copied.wait(pe, q)
                        biased[1 - u].wait(pe, i, 1, behind=1 - u)
                        for g in range(QG):
                            side = slice((g % 2) * C, (g % 2) * C + C)
                            mm = nc.tensor.matmul(m0[:, g % 2, (g // 2) * HID:(g // 2 + 1) * HID], hT[u][side, g // 2, :],
                                                  w0[side, :], start=True, stop=True)
                            if g == QG - 2:
                                mm.then_inc(even_done, 1)
                        mm.then_inc(messaged[u].sem, 1)

                    def message(i, u, layer):
                        rectified[u].wait(pe, i, layer)
                        if layer == 1:
                            biased[u].wait(pe, i, behind=1)
                        else:
                            biased[u].wait(pe, i, layer)
                        for g in range(QG):
                            mm = nc.tensor.matmul(mp[u][:, g, :], hid[u][:, g, :], wh[:, layer - 1, :], start=True, stop=True)
                        mm.then_inc(messaged[u].sem, 1)

                    def aggregate(i, u, layer):
                        biased[u].wait(pe, i, layer + 1)
                        if layer == 0:
                            rectified[u].wait(pe, i, behind=1)
                        else:
                            rectified[u].wait(pe, i, layer)
                        for g in range(QG):
                            mm = nc.tensor.matmul(ap[u][:, g, :], msg[u][:, g, :], ATf[u][:, g, :], start=True, stop=True)
                        mm.then_inc(summed[u].sem, 1)

                    def join(i, u):
                        q = i * 2 + u
                        rectified[u].wait(pe, i)
                        added.wait(pe, q, 1, behind=1)
                        for g in range(QG):
                            mm = nc.tensor.matmul(op[:, g, :], hid[u][:, g, :], wo, start=True, stop=True)
                        mm.then_inc(joined.sem, 1)

                    for t in [turned, joined] + messaged + summed:
                        t.begin(pe)
                    pe.sem_inc(even_done, 1)
                    pe.wait_ge(loaded, 144)
                    turn(0, 0)
                    turn(0, 1)

                    def two_quads(i, ahead):
                        first_message(i, 0)
                        first_message(i, 1)
                        aggregate(i, 0, 0)
                        aggregate(i, 1, 0)
                        for layer in range(1, LAYERS):
                            message(i, 0, layer)
                            message(i, 1, layer)
                            if ahead and layer == LAYERS - 1:
                                turn(i + 1, 0)
                            aggregate(i, 0, layer)
                            aggregate(i, 1, layer)
                        join(i, 0)
                        join(i, 1)
                        if ahead:
                            turn(i + 1, 1)
                    with pe.Fori(0, QUADS // 2 - 1) as i:
                        two_quads(i, True)
                    two_quads(QUADS // 2 - 1, False)

                @block.scalar
                def _(act):
                    def copy_in(i, u):
                        q = i * 2 + u
                        turned.wait(act, q)
                        messaged[u].wait(act, i, 1, behind=1)
                        nc.scalar.copy(hT[u], tp[:, :, 0:N]).then_inc(copied.sem, 1)
                        summed[u].wait(act, i, behind=1)
                        nc.scalar.copy(ATf[u], AT[:, bass.ds(q * QG, QG), :]).then_inc(copied.sem, 1)

                    def rectify(i, u, layer):
                        q = i * 2 + u
                        summed[u].wait(act, i, layer + 1)
                        if layer == 0:
                            joined.wait(act, q, behind=2)
                        nc.scalar.activation(hid[u], ap[u][:], ACT.Relu).then_inc(rectified[u].sem, 1)

                    for t in [copied] + rectified:
                        t.begin(act)
                    copy_in(0, 0)
                    copy_in(0, 1)

                    def two_quads(i, ahead):
                        for layer in range(LAYERS):
                            rectify(i, 0, layer)
                            if ahead and layer == LAYERS - 1:
                                copy_in(i + 1, 0)
                            rectify(i, 1, layer)
                        if ahead:
                            copy_in(i + 1, 1)
                    with act.Fori(0, QUADS // 2 - 1) as i:
                        two_quads(i, True)
                    two_quads(QUADS // 2 - 1, False)

                @block.vector
                def _(dve):
                    V = nc.vector

                    def add_bias(i, u, layer):
                        q = i * 2 + u
                        messaged[u].wait(dve, i, layer + 1)
                        if layer == 0:
                            dve.wait_ge(even_done, q + 2)
                            summed[u].wait(dve, i, behind=1)
                            V.tensor_tensor(msg[u].rearrange("p (a b) c -> p b a c", b=2),
                                            m0[:, :, 0:2 * HID].rearrange("p b (a c) -> p b a c", a=2),
                                            bb[:, 0, :].unsqueeze(1).unsqueeze(1).broadcast_to([N, 2, 2, HID]),
                                            ALU.add).then_inc(biased[u].sem, 1)
                        else:
                            summed[u].wait(dve, i, layer)
                            V.tensor_tensor(msg[u], mp[u][:], bb[:, layer, :].unsqueeze(1).broadcast_to([N, QG, HID]),
                                            ALU.add).then_inc(biased[u].sem, 1)

                    def finish(i, u):
                        q = i * 2 + u
                        quad = bass.ds(q * QG, QG)
                        joined.wait(dve, q)
                        added.wait(dve, q, behind=1)
                        V.tensor_tensor(y1[u], op[:, 0:QG, :], bo.unsqueeze(1).broadcast_to([N, QG, C]), ALU.add).then_inc(added.sem, 1)
                        added.wait(dve, q, 1)
                        V.tensor_tensor(y2[u], y1[u], mask[:, quad].unsqueeze(2).broadcast_to([N, QG, C]), ALU.mult).then_inc(added.sem, 1)
                        added.wait(dve, q, 2)
                        V.tensor_tensor(X[:, quad, :], X[:, quad, :], y2[u], ALU.add).then_inc(added.sem, 1)

                    for t in [added] + biased:
                        t.begin(dve)
                    dve.wait_ge(loaded, 144)
                    with dve.Fori(0, QUADS // 2) as i:
                        for layer in range(LAYERS):
                            add_bias(i, 0, layer)
                            add_bias(i, 1, layer)
                        finish(i, 0)
                        finish(i, 1)

        def stage_aggregation():
            nonlocal degree, rdeg, share, amp, att, wcat, wm, bias, MAXQ, MINQ
            used[0] = 0
            degree, rdeg, share, amp, att = [take([N, B]) for _ in range(5)]
            wcat, wm, bias = take([N, 3 * C]), take([N, 2, 3, C]), take([N, 3 * C])
            MAXQ, MINQ = take([N, B, C]), take([N, B, C])
            base = used[0]
            for stage in (stage_degrees, stage_neighbour_terms, stage_extremes,
                          lambda: stage_general("xg_", False), stage_pna):
                used[0] = base
                stage()

        degree = rdeg = share = amp = att = wcat = wm = bias = MAXQ = MINQ = None

        def stage_attention():
            nonlocal x2, uw, ox, coef, cu, ncu, cox, hcox, selfl, SUMS
            used[0] = 0
            x2, uw, ox, coef, cu, ncu, cox, hcox, selfl = [take([N, B]) for _ in range(9)]
            SUMS = take([N, B, C + 2])
            base = used[0]
            for stage in (stage_columns, stage_pairs, stage_expmap):
                used[0] = base
                stage()

        x2 = uw = ox = coef = cu = ncu = cox = hcox = selfl = SUMS = None

        def stage_store():
            stored = sem("stored")
            with nc.Block() as block:
                @block.sync
                def _(sp):
                    sp.dma_start(out.rearrange("g i c -> i g c"), X[:]).then_inc(stored, 16)
                    sp.wait_ge(stored, 16)

        stage_constants()
        stage_thinned()
        stage_norm(0, True)
        stage_first()
        stage_mlp()
        end_layer()
        stage_norm(1, False)
        stage_attention()
        end_layer()
        stage_positions()
        stage_norm(2, False)
        stage_aggregation()
        stage_norm(3, False)
        used[0] = 0
        stage_gcn()
        stage_store()
        end_layer()


def kernel(**inputs):
    import numpy as _np
    import concourse.bacc as _bacc
    from concourse import mybir as _mybir
    from concourse.bass_utils import run_bass_kernel_spmd as _run

    nc = _bacc.Bacc("TRN2", target_bir_lowering=False, num_devices=1)
    arrays, weights = {}, {}
    for name in inputs:
        a = _np.ascontiguousarray(inputs[name])
        if a.dtype == _np.bool_:
            a = a.view(_np.uint8)
        arrays[f"in_{name}_dram"] = a
        weights[name] = nc.dram_tensor(f"in_{name}_dram", a.shape, _mybir.dt.from_np(a.dtype), kind="ExternalInput").ap()
    x, adj, nodemask = (weights.pop(n) for n in ("x", "adj", "nodemask"))
    out = nc.dram_tensor("out_0_dram", x.shape, _mybir.dt.float32, kind="ExternalOutput").ap()
    build(nc, x, adj, nodemask, weights, out)
    r = _run(nc, [arrays], core_ids=[0])
    return r.results[0]["out_0_dram"]
```
